# Optimizing a Trainium2 kernel written in Bass

```python
import numpy as np
import jax
import jax.numpy as jnp

def _softmax(x, axis=-1):
    return jax.nn.softmax(x, axis=axis)

def _gelu(x):
    return jax.nn.gelu(x, approximate=True)

def _silu(x):
    return jax.nn.silu(x)

def _sigmoid(x):
    return jax.nn.sigmoid(x)

def _layernorm(x, axis=-1, eps=1e-05):
    m = jnp.mean(x, axis=axis, keepdims=True)
    v = jnp.var(x, axis=axis, keepdims=True)
    return (x - m) / jnp.sqrt(v + eps)

def _scatter_add(tgt, idx, src, axis=0):
    return tgt.at[idx].add(src)

def _segment_sum(src, seg, n):
    return jax.ops.segment_sum(src, seg, n)
kernel_name = 'mk_xattn_ffn_d2_seqx_r4_6b42f2'

def setup_inputs(seed: int=0):
    np.random.seed(seed)
    _w = jnp.asarray

    def _rec_inputs():
        import jax
        import jax.numpy as jnp
        _rk = jax.random.key(seed)
        x = -0.0003929 + 0.9999 * jax.random.normal(jax.random.fold_in(_rk, 1), (4, 512, 256), jnp.float32)
        _lenS = 512 - jax.random.randint(jax.random.fold_in(_rk, 7), (4,), 0, max(1, 512 // 4) + 1, jnp.int32)
        _lenS2 = 512 - jax.random.randint(jax.random.fold_in(_rk, 8), (4,), 0, max(1, 512 // 4) + 1, jnp.int32)
        _ctx_1024P = jax.random.normal(jax.random.fold_in(_rk, 12), (4, 16, 256), jnp.float32)
        _ctx_1024c = jax.random.dirichlet(jax.random.fold_in(_rk, 512), 0.3 * jnp.ones((16,), jnp.float32), (4, 512))
        _ctx_1024t = jnp.einsum('bsk,bkd->bsd', _ctx_1024c, _ctx_1024P)
        _ctx_1024t = _ctx_1024t * jax.lax.rsqrt(jnp.mean(jnp.square(_ctx_1024t)) + 1e-12) * 0.953939
        ctx_1024 = -0.000514642 + 1.00011 * (_ctx_1024t + 0.3 * jax.random.normal(jax.random.fold_in(_rk, 612), (4, 512, 256), jnp.float32))
        _validS = jnp.arange(512)[None, :] < _lenS[:, None]
        _validS2 = jnp.arange(512)[None, :] < _lenS2[:, None]
        _causal = jnp.tril(jnp.ones((512, 512), dtype=bool))
        mask_BxS_ik0 = jnp.where(jnp.broadcast_to(_validS[:, :], (4, 512)), 0, 1).astype(jnp.int32)
        mask_BxS2_ik1 = jnp.where(jnp.broadcast_to(_validS2[:, :], (4, 512)), 1, 0).astype(jnp.int32)
        return (x, ctx_1024, mask_BxS_ik0, mask_BxS2_ik1)
    x, ctx_1024, mask_BxS_ik0, mask_BxS2_ik1 = _rec_inputs()

    def _L0_xattn_setup():
        import jax, jax.numpy as jnp
        import numpy as np
        LN_EPS = 1e-05
        NEG = -1000000000.0

        def _layernorm(x, w):
            xf = x.astype(jnp.float32)
            mu = jnp.mean(xf, axis=-1, keepdims=True)
            var = jnp.mean(jnp.square(xf - mu), axis=-1, keepdims=True)
            return (xf - mu) * jax.lax.rsqrt(var + LN_EPS) * w
        key = jax.random.key(seed)
        ks = jax.random.split(key, 8)
        B, S, L, dim = (8, 512, 64, 256)
        x = jax.random.normal(ks[0], (B, S, dim), dtype=jnp.float32)
        style_tokens = jax.random.normal(ks[1], (B, L, dim), dtype=jnp.float32)
        xm = jax.random.randint(ks[2], (B, S), 0, 2).astype(jnp.int32)
        sm = jax.random.randint(ks[3], (B, L), 0, 2).astype(jnp.int32)
        xm = xm.at[:, 0].set(1)
        sm = sm.at[:, 0].set(1)
        scale = 1.0 / np.sqrt(dim)
        Wq = jax.random.normal(ks[4], (dim, dim), dtype=jnp.float32) * scale
        Wkv = jax.random.normal(ks[5], (dim, 2 * dim), dtype=jnp.float32) * scale
        Wo = jax.random.normal(ks[6], (dim, dim), dtype=jnp.float32) * scale
        ln_w = jnp.ones((dim,), dtype=jnp.float32)
        return {'x': x, 'x_attention_mask': xm, 'style_tokens': style_tokens, 'style_attention_mask': sm, 'ln_w': ln_w, 'Wq': Wq, 'Wkv': Wkv, 'Wo': Wo}
    _L0_xattn_all = _L0_xattn_setup()
    _L0_xattn_in = {k: v for k, v in _L0_xattn_all.items() if k in ('ln_w', 'Wq', 'Wkv', 'Wo')}
    del _L0_xattn_all

    def _L0_ffn_setup():
        import jax, jax.numpy as jnp
        import numpy as np
        N_EMBD = 256
        NUM_EXPERTS = 8
        TOP_K = 2

        def new_gelu(x):
            c = jnp.sqrt(2.0 / jnp.pi).astype(x.dtype)
            return 0.5 * x * (1.0 + jnp.tanh(c * (x + 0.044715 * x ** 3)))
        key = jax.random.key(seed)
        ks = jax.random.split(key, 6)
        C, E, H = (N_EMBD, NUM_EXPERTS, 4 * N_EMBD)
        x = jax.random.normal(ks[0], (4, 512, C), dtype=jnp.float32)
        router_w = 0.02 * jax.random.normal(ks[1], (E, C), dtype=jnp.float32)
        w1 = 0.02 * jax.random.normal(ks[2], (E, H, C), dtype=jnp.float32)
        b1 = jnp.zeros((E, H), dtype=jnp.float32)
        w2 = 0.02 * jax.random.normal(ks[3], (E, C, H), dtype=jnp.float32)
        b2 = jnp.zeros((E, C), dtype=jnp.float32)
        return {'x': x, 'router_w': router_w, 'w1': w1, 'b1': b1, 'w2': w2, 'b2': b2}
    _L0_ffn_all = _L0_ffn_setup()
    _L0_ffn_in = {k: v for k, v in _L0_ffn_all.items() if k in ('router_w', 'w1', 'b1', 'w2', 'b2')}
    del _L0_ffn_all

    def _L1_xattn_setup():
        import jax, jax.numpy as jnp
        import numpy as np
        B, S, D = (1, 1024, 256)
        NUM_HEADS, HEAD_DIM = (16, 64)
        WINDOW = 128
        EMBED = NUM_HEADS * HEAD_DIM
        key = jax.random.key(seed)
        ks = jax.random.split(key, 7)
        scale_in = 1.0 / np.sqrt(D)
        scale_e = 1.0 / np.sqrt(EMBED)
        return {'query': jax.random.normal(ks[0], (B, S, D), dtype=jnp.float32), 'key': jax.random.normal(ks[1], (B, S, D), dtype=jnp.float32), 'value': jax.random.normal(ks[2], (B, S, D), dtype=jnp.float32), 'Wq': jax.random.normal(ks[3], (D, EMBED), dtype=jnp.float32) * scale_in, 'Wk': jax.random.normal(ks[4], (D, EMBED), dtype=jnp.float32) * scale_in, 'Wv': jax.random.normal(ks[5], (D, EMBED), dtype=jnp.float32) * scale_in, 'Wo': jax.random.normal(ks[6], (EMBED, D), dtype=jnp.float32) * scale_e}
    _L1_xattn_all = _L1_xattn_setup()
    _L1_xattn_in = {k: v for k, v in _L1_xattn_all.items() if k in ('Wq', 'Wk', 'Wv', 'Wo')}
    del _L1_xattn_all

    def _L1_ffn_setup():
        import jax, jax.numpy as jnp
        import numpy as np
        BLOCK = 32
        W_BITS = 4
        ACT_BITS = 16

        def act_qdq(x):
            qmax = 2.0 ** (ACT_BITS - 1) - 1.0
            scale = jnp.maximum(jnp.max(jnp.abs(x)) / qmax, 1e-12)
            return jnp.clip(jnp.round(x / scale), -qmax - 1.0, qmax) * scale

        def fixed_qdq_u16(x):
            scale = 1.0 / 65536.0
            return jnp.clip(jnp.round(x / scale), 0.0, 65535.0) * scale

        def lpbq_dequant(w):
            O, I = w.shape
            qmax = 2.0 ** (W_BITS - 1) - 1.0
            wb = w.reshape(O, I // BLOCK, BLOCK)
            s = jnp.maximum(jnp.max(jnp.abs(wb), axis=-1, keepdims=True) / qmax, 1e-12)
            wq = jnp.clip(jnp.round(wb / s), -qmax - 1.0, qmax) * s
            return wq.reshape(O, I)
        key = jax.random.key(seed)
        k1, k2, k3, k4 = jax.random.split(key, 4)
        B, S, H, I = (2, 1024, 256, 768)
        x = jax.random.normal(k1, (B, S, H), jnp.float32)
        w_gate = jax.random.normal(k2, (I, H), jnp.float32) * 0.02
        w_up = jax.random.normal(k3, (I, H), jnp.float32) * 0.02
        w_down = jax.random.normal(k4, (H, I), jnp.float32) * 0.02
        return {'x': x, 'w_gate': w_gate, 'w_up': w_up, 'w_down': w_down}
    _L1_ffn_all = _L1_ffn_setup()
    _L1_ffn_in = {k: v for k, v in _L1_ffn_all.items() if k in ('w_gate', 'w_up', 'w_down')}
    del _L1_ffn_all
    return {'x': x, 'ctx_1024': ctx_1024, 'mask_BxS_ik0': mask_BxS_ik0, 'mask_BxS2_ik1': mask_BxS2_ik1, 'L0_xattn_ln_w': _L0_xattn_in['ln_w'], 'L0_xattn_Wq': _L0_xattn_in['Wq'], 'L0_xattn_Wkv': _L0_xattn_in['Wkv'], 'L0_xattn_Wo': _L0_xattn_in['Wo'], 'L0_ffn_router_w': _L0_ffn_in['router_w'], 'L0_ffn_w1': _L0_ffn_in['w1'], 'L0_ffn_b1': _L0_ffn_in['b1'], 'L0_ffn_w2': _L0_ffn_in['w2'], 'L0_ffn_b2': _L0_ffn_in['b2'], 'L1_xattn_Wq': _L1_xattn_in['Wq'], 'L1_xattn_Wk': _L1_xattn_in['Wk'], 'L1_xattn_Wv': _L1_xattn_in['Wv'], 'L1_xattn_Wo': _L1_xattn_in['Wo'], 'L1_ffn_w_gate': _L1_ffn_in['w_gate'], 'L1_ffn_w_up': _L1_ffn_in['w_up'], 'L1_ffn_w_down': _L1_ffn_in['w_down']}

def reference(x, ctx_1024, mask_BxS_ik0, mask_BxS2_ik1, L0_xattn_ln_w, L0_xattn_Wq, L0_xattn_Wkv, L0_xattn_Wo, L0_ffn_router_w, L0_ffn_w1, L0_ffn_b1, L0_ffn_w2, L0_ffn_b2, L1_xattn_Wq, L1_xattn_Wk, L1_xattn_Wv, L1_xattn_Wo, L1_ffn_w_gate, L1_ffn_w_up, L1_ffn_w_down):
    import jax
    import jax.numpy as jnp

    def _L0_xattn_ref(x, x_attention_mask, style_tokens, style_attention_mask, ln_w, Wq, Wkv, Wo):
        import jax, jax.numpy as jnp
        import numpy as np
        LN_EPS = 1e-05
        NEG = -1000000000.0

        def _layernorm(x, w):
            xf = x.astype(jnp.float32)
            mu = jnp.mean(xf, axis=-1, keepdims=True)
            var = jnp.mean(jnp.square(xf - mu), axis=-1, keepdims=True)
            return (xf - mu) * jax.lax.rsqrt(var + LN_EPS) * w
        B, S, dim = x.shape
        H = 16
        D = dim // H
        xq = _layernorm(x, ln_w)
        q = (xq @ Wq).reshape(B, S, H, D)
        kv = (style_tokens @ Wkv).reshape(B, -1, 2, H, D)
        k, v = (kv[:, :, 0], kv[:, :, 1])
        scores = jnp.einsum('bshd,blhd->bhsl', q, k) / np.sqrt(D)
        kvm = style_attention_mask[:, None, None, :]
        scores = jnp.where(kvm > 0, scores, NEG)
        attn = jax.nn.softmax(scores, axis=-1)
        out = jnp.einsum('bhsl,blhd->bshd', attn, v)
        out = out * x_attention_mask[:, :, None, None].astype(out.dtype)
        out = out.reshape(B, S, dim)
        return out @ Wo

    def _L0_ffn_ref(x, router_w, w1, b1, w2, b2):
        import jax, jax.numpy as jnp
        import numpy as np
        N_EMBD = 256
        NUM_EXPERTS = 8
        TOP_K = 2

        def new_gelu(x):
            c = jnp.sqrt(2.0 / jnp.pi).astype(x.dtype)
            return 0.5 * x * (1.0 + jnp.tanh(c * (x + 0.044715 * x ** 3)))
        B, T, C = x.shape
        E = router_w.shape[0]
        x_flat = x.reshape(B * T, C)
        router_logits = x_flat @ router_w.T
        router_probs = jax.nn.softmax(router_logits, axis=-1)
        top_k_probs, top_k_idx = jax.lax.top_k(router_probs, TOP_K)
        top_k_probs = top_k_probs / (top_k_probs.sum(axis=-1, keepdims=True) + 1e-08)
        cw = (jax.nn.one_hot(top_k_idx, E, dtype=x.dtype) * top_k_probs[..., None]).sum(axis=1)
        output = jnp.zeros_like(x_flat)
        for e in range(E):
            h = new_gelu(x_flat @ w1[e].T + b1[e])
            out_e = h @ w2[e].T + b2[e]
            output = output + cw[:, e:e + 1] * out_e
        return output.reshape(B, T, C)

    def _L1_xattn_ref(query, key, value, Wq, Wk, Wv, Wo):
        import jax, jax.numpy as jnp
        import numpy as np
        B, S, D = (1, 1024, 256)
        NUM_HEADS, HEAD_DIM = (16, 64)
        WINDOW = 128
        EMBED = NUM_HEADS * HEAD_DIM
        Bq, Sq, _ = query.shape
        q = (query @ Wq).reshape(Bq, Sq, NUM_HEADS, HEAD_DIM).transpose(0, 2, 1, 3)
        k = (key @ Wk).reshape(Bq, Sq, NUM_HEADS, HEAD_DIM).transpose(0, 2, 1, 3)
        v = (value @ Wv).reshape(Bq, Sq, NUM_HEADS, HEAD_DIM).transpose(0, 2, 1, 3)
        idx = jnp.arange(Sq)
        local_mask = jnp.abs(idx[:, None] - idx[None, :]) > WINDOW
        scores = jnp.einsum('bhqd,bhkd->bhqk', q, k) / jnp.sqrt(jnp.float32(HEAD_DIM))
        scores = jnp.where(local_mask, -jnp.inf, scores)
        attn = jax.nn.softmax(scores, axis=-1)
        out = jnp.einsum('bhqk,bhkd->bhqd', attn, v)
        out = out.transpose(0, 2, 1, 3).reshape(Bq, Sq, EMBED)
        return out @ Wo

    def _L1_ffn_ref(x, w_gate, w_up, w_down):
        import jax, jax.numpy as jnp
        import numpy as np
        BLOCK = 32
        W_BITS = 4
        ACT_BITS = 16

        def act_qdq(x):
            qmax = 2.0 ** (ACT_BITS - 1) - 1.0
            scale = jnp.maximum(jnp.max(jnp.abs(x)) / qmax, 1e-12)
            return jnp.clip(jnp.round(x / scale), -qmax - 1.0, qmax) * scale

        def fixed_qdq_u16(x):
            scale = 1.0 / 65536.0
            return jnp.clip(jnp.round(x / scale), 0.0, 65535.0) * scale

        def lpbq_dequant(w):
            O, I = w.shape
            qmax = 2.0 ** (W_BITS - 1) - 1.0
            wb = w.reshape(O, I // BLOCK, BLOCK)
            s = jnp.maximum(jnp.max(jnp.abs(wb), axis=-1, keepdims=True) / qmax, 1e-12)
            wq = jnp.clip(jnp.round(wb / s), -qmax - 1.0, qmax) * s
            return wq.reshape(O, I)
        x = act_qdq(x)
        up = act_qdq(x @ lpbq_dequant(w_up).T)
        gate = act_qdq(x @ lpbq_dequant(w_gate).T)
        sig = fixed_qdq_u16(jax.nn.sigmoid(gate))
        gate = act_qdq(gate * sig)
        o = act_qdq(gate * up)
        return o @ lpbq_dequant(w_down).T
    x = x + _L0_xattn_ref(_layernorm(x, axis=-1), mask_BxS_ik0, ctx_1024, mask_BxS2_ik1, L0_xattn_ln_w, L0_xattn_Wq, L0_xattn_Wkv, L0_xattn_Wo)
    x = x + _L0_ffn_ref(_layernorm(x, axis=-1), L0_ffn_router_w, L0_ffn_w1, L0_ffn_b1, L0_ffn_w2, L0_ffn_b2)
    x = x + _L1_xattn_ref(_layernorm(x, axis=-1), ctx_1024, ctx_1024, L1_xattn_Wq, L1_xattn_Wk, L1_xattn_Wv, L1_xattn_Wo)
    x = x + _L1_ffn_ref(_layernorm(x, axis=-1), L1_ffn_w_gate, L1_ffn_w_up, L1_ffn_w_down)
    return x

_drawn_inputs = setup_inputs


def setup_inputs(seed=0):
    import zlib

    import numpy as np

    out = dict(_drawn_inputs(seed))
    spreads = {'L0_xattn_ln_w': (1.0, 0.6), 'L0_ffn_b1': (0.0, 0.357), 'L0_ffn_b2': (0.0, 0.1)}
    factors = {}
    for name, (base, spread) in spreads.items():
        noise = np.random.default_rng([zlib.crc32(name.encode()), seed]).standard_normal(out[name].shape)
        drawn = base * np.exp(spread * noise) if base else spread * noise
        out[name] = jnp.asarray(drawn.astype(out[name].dtype))
    for name, factor in factors.items():
        out[name] = (out[name] * factor).astype(out[name].dtype)
    return out
```

```python
from contextlib import ExitStack

import numpy as np

import concourse.bass as bass
from concourse import mybir

ALU = mybir.AluOpType
ACT = mybir.ActivationFunctionType
AX = mybir.AxisListType
F32 = mybir.dt.float32
F32R = mybir.dt.float32r
BF16 = mybir.dt.bfloat16
I32 = mybir.dt.int32
I16 = mybir.dt.int16
U32 = mybir.dt.uint32

P = 128
B, S, D = 4, 512, 256
T = B * S
NT = T // P
TPB = S // P
KC = D // P
LN_EPS = 1e-5
NEG = -1e9

H0, DH0 = 16, 16
G0 = 4
NG0 = H0 // G0
SLOT = P // G0


def round_f32r(v):
    bits = np.array([v], np.float32).view(np.uint32).astype(np.uint64)
    return float(((bits + 0x800) & 0xFFFFF000).astype(np.uint32).view(np.float32)[0])


class Chain:

    def __init__(self, engine, sem):
        self.engine, self.sem, self.base, self.turn, self.per, self.n = engine, sem, 0, None, 0, 0

    def loop(self, turn, per):
        self.turn, self.per, self.n = turn, per, 0

    def end(self, turns):
        assert self.n == self.per, (self.sem, self.n, self.per)
        self.base += turns * self.per
        self.turn, self.n = None, 0

    def add(self, instruction):
        instruction.then_inc(self.sem, 1)
        self.n += 1

    def wait(self):
        at = self.base + self.n
        self.engine.wait_ge(self.sem, at if self.turn is None else self.turn * self.per + at)

    def step(self, instruction):
        self.add(instruction)
        self.wait()

    def close(self):
        self.base += self.n
        self.n = 0


def rsqrt_steps(nc, chain, out, v, tmp):
    chain.step(nc.vector.tensor_scalar(out.bitcast(I32), v.bitcast(I32), -0.5, float(0x5F3759DF), ALU.mult, ALU.add))
    for _ in range(3):
        chain.step(nc.vector.scalar_tensor_tensor(out=tmp, in0=out, scalar=-0.5, in1=out, op0=ALU.mult, op1=ALU.mult))
        chain.step(nc.vector.tensor_tensor(tmp, tmp, v, ALU.mult))
        chain.step(nc.vector.scalar_tensor_tensor(out=out, in0=tmp, scalar=1.5, in1=out, op0=ALU.add, op1=ALU.mult))


RSQRT_STEPS = 10


def layernorm_steps(nc, chain, x_tok, tile0, out, st, twice, last_sem):
    v = nc.vector
    for i in range(TPB):
        chain.add(v.bn_stats(st["stats"][:, i, :], x_tok[:, bass.ds(tile0 + i, 1), :].rearrange("p a d -> p (a d)")))
    chain.wait()
    chain.add(v.memset(st["carrier"][:], 0.0))
    for i in range(TPB):
        chain.add(v.bn_aggr(st["mv"][:, i, :], st["stats"][:, i, :]))
    chain.wait()
    mean, var = st["mv"][:, :, 0], st["mv"][:, :, 1]
    chain.step(v.tensor_scalar(st["ve"][:], var, LN_EPS, None, ALU.add))
    rsqrt_steps(nc, chain, st["r"][:], st["ve"][:], st["tmp"][:])
    if twice:
        chain.step(v.tensor_tensor(st["ve"][:], st["r"][:], st["r"][:], ALU.mult))
        chain.step(v.tensor_tensor(st["ve"][:], st["ve"][:], var, ALU.mult))
        chain.step(v.tensor_scalar(st["ve"][:], st["ve"][:], LN_EPS, None, ALU.add))
        rsqrt_steps(nc, chain, st["r2"][:], st["ve"][:], st["tmp"][:])
        chain.step(v.tensor_tensor(st["r"][:], st["r"][:], st["r2"][:], ALU.mult))
    chain.step(v.scalar_tensor_tensor(out=st["nm"][:], in0=mean, scalar=-1.0, in1=st["r"][:], op0=ALU.mult, op1=ALU.mult))
    for i in range(TPB):
        ins = v.tensor_scalar(out[:, i, :], x_tok[:, bass.ds(tile0 + i, 1), :].rearrange("p a d -> p (a d)"),
                              st["r"][:, i:i + 1], st["nm"][:, i:i + 1], ALU.mult, ALU.add)
        if i == TPB - 1:
            ins.then_inc(last_sem, 1)


def layernorm_links(twice):
    return 2 * TPB + 2 + RSQRT_STEPS + 1 + (4 + RSQRT_STEPS if twice else 0)


def layernorm_buffers(sb, tag):
    return {"stats": sb(f"{tag}_stats", [P, TPB, 6], F32), "mv": sb(f"{tag}_mv", [P, TPB, 2], F32), "carrier": sb(f"{tag}_carrier", [P, 1], F32),
            **{n: sb(f"{tag}_{n}", [P, TPB], F32) for n in ("ve", "r", "r2", "tmp", "nm")}}


def scopes(nc, ctx):
    def sb(name, shape, dt=F32):
        return ctx.enter_context(nc.sbuf_tensor(name, shape, dt))

    def sem(name):
        return ctx.enter_context(nc.semaphore(name))

    return sb, sem


def load_inputs(nc, x_dram, x_tok, ident, xmask_dram, xmask_i, xmask):
    with ExitStack() as ctx:
        sb, sem = scopes(nc, ctx)
        loaded, stored, built = sem("x_loaded"), sem("xmask_ready"), sem("ident_built")
        block = ctx.enter_context(nc.Block())

        @block.sync
        def _(sp):
            sp.dma_start(x_tok[:], x_dram.rearrange("b (t p) d -> p (b t) d", p=P)).then_inc(loaded, 16)
            sp.dma_start(xmask_i[:], xmask_dram).then_inc(loaded, 16)
            sp.wait_ge(loaded, 32)

        @block.gpsimd
        def _(pool):
            pool.memset(ident[:], 0.0).then_inc(built, 1)
            pool.wait_ge(built, 1)
            pool.affine_select(out=ident[:], in_=ident[:], compare_op=ALU.not_equal, fill=1.0, base=0,
                               pattern=[[-1, P]], channel_multiplier=1).then_inc(built, 1)
            pool.wait_ge(built, 2)

        @block.vector
        def _(dve):
            dve.wait_ge(loaded, 32)
            nc.vector.tensor_copy(xmask[:], xmask_i[:]).then_inc(stored, 1)
            dve.wait_ge(stored, 1)


def project_l0(nc, psum, x_tok, ident, ctxT_dram, kvmask_dram, ln_w_dram, wq_dram, wk_dram, wv_dram,
               q_scr, k_scr, kneg_scr, v_scr):
    HI, LO = 0, 1
    MG = P // (G0 * DH0)
    with ExitStack() as ctx:
        sb, sem = scopes(nc, ctx)
        wq, wk, wv = (sb(n, [P, KC, D]) for n in ("wq0", "wk0", "wv0"))
        lnw = sb("lnw", [P, KC])
        ctxT = sb("ctxT", [P, KC, S])
        kv_i = sb("kv_i", [P, T], I32)
        kv = sb("kv", [P, T])
        sc_mul, sc_add = sb("sc_mul", [2, 1]), sb("sc_add", [2, 1])
        kneg = sb("kneg", [2, T], F32R)
        hn = sb("hn", [P, TPB, D])
        hT = sb("hT", [P, KC, S])
        km = sb("km", [P, KC, S])
        parts = {n: sb(n, [P, KC, S], F32R) for n in ("q_hi", "q_lo", "k_hi", "k_lo")}
        vaug = sb("vaug", [P, TPB, H0 * SLOT])
        st = layernorm_buffers(sb, "ln0")
        ps_t, ps_q, ps_k, ps_v = psum[:, 0:2], psum[:, 2:4], psum[:, 4:6], psum[:, 6:8]

        w_in, kv_in, ctx_in = sem("w_in"), sem("kv_in"), sem("ctx_in")
        link = sem("dve_link")
        hn_ready, hT_psum, hT_ready = sem("hn_ready"), sem("hT_psum"), sem("hT_ready")
        q_psum, k_psum, v_psum = sem("q_psum"), sem("k_psum"), sem("v_psum")
        km_ready, kneg_ready, ones_ready = sem("km_ready"), sem("kneg_ready"), sem("ones_ready")
        k_hi_ready, q_hi_ready, k_lo_ready, q_lo_ready = (sem(n) for n in ("k_hi_ready", "q_hi_ready", "k_lo_ready", "q_lo_ready"))
        v_ready = sem("v_ready")
        k_out, v_out, q_out, kneg_out = sem("k_out"), sem("v_out"), sem("q_out"), sem("kneg_out")
        block = ctx.enter_context(nc.Block())

        def rows(scr, part, b):
            return scr[part, bass.ds(b, 1)].rearrange("a (k p) n -> p (a k) n", p=P)

        @block.sync
        def _(sp):
            sp.dma_start(ctxT[:], ctxT_dram[0].rearrange("(k p) n -> p k n", p=P)).then_inc(ctx_in, 16)
            for w, dram in ((wk, wk_dram), (wv, wv_dram), (wq, wq_dram)):
                sp.dma_start(w[:], dram.rearrange("(k p) n -> p k n", p=P)).then_inc(w_in, 16)
            sp.dma_start(lnw[:], ln_w_dram).then_inc(w_in, 16)
            sp.dma_start(kv_i[:], kvmask_dram.partition_broadcast(P)).then_inc(kv_in, 16)

            def turn(b, more):
                if more:
                    sp.wait_ge(v_psum, b + 1)
                    sp.dma_start(ctxT[:], ctxT_dram[bass.ds(b + 1, 1)].rearrange("a (k p) n -> p (a k) n", p=P)).then_inc(ctx_in, 16)
                sp.wait_ge(k_lo_ready, b + 1)
                sp.dma_start(rows(k_scr, HI, b), parts["k_hi"][:].bitcast(F32)).then_inc(k_out, 16)
                sp.dma_start(rows(k_scr, LO, b), parts["k_lo"][:].bitcast(F32)).then_inc(k_out, 16)
                sp.wait_ge(v_ready, 2 * b + 2)
                for g in range(NG0):
                    sp.dma_start(v_scr[bass.ds(b, 1), g].rearrange("a t p n -> p (a t) n"),
                                 vaug[:, :, g * P:(g + 1) * P]).then_inc(v_out, 16)
                sp.wait_ge(q_lo_ready, b + 1)
                sp.dma_start(rows(q_scr, HI, b), parts["q_hi"][:].bitcast(F32)).then_inc(q_out, 16)
                sp.dma_start(rows(q_scr, LO, b), parts["q_lo"][:].bitcast(F32)).then_inc(q_out, 16)

            with sp.Fori(0, B - 1) as b:
                turn(b, True)
            turn(B - 1, False)
            sp.wait_ge(kneg_ready, 1)
            for g in range(NG0):
                sp.dma_start(kneg_scr[:, g].rearrange("b r n -> r b n"),
                             kneg[:].bitcast(F32).rearrange("r (b n) -> r b n", b=B)).then_inc(kneg_out, 16)
            sp.wait_ge(kneg_out, 16 * NG0)
            sp.wait_ge(k_out, 32 * B)
            sp.wait_ge(v_out, 16 * NG0 * B)
            sp.wait_ge(q_out, 32 * B)

        @block.tensor
        def _(pe):
            pe.wait_ge(w_in, 64)
            with pe.Fori(0, B) as b:
                pe.wait_ge(ctx_in, 16 * b + 16)
                for m in range(KC):
                    for k in range(KC):
                        last = nc.tensor.matmul(ps_k[:, m], wk[:, k, m * P:(m + 1) * P], ctxT[:, k], start=k == 0, stop=k == KC - 1)
                last.then_inc(k_psum, 1)
                for t in range(TPB):
                    for k in range(KC):
                        last = nc.tensor.matmul(ps_v[:, t // 2, (t % 2) * D:(t % 2 + 1) * D], ctxT[:, k, t * P:(t + 1) * P],
                                                wv[:, k], start=k == 0, stop=k == KC - 1)
                last.then_inc(v_psum, 1)
                pe.wait_ge(hn_ready, b + 1)
                for k in range(KC):
                    for t in range(TPB):
                        last = nc.tensor.transpose(ps_t[:, k, t * P:(t + 1) * P], hn[:, t, k * P:(k + 1) * P], ident[:])
                last.then_inc(hT_psum, 1)
                pe.wait_ge(hT_ready, KC * b + KC)
                for m in range(KC):
                    for k in range(KC):
                        last = nc.tensor.matmul(ps_q[:, m], wq[:, k, m * P:(m + 1) * P], hT[:, k], start=k == 0, stop=k == KC - 1)
                last.then_inc(q_psum, 1)
                pe.wait_ge(km_ready, b + 1)
                pe.wait_ge(v_ready, 2 * b + 2)
                pe.wait_ge(q_lo_ready, b + 1)

        @block.scalar
        def _(act):
            act.wait_ge(w_in, 64)
            act.wait_ge(ones_ready, 1)
            with act.Fori(0, B) as b:
                act.wait_ge(km_ready, b + 1)
                nc.scalar.activation(parts["k_hi"][:], km[:], ACT.Copy).then_inc(k_hi_ready, 1)
                act.wait_ge(v_psum, b + 1)
                for half in range(2):
                    out = vaug[:, 2 * half:2 * half + 2].rearrange("p t (h e) -> p (t h) e", e=SLOT)[:, :, 0:DH0]
                    nc.scalar.activation(out, ps_v[:, half].rearrange("p (h e) -> p h e", e=DH0), ACT.Copy).then_inc(v_ready, 1)
                act.wait_ge(hT_psum, b + 1)
                for k in range(KC):
                    nc.scalar.activation(hT[:, k], ps_t[:, k], ACT.Copy, scale=lnw[:, k:k + 1]).then_inc(hT_ready, 1)
                act.wait_ge(q_psum, b + 1)
                nc.scalar.activation(parts["q_hi"][:], ps_q, ACT.Copy, scale=DH0 ** -0.5).then_inc(q_hi_ready, 1)
                act.wait_ge(k_out, 32 * b + 32)
                act.wait_ge(v_out, 16 * NG0 * b + 16 * NG0)
                act.wait_ge(q_out, 32 * b + 32)

        @block.vector
        def _(dve):
            v = nc.vector
            chain = Chain(dve, link)
            v.memset(vaug[:], 1.0).then_inc(ones_ready, 1)
            hi = round_f32r(NEG)
            chain.add(v.memset(sc_mul[:], -(NEG - hi)))
            chain.step(v.memset(sc_add[:], NEG - hi))
            chain.add(v.memset(sc_mul[0:1], -hi))
            chain.step(v.memset(sc_add[0:1], hi))
            dve.wait_ge(kv_in, 16)
            chain.step(v.tensor_scalar(kv[:], kv_i[:], 0.0, None, ALU.is_gt))
            v.tensor_scalar(kneg[:], kv[0:2], sc_mul[:, 0:1], sc_add[:, 0:1], ALU.mult, ALU.add).then_inc(kneg_ready, 1)
            chain.close()
            with dve.Fori(0, B) as b:
                chain.loop(b, layernorm_links(True))
                layernorm_steps(nc, chain, x_tok, b * TPB, hn, st, True, hn_ready)
                chain.end(B)
                dve.wait_ge(k_psum, b + 1)
                for m in range(KC):
                    ins = v.tensor_tensor(km[:, m], ps_k[:, m], kv[:, bass.ds(b * S, S)], ALU.mult)
                ins.then_inc(km_ready, 1)
                dve.wait_ge(k_hi_ready, b + 1)
                v.tensor_tensor(parts["k_lo"][:], km[:], parts["k_hi"][:].bitcast(F32), ALU.subtract).then_inc(k_lo_ready, 1)
                dve.wait_ge(q_hi_ready, b + 1)
                v.scalar_tensor_tensor(out=parts["q_lo"][:], in0=ps_q, scalar=DH0 ** -0.5,
                                       in1=parts["q_hi"][:].bitcast(F32), op0=ALU.mult, op1=ALU.subtract).then_inc(q_lo_ready, 1)
                dve.wait_ge(k_out, 32 * b + 32)
                dve.wait_ge(q_out, 32 * b + 32)


def attend_l0(nc, psum, q_scr, k_scr, kneg_scr, v_scr, attnT):
    NGRP = B * NG0
    AHEAD, NBUF = 2, 4
    R_MASK, R_MAX, R_ALL = 4 * DH0, 4 * DH0 + 2, 4 * DH0 + 4
    LOADS = 2 * 4 + 1 + 1
    MAX_IN = 16 * 2 * 4
    with ExitStack() as ctx:
        sb, sem = scopes(nc, ctx)
        qs = [sb(f"qs{n}", [R_ALL, G0, S], F32R) for n in range(NBUF)]
        ks = [sb(f"ks{n}", [R_ALL, G0, S], F32R) for n in range(NBUF)]
        vs = [sb(f"vs{n}", [P, TPB, G0 * SLOT]) for n in range(NBUF)]
        nmax = sb("nmax", [P, NBUF, G0 * TPB])
        mparts = sb("mparts", [P, 2 * G0 * TPB])
        mpartsT = sb("mpartsT", [P, NBUF, 2 * G0 * TPB], F32)
        mhi = sb("mhi", [P, G0 * TPB], F32R)
        probs = sb("probs", [P, 2, G0, S])
        marks = sb("marks", [P, 2 * 2])
        ps_s1, ps_s2, ps_o = psum[:, 0:2], psum[:, 2:6], psum[:, 6:8]

        loaded = [sem(f"grp_loaded{n}") for n in range(NBUF)]
        rows_set, link = sem("rows_set"), sem("a0_link")
        s1_psum, s1_max, maxT_ready = sem("s1_psum"), sem("s1_max"), sem("maxT_ready")
        max_in = [sem(f"max_in{n}") for n in range(NBUF)]
        s2_psum, probs_ready, pv_done, o_read = sem("s2_psum"), sem("probs_ready"), sem("pv_done"), sem("o_read")
        block = ctx.enter_context(nc.Block())

        FREE = 2

        def turns(engine, body):
            with engine.Fori(0, NGRP // NBUF - 1) as t:
                body(t * NBUF, True)
            body(NGRP - NBUF, False)

        @block.sync
        def _(sp):
            def load(i, n):
                for dst, scr, order in ((qs[n], q_scr, (0, 0, 1, 1)), (ks[n], k_scr, (0, 1, 0, 1))):
                    for r, part in enumerate(order):
                        sp.dma_start(dst[r * DH0:(r + 1) * DH0].bitcast(F32),
                                     scr[part].rearrange("b (g j d) n -> d (b g) j n", j=G0, d=DH0)[:, bass.ds(i, 1)]
                                     .rearrange("d a j n -> d (a j) n")).then_inc(loaded[n], 16)
                neg = kneg_scr.rearrange("b g r n -> r (b g) n")[:, bass.ds(i, 1)]
                sp.dma_start(ks[n][R_MASK:R_MASK + 2].bitcast(F32), neg.to_broadcast([2, G0, S])).then_inc(loaded[n], 16)
                sp.dma_start(vs[n][:], v_scr.rearrange("b g t p n -> p (b g) t n")[:, bass.ds(i, 1)]
                             .rearrange("p a t n -> p (a t) n")).then_inc(loaded[n], 16)

            def put_max(i, n):
                sp.wait_ge(maxT_ready, i + 1)
                for part in range(2):
                    dst = qs[n][R_MAX + part:R_MAX + part + 1].bitcast(F32).rearrange("r j (t c q) -> r c (j t) q", c=4, q=32)
                    for c in range(4):
                        sp.dma_start(dst[:, c], mpartsT[32 * c + 16 * part:32 * c + 16 * part + 16, n, :]).then_inc(max_in[n], 16)

            sp.wait_ge(rows_set, 1)
            for i in range(AHEAD + 1):
                load(i, i)
            put_max(0, 0)

            def body(i0, more):
                for n in range(NBUF):
                    i = i0 + n
                    if more or n < NBUF - 1:
                        put_max(i + 1, (n + 1) % NBUF)
                    if more or n + AHEAD + 1 < NBUF:
                        sp.wait_ge(pv_done, i * TPB + FREE)
                        load(i + AHEAD + 1, (n + AHEAD + 1) % NBUF)

            turns(sp, body)

        @block.tensor
        def _(pe):
            def s1(i, n, s0, s1_, wait_bank):
                for s in range(s0, s1_):
                    j, t = divmod(s, TPB)
                    if wait_bank or s >= 2:
                        pe.wait_ge(s1_max, i * 16 + s - 1)
                    nc.tensor.matmul(ps_s1[:, s % 2], qs[n][0:R_MAX, j, t * P:(t + 1) * P], ks[n][0:R_MAX, j, :],
                                     start=True, stop=True).then_inc(s1_psum, 1)

            def s2(i, n, c, half):
                if c == half == 0:
                    pe.wait_ge(max_in[n], (i - n) * (MAX_IN // NBUF) + MAX_IN)
                for j in (2 * half, 2 * half + 1):
                    ins = nc.tensor.matmul(ps_s2[:, j], ks[n][:, j, c * P:(c + 1) * P], qs[n][:, j, :], start=True, stop=True)
                ins.then_inc(s2_psum, 1)

            for i in range(AHEAD):
                pe.wait_ge(loaded[i], 16 * LOADS)
                s1(i, i, 0, 16, i > 0)
            s2(0, 0, 0, 0)
            s2(0, 0, 0, 1)

            def body(i0, more):
                for n in range(NBUF):
                    i, na = i0 + n, (n + AHEAD) % NBUF
                    ahead = more or n + AHEAD < NBUF
                    if ahead:
                        pe.wait_ge(loaded[na], (i + AHEAD - na) * (16 * LOADS // NBUF) + 16 * LOADS)
                    for c in range(TPB):
                        step = i * TPB + c
                        i2, n2, c2 = (i, n, c + 1) if c + 1 < TPB else (i + 1, (n + 1) % NBUF, 0)
                        for half in range(2):
                            pe.wait_ge(probs_ready, step * 2 + half + 1)
                            if more or n2 or c2:
                                s2(i2, n2, c2, half)
                            if half == 1:
                                if c == 0:
                                    pe.wait_ge(o_read, i - 1 + FREE)
                                for j in range(G0):
                                    ins = nc.tensor.matmul(ps_o[SLOT * j:SLOT * (j + 1), n % 2], vs[n][:, c, SLOT * j:SLOT * (j + 1)],
                                                           probs[:, c % 2, j, :], start=c == 0, stop=c == TPB - 1)
                                ins.then_inc(pv_done, 1)
                            if ahead:
                                s1(i + AHEAD, na, 4 * c + 2 * half, 4 * c + 2 * half + 2, True)

            turns(pe, body)

        @block.scalar
        def _(act):
            def exps(step, c):
                for half in range(2):
                    act.wait_ge(s2_psum, step * 2 + half + 1)
                    if half == 0:
                        act.wait_ge(pv_done, step - 1 + FREE)
                    nc.scalar.activation(probs[:, c % 2, 2 * half:2 * half + 2], ps_s2[:, 2 * half:2 * half + 2],
                                         ACT.Exp).then_inc(probs_ready, 1)

            exps(0, 0)
            exps(1, 1)

            def body(i0, more):
                for n in range(NBUF):
                    i = i0 + n
                    exps(i * TPB + 2, 2)
                    exps(i * TPB + 3, 3)
                    if more or n < NBUF - 1:
                        exps(i * TPB + 4, 0)
                        exps(i * TPB + 5, 1)
                    act.wait_ge(pv_done, (i + 1) * TPB + FREE)
                    nc.scalar.activation(attnT[:, bass.ds(i, 1)].rearrange("p a n -> p (a n)"), ps_o[:, n % 2], ACT.Copy).then_inc(o_read, 1)

            turns(act, body)

        @block.vector
        def _(dve):
            v = nc.vector
            chain = Chain(dve, link)
            for f in range(FREE):
                v.memset(marks[:, 2 * f:2 * f + 1], 0.0).then_inc(pv_done, 1)
                v.memset(marks[:, 2 * f + 1:2 * f + 2], 0.0).then_inc(o_read, 1)
            dve.wait_ge(o_read, FREE)
            for n in range(NBUF):
                v.memset(qs[n][R_MASK:R_ALL].bitcast(F32), 1.0)
                ins = v.memset(ks[n][R_MASK:R_ALL].bitcast(F32), 1.0)
            ins.then_inc(rows_set, 1)

            def maxima(i, n, s0, s1_):
                for s in range(s0, s1_):
                    dve.wait_ge(s1_psum, i * 16 + s + 1)
                    v.tensor_reduce(nmax[:, n, s:s + 1], ps_s1[:, s % 2], AX.X, ALU.max, negate=True).then_inc(s1_max, 1)

            def split_max(i, n):
                dve.wait_ge(s1_max, i * 16 + 16)
                chain.step(v.tensor_copy(mhi[:], nmax[:, n]))
                chain.add(v.tensor_copy(mparts[:, 0:16], mhi[:].bitcast(F32)))
                chain.step(v.tensor_tensor(mparts[:, 16:32], nmax[:, n], mhi[:].bitcast(F32), ALU.subtract))
                v.transpose(mpartsT[:, n], mparts[:]).then_inc(maxT_ready, 1)
                dve.wait_ge(maxT_ready, i + 1)

            for i in range(AHEAD):
                maxima(i, i, 0, 16)
            split_max(0, 0)
            chain.close()

            def body(i0, more):
                for n in range(NBUF):
                    i = i0 + n
                    ahead = more or n + AHEAD < NBUF
                    if more or n < NBUF - 1:
                        split_max(i + 1, (n + 1) % NBUF)
                    if ahead:
                        maxima(i + AHEAD, (n + AHEAD) % NBUF, 0, 16)

            with dve.Fori(0, NGRP // NBUF - 1) as t:
                chain.loop(t, NBUF * 3)
                body(t * NBUF, True)
                chain.end(NGRP // NBUF - 1)
            body(NGRP - NBUF, False)


def finish_l0(nc, psum, x_tok, attnT, sum_scr, rec_scr, wo_dram, xmask):
    NGRP = B * NG0
    with ExitStack() as ctx:
        sb, sem = scopes(nc, ctx)
        wo = sb("wo0", [P, NG0, D])
        sums, inv = sb("sums", [P, NGRP * G0 * S // P]), sb("inv", [P, NGRP * G0 * S // P])
        scale = sb("scale", [P, 2, NG0, S])
        at = sb("at", [P, 2, NG0, S])
        w_in, sums_out, sums_in, inv_ready, inv_out = sem("wo_in"), sem("sums_out"), sem("sums_in"), sem("inv_ready"), sem("inv_out")
        scale_in = [sem(f"scale_in{n}") for n in range(2)]
        at_ready, y_psum, y_read = sem("at_ready"), sem("y_psum"), sem("y_read")
        block = ctx.enter_context(nc.Block())

        @block.sync
        def _(sp):
            sp.dma_start(wo[:], wo_dram).then_inc(w_in, 16)
            for j in range(G0):
                sp.dma_start(sum_scr[:, j].unsqueeze(0), attnT[SLOT * j + DH0:SLOT * j + DH0 + 1]).then_inc(sums_out, 16)
            sp.wait_ge(sums_out, 16 * G0)
            sp.dma_start(sums[:], sum_scr.rearrange("g j (a m) -> (g j a) m", a=P // (NGRP * G0))).then_inc(sums_in, 16)
            sp.wait_ge(inv_ready, 1)
            sp.dma_start(rec_scr.rearrange("g j (a m) -> (g j a) m", a=P // (NGRP * G0)), inv[:]).then_inc(inv_out, 16)
            sp.wait_ge(inv_out, 16)

            def spread(b, n):
                for j in range(G0):
                    src = rec_scr[bass.ds(b * NG0, NG0), j].unsqueeze(0).to_broadcast([SLOT, NG0, S])
                    sp.dma_start(scale[SLOT * j:SLOT * (j + 1), n], src).then_inc(scale_in[n], 16)

            spread(0, 0)
            spread(1, 1)
            with sp.Fori(1, B // 2) as t:
                for n in range(2):
                    sp.wait_ge(at_ready, 2 * t + n - 1)
                    spread(2 * t + n, n)

        @block.gpsimd
        def _(pool):
            with pool.Fori(0, B // 2) as t:
                for n in range(2):
                    pool.wait_ge(scale_in[n], 16 * G0 * t + 16 * G0)
                    nc.gpsimd.tensor_tensor(at[:, n], attnT[:, bass.ds((2 * t + n) * NG0, NG0)], scale[:, n], ALU.mult).then_inc(at_ready, 1)
                for n in range(2):
                    pool.wait_ge(y_psum, (2 * t + n + 1) * TPB)

        @block.tensor
        def _(pe):
            pe.wait_ge(w_in, 16)
            with pe.Fori(0, B // 2) as t:
                for n in range(2):
                    pe.wait_ge(at_ready, 2 * t + n + 1)
                    for i in range(TPB):
                        for g in range(NG0):
                            last = nc.tensor.matmul(psum[:, 4 * n + i, 0:D], at[:, n, g, i * P:(i + 1) * P], wo[:, g], start=g == 0, stop=g == NG0 - 1)
                        last.then_inc(y_psum, 1)
                pe.wait_ge(y_read, (2 * t + 2) * TPB)

        @block.vector
        def _(dve):
            dve.wait_ge(sums_in, 16)
            nc.vector.reciprocal(inv[:], sums[:]).then_inc(inv_ready, 1)
            with dve.Fori(0, B // 2) as t:
                for n in range(2):
                    for i in range(TPB):
                        tile = (2 * t + n) * TPB + i
                        dve.wait_ge(y_psum, tile + 1)
                        x = x_tok[:, bass.ds(tile, 1)].rearrange("p a d -> p (a d)")
                        nc.vector.scalar_tensor_tensor(out=x, in0=psum[:, 4 * n + i, 0:D], scalar=xmask[:, bass.ds(tile, 1)], in1=x,
                                                       op0=ALU.mult, op1=ALU.add).then_inc(y_read, 1)
            dve.wait_ge(y_read, NT)


E0, HID = 8, 1024
MH = HID // P
CPE = B


def route_l0(nc, psum, x_tok, ident, router_dram, b2_dram, hT_all, cw):
    with ExitStack() as ctx:
        sb, sem = scopes(nc, ctx)
        wr, b2 = sb("wr", [P, KC, E0]), sb("b2", [E0, D])
        hn = sb("hn1", [P, TPB, D])
        hT = sb("hT1", [P, KC, S])
        st = layernorm_buffers(sb, "ln1")
        logits, probs, top = sb("logits", [P, NT, E0]), sb("rprobs", [P, NT, E0]), sb("top", [P, NT, E0])
        idx, idx_f, iota_i, iota = sb("idx", [P, NT, E0], U32), sb("idx_f", [P, NT, E0]), sb("iota_i", [P, E0], I32), sb("iota", [P, E0])
        hot, col, col2 = sb("hot", [P, NT, E0]), sb("col", [P, NT]), sb("col2", [P, NT])
        cwT = sb("cwT", [E0, NT, P])
        ps_t, ps_l = psum[:, 0:2], psum[:, 2]
        w_in, link, hn_ready, hT_psum, hT_ready = sem("r_in"), sem("r_link"), sem("r_hn"), sem("r_hT_psum"), sem("r_hT")
        l_psum, iota_ready, e_ready, shifted, cwT_psum, cwT_ready, y_psum = (
            sem(f"r_{n}") for n in ("logits", "iota", "exp", "shifted", "cwT_psum", "cwT", "y"))
        block = ctx.enter_context(nc.Block())

        @block.sync
        def _(sp):
            sp.dma_start(wr[:], router_dram.rearrange("(k p) e -> p k e", p=P)).then_inc(w_in, 16)
            sp.dma_start(b2[:], b2_dram).then_inc(w_in, 16)

        @block.gpsimd
        def _(pool):
            pool.iota(iota_i[:], pattern=[[1, E0]], base=0, channel_multiplier=0).then_inc(iota_ready, 1)

        @block.tensor
        def _(pe):
            pe.wait_ge(w_in, 32)
            with pe.Fori(0, B) as b:
                pe.wait_ge(hn_ready, b + 1)
                for k in range(KC):
                    for t in range(TPB):
                        last = nc.tensor.transpose(ps_t[:, k, t * P:(t + 1) * P], hn[:, t, k * P:(k + 1) * P], ident[:])
                last.then_inc(hT_psum, 1)
                pe.wait_ge(hT_ready, 2 * b + 2)
                for t in range(TPB):
                    for k in range(KC):
                        last = nc.tensor.matmul(ps_l[:, bass.ds(b * (TPB * E0) + t * E0, E0)], hT[:, k, t * P:(t + 1) * P], wr[:, k], start=k == 0, stop=k == KC - 1)
                last.then_inc(l_psum, 1)
            pe.wait_ge(shifted, 2)
            for t in range(NT):
                last = nc.tensor.transpose(psum[0:E0, 3 + t // 4, (t % 4) * P:(t % 4 + 1) * P], cw[:, t, :], ident[:])
            last.then_inc(cwT_psum, 1)
            pe.wait_ge(cwT_ready, 1)
            for t in range(NT):
                nc.tensor.matmul(psum[:, t // 2, (t % 2) * D:(t % 2 + 1) * D], cwT[:, t], b2[:], start=True, stop=True).then_inc(y_psum, 1)

        @block.scalar
        def _(act):
            with act.Fori(0, B) as b:
                act.wait_ge(hT_psum, b + 1)
                nc.scalar.activation(hT[:], ps_t, ACT.Copy).then_inc(hT_ready, 1)
                nc.scalar.activation(hT_all[:, :, bass.ds(b * S, S)], ps_t, ACT.Copy).then_inc(hT_ready, 1)
                act.wait_ge(l_psum, b + 1)
            act.wait_ge(shifted, 1)
            nc.scalar.activation(probs[:], logits[:], ACT.Exp).then_inc(e_ready, 1)
            act.wait_ge(cwT_psum, 1)
            nc.scalar.activation(cwT[:].rearrange("e t p -> e (t p)"), psum[0:E0, 3:7].rearrange("e k n -> e (k n)"), ACT.Copy).then_inc(cwT_ready, 1)

        @block.vector
        def _(dve):
            v = nc.vector
            chain = Chain(dve, link)
            with dve.Fori(0, B) as b:
                chain.loop(b, layernorm_links(False))
                layernorm_steps(nc, chain, x_tok, b * TPB, hn, st, False, hn_ready)
                chain.end(B)
                dve.wait_ge(hT_psum, b + 1)
            wide = [P, NT, E0]
            dve.wait_ge(l_psum, B)
            lg = ps_l[:, 0:NT * E0].rearrange("p (t e) -> p t e", e=E0)
            chain.step(v.tensor_reduce(col[:], lg, AX.X, ALU.max))
            v.tensor_tensor(logits[:], lg, col[:].unsqueeze(2).to_broadcast(wide), ALU.subtract).then_inc(shifted, 1)
            dve.wait_ge(e_ready, 1)
            chain.step(v.tensor_reduce(col[:], probs[:], AX.X, ALU.add))
            chain.step(v.reciprocal(col2[:], col[:]))
            chain.step(v.tensor_tensor(logits[:], probs[:], col2[:].unsqueeze(2).to_broadcast(wide), ALU.mult))
            for t in range(NT):
                chain.add(v.max(top[:, t], logits[:, t]))
            chain.wait()
            for t in range(NT):
                chain.add(v.max_index(idx[:, t], top[:, t], logits[:, t]))
            dve.wait_ge(iota_ready, 1)
            chain.add(v.tensor_copy(iota[:], iota_i[:]))
            chain.wait()
            chain.step(v.tensor_copy(idx_f[:], idx[:]))
            chain.step(v.tensor_tensor(col[:], top[:, :, 0], top[:, :, 1], ALU.add))
            chain.step(v.tensor_scalar(col[:], col[:], 1e-8, None, ALU.add))
            chain.step(v.reciprocal(col2[:], col[:]))
            chain.step(v.tensor_tensor(top[:, :, 0:2], top[:, :, 0:2], col2[:].unsqueeze(2).to_broadcast([P, NT, 2]), ALU.mult))
            iota_w = iota[:].unsqueeze(1).to_broadcast(wide)
            chain.step(v.tensor_tensor(cw[:], iota_w, idx_f[:, :, 0:1].to_broadcast(wide), ALU.is_equal))
            chain.step(v.tensor_tensor(cw[:], cw[:], top[:, :, 0:1].to_broadcast(wide), ALU.mult))
            chain.step(v.tensor_tensor(hot[:], iota_w, idx_f[:, :, 1:2].to_broadcast(wide), ALU.is_equal))
            chain.step(v.tensor_tensor(hot[:], hot[:], top[:, :, 1:2].to_broadcast(wide), ALU.mult))
            v.tensor_tensor(cw[:], cw[:], hot[:], ALU.add).then_inc(shifted, 1)
            chain.close()
            for t in range(NT):
                dve.wait_ge(y_psum, t - t % 2 + 2)
                chain.add(v.tensor_tensor(x_tok[:, t], x_tok[:, t], psum[:, t // 2, (t % 2) * D:(t % 2 + 1) * D], ALU.add))
            chain.wait()


def experts_l0(nc, psum, x_tok, hT_all, cw, w1_dram, b1_dram, w2_dram):
    with ExitStack() as ctx:
        sb, sem = scopes(nc, ctx)
        w1 = [sb(f"w1_{n}", [P, KC, HID]) for n in range(2)]
        w2 = [sb(f"w2_{n}", [P, MH, D]) for n in range(2)]
        b1 = [sb(f"b1_{n}", [P, MH]) for n in range(2)]
        hid = sb("hid", [P, 2, MH, S])
        w_in = [sem(f"e_w_in{n}") for n in range(2)]
        h_psum, h_ready, y_psum, y_read = sem("e_h_psum"), sem("e_h"), sem("e_y_psum"), sem("e_y_read")
        block = ctx.enter_context(nc.Block())

        @block.sync
        def _(sp):
            def load(e, n):
                sp.dma_start(w1[n][:], w1_dram[bass.ds(e, 1)].rearrange("a (k p) h -> p (a k) h", p=P)).then_inc(w_in[n], 16)
                sp.dma_start(w2[n][:], w2_dram[bass.ds(e, 1)].rearrange("a (m p) c -> p (a m) c", p=P)).then_inc(w_in[n], 16)
                sp.dma_start(b1[n][:], b1_dram[bass.ds(e, 1)].rearrange("a p m -> p (a m)")).then_inc(w_in[n], 16)

            load(0, 0)
            load(1, 1)
            with sp.Fori(0, E0 // 2 - 1) as t:
                for n in range(2):
                    sp.wait_ge(y_psum, (2 * t + n + 1) * NT)
                    load(2 * t + n + 2, n)

        @block.tensor
        def _(pe):
            with pe.Fori(0, E0 // 2) as t:
                for n in range(2):
                    e = 2 * t + n
                    pe.wait_ge(w_in[n], 48 * t + 48)
                    for c in range(CPE):
                        for m in range(MH):
                            if not (n == c == 0 and m < 4):
                                pe.wait_ge(h_ready, (e * CPE + c) * MH + m - 3)
                            for k in range(KC):
                                last = nc.tensor.matmul(psum[:, m % 4], w1[n][:, k, m * P:(m + 1) * P], hT_all[:, k, c * S:(c + 1) * S], start=k == 0, stop=k == KC - 1)
                            last.then_inc(h_psum, 1)
                        pe.wait_ge(h_ready, (e * CPE + c + 1) * MH)
                        for i in range(TPB):
                            if not (n == c == 0):
                                pe.wait_ge(y_read, (e * CPE + c - 1) * TPB + i + 1)
                            for m in range(MH):
                                last = nc.tensor.matmul(psum[:, 4 + i, 0:D], hid[:, c % 2, m, i * P:(i + 1) * P], w2[n][:, m], start=m == 0, stop=m == MH - 1)
                            last.then_inc(y_psum, 1)
                pe.wait_ge(y_read, (2 * t + 2) * NT)

        @block.scalar
        def _(act):
            with act.Fori(0, E0 // 2) as t:
                for n in range(2):
                    for c in range(CPE):
                        for m in range(MH):
                            act.wait_ge(h_psum, ((2 * t + n) * CPE + c) * MH + m + 1)
                            nc.scalar.activation(hid[:, c % 2, m], psum[:, m % 4], ACT.Gelu_apprx_tanh, bias=b1[n][:, m:m + 1]).then_inc(h_ready, 1)

        @block.vector
        def _(dve):
            with dve.Fori(0, E0 // 2) as t:
                for n in range(2):
                    e = 2 * t + n
                    for c in range(CPE):
                        for i in range(TPB):
                            tile = c * TPB + i
                            dve.wait_ge(y_psum, e * NT + tile + 1)
                            nc.vector.scalar_tensor_tensor(out=x_tok[:, tile], in0=psum[:, 4 + i, 0:D], scalar=cw[:, tile, bass.ds(e, 1)],
                                                           in1=x_tok[:, tile], op0=ALU.mult, op1=ALU.add).then_inc(y_read, 1)
                dve.wait_ge(y_read, (2 * t + 2) * NT)


H1, DH1 = 16, 64
NP1 = H1 // 2
E1 = H1 * DH1
W3 = 3 * P
MASKED = -1e30


def attend_l1(nc, psum, x_tok, ident, ctxT_dram, wq_dram, wk_dram, wv_dram, wo_dram):
    UNITS = NP1 * TPB
    with ExitStack() as ctx:
        sb, sem = scopes(nc, ctx)
        wq, wk, wv = (sb(n, [P, KC, E1]) for n in ("wq1", "wk1", "wv1"))
        wo = sb("wo1", [P, NP1, D])
        ctxT, hn, hT = sb("ctxT1", [P, KC, S]), sb("hn2", [P, TPB, D]), sb("hT2", [P, KC, S])
        vv = sb("v1", [P, TPB, E1])
        attnT = sb("attnT1", [P, NP1, S])
        xa, xb, ya = (sb(n, [P, 2, 2, S], F32R) for n in ("q_hilo", "q_lohi", "k_hilo"))
        band_f, band, ident_b = sb("band_f", [P, 3, P]), sb("band", [P, 3, P], BF16), sb("ident_b", [P, P], BF16)
        pr = sb("pr", [P, TPB, 2, W3])
        prT = sb("prT", [P, 2, 2, W3])
        nmax, sums, inv = (sb(n, [P, TPB, 2]) for n in ("nmax1", "sums1", "inv1"))
        st = layernorm_buffers(sb, "ln2")
        names = ("w_in", "ctx_in", "band_fill", "band_ready", "link", "hn_ready", "hT_psum", "hT_ready", "v_psum", "v_ready",
                 "q_psum", "q_hi", "q_lo", "k_psum", "k_hi", "k_lo", "s_psum", "max_ready", "exp_ready", "inv_ready",
                 "p_ready", "t_psum", "t_read", "pv_done", "o_read", "y_psum", "y_read")
        s = {n: sem(f"l1_{n}") for n in names}
        xb_in = [sem(f"l1_xb_in{n}") for n in range(2)]
        block = ctx.enter_context(nc.Block())

        def window(qt):
            k0, k1 = max(0, qt - 1), min(TPB - 1, qt + 1)
            return k0, (k1 - k0 + 1) * P

        @block.sync
        def _(sp):
            for w, dram in ((wq, wq_dram), (wk, wk_dram), (wv, wv_dram)):
                sp.dma_start(w[:], dram.rearrange("(k p) n -> p k n", p=P)).then_inc(s["w_in"], 16)
            sp.dma_start(wo[:], wo_dram.rearrange("(m p) n -> p m n", p=P)).then_inc(s["w_in"], 16)

            def load_ctx(b):
                sp.dma_start(ctxT[:], ctxT_dram[bass.ds(b, 1)].rearrange("a (k p) n -> p (a k) n", p=P)).then_inc(s["ctx_in"], 16)

            def turn(b, more):
                for p in range(NP1):
                    n = p % 2
                    sp.wait_ge(s["q_lo"], b * NP1 + p + 1)
                    sp.dma_start(xb[0:DH1, n].bitcast(F32), xa[DH1:P, n].bitcast(F32)).then_inc(xb_in[n], 16)
                    sp.dma_start(xb[DH1:P, n].bitcast(F32), xa[0:DH1, n].bitcast(F32)).then_inc(xb_in[n], 16)
                if more:
                    sp.wait_ge(s["k_lo"], b * NP1 + NP1)
                    load_ctx(b + 1)

            load_ctx(0)
            with sp.Fori(0, B - 1) as b:
                turn(b, True)
            turn(B - 1, False)

        @block.gpsimd
        def _(pool):
            pool.memset(band_f[:], 0.0).then_inc(s["band_fill"], 1)
            pool.wait_ge(s["band_fill"], 1)
            pool.affine_select(out=band_f[:, 0], in_=band_f[:, 0], compare_op=ALU.is_ge, fill=MASKED, base=0, pattern=[[1, P]], channel_multiplier=-1).then_inc(s["band_fill"], 1)
            pool.affine_select(out=band_f[:, 2], in_=band_f[:, 2], compare_op=ALU.is_ge, fill=MASKED, base=0, pattern=[[-1, P]], channel_multiplier=1).then_inc(s["band_fill"], 1)
            with pool.Fori(0, B) as b:
                for u in range(UNITS):
                    qt = u % TPB
                    _, w = window(qt)
                    pool.wait_ge(s["inv_ready"], b * UNITS + u + 1)
                    nc.gpsimd.tensor_tensor(pr[:, qt, :, 0:w], pr[:, qt, :, 0:w], inv[:, qt].unsqueeze(2).to_broadcast([P, 2, w]),
                                            ALU.mult).then_inc(s["p_ready"], 1)

        @block.tensor
        def _(pe):
            mm = nc.tensor.matmul

            def project(b, p, w, src, done, prev, prev_n):
                if prev_n is not None:
                    pe.wait_ge(s[prev], prev_n)
                for k in range(KC):
                    last = mm(psum[:, 7], w[:, k, p * P:(p + 1) * P], src[:, k], start=k == 0, stop=k == KC - 1)
                last.then_inc(s[done], 1)

            def q_of(b, p):
                project(b, p, wq, hT, "q_psum", "k_lo", b * NP1 + p if p else None)

            def k_of(b, p):
                project(b, p, wk, ctxT, "k_psum", "q_lo", b * NP1 + p + 1)

            def scores(b, u):
                p, qt = divmod(u, TPB)
                n, (k0, w) = p % 2, window(qt)
                if qt == 0:
                    pe.wait_ge(s["k_lo"], b * NP1 + p + 1)
                    pe.wait_ge(xb_in[n], b * (NP1 * 16) + (p // 2 + 1) * 32)
                if u >= 2:
                    pe.wait_ge(s["exp_ready"], b * UNITS + u - 1)
                for a in range(2):
                    out = psum[:, 2 * (u % 2) + a, 0:w]
                    mm(out, xa[:, n, a, qt * P:(qt + 1) * P], ya[:, n, a, k0 * P:k0 * P + w], start=True, stop=False)
                    mm(out, xb[:, n, a, qt * P:(qt + 1) * P], ya[:, n, a, k0 * P:k0 * P + w], start=False, stop=False)
                    off = P if qt == 0 else 0
                    last = mm(out, ident_b[:], band[:].rearrange("p c n -> p (c n)")[:, off:off + w], start=False, stop=True)
                last.then_inc(s["s_psum"], 1)

            def turn_probs(b, u):
                qt = u % TPB
                _, w = window(qt)
                pe.wait_ge(s["p_ready"], b * UNITS + u + 1)
                if u:
                    pe.wait_ge(s["t_read"], b * UNITS + u)
                for a in range(2):
                    for c in range(w // P):
                        last = nc.tensor.transpose(psum[:, 4 + a, c * P:(c + 1) * P], pr[:, qt, a, c * P:(c + 1) * P], ident[:])
                last.then_inc(s["t_psum"], 1)

            def product(b, u):
                p, qt = divmod(u, TPB)
                k0, w = window(qt)
                pe.wait_ge(s["t_read"], b * UNITS + u + 1)
                if qt == 0 and p:
                    pe.wait_ge(s["o_read"], b * NP1 + p)
                for c in range(w // P):
                    for a in range(2):
                        last = mm(psum[DH1 * a:DH1 * (a + 1), 6, qt * P:(qt + 1) * P], vv[:, k0 + c, p * P + a * DH1:p * P + (a + 1) * DH1],
                                  prT[:, u % 2, a, c * P:(c + 1) * P], start=c == 0, stop=c == w // P - 1)
                last.then_inc(s["pv_done"], 1)

            pe.wait_ge(s["w_in"], 64)
            pe.wait_ge(s["band_ready"], 1)
            with pe.Fori(0, B) as b:
                pe.wait_ge(s["hn_ready"], b + 1)
                for k in range(KC):
                    for t in range(TPB):
                        last = nc.tensor.transpose(psum[:, k, t * P:(t + 1) * P], hn[:, t, k * P:(k + 1) * P], ident[:])
                last.then_inc(s["hT_psum"], 1)
                pe.wait_ge(s["ctx_in"], b * 16 + 16)
                for i in range(2 * TPB):
                    t, half = divmod(i, 2)
                    if i >= 4:
                        pe.wait_ge(s["v_ready"], b * 8 + i - 3)
                    for k in range(KC):
                        last = mm(psum[:, 2 + i % 4], ctxT[:, k, t * P:(t + 1) * P], wv[:, k, half * S:(half + 1) * S], start=k == 0, stop=k == KC - 1)
                    last.then_inc(s["v_psum"], 1)
                pe.wait_ge(s["hT_ready"], b + 1)
                q_of(b, 0)
                k_of(b, 0)
                q_of(b, 1)
                pe.wait_ge(s["v_ready"], b * 8 + 8)
                scores(b, 0)
                scores(b, 1)
                for u in range(UNITS):
                    p, qt = divmod(u, TPB)
                    if qt == 0 and p + 1 < NP1:
                        k_of(b, p + 1)
                    if u + 2 < UNITS:
                        scores(b, u + 2)
                    if qt == 3 and p + 2 < NP1:
                        q_of(b, p + 2)
                    turn_probs(b, u)
                    if u:
                        product(b, u - 1)
                product(b, UNITS - 1)
                pe.wait_ge(s["o_read"], b * NP1 + NP1)
                for i in range(TPB):
                    for p in range(NP1):
                        last = mm(psum[:, i, 0:D], attnT[:, p, i * P:(i + 1) * P], wo[:, p], start=p == 0, stop=p == NP1 - 1)
                    last.then_inc(s["y_psum"], 1)
                pe.wait_ge(s["y_read"], b * TPB + TPB)

        @block.scalar
        def _(act):
            def hi(b, p, name, dst, scale):
                act.wait_ge(s[name + "_psum"], b * NP1 + p + 1)
                for a in range(2):
                    last = nc.scalar.activation(dst[0:DH1, p % 2, a], psum[DH1 * a:DH1 * (a + 1), 7], ACT.Copy, scale=scale)
                last.then_inc(s[name + "_hi"], 1)

            def exps(b, u):
                qt = u % TPB
                _, w = window(qt)
                act.wait_ge(s["max_ready"], b * UNITS + u + 1)
                if u >= 4:
                    act.wait_ge(s["t_psum"], b * UNITS + u - 3)
                for a in range(2):
                    last = nc.scalar.activation(pr[:, qt, a, 0:w], psum[:, 2 * (u % 2) + a, 0:w], ACT.Exp, bias=nmax[:, qt, a:a + 1],
                                                accum_out=sums[:, qt, a:a + 1])
                last.then_inc(s["exp_ready"], 1)

            with act.Fori(0, B) as b:
                act.wait_ge(s["hT_psum"], b + 1)
                nc.scalar.activation(hT[:], psum[:, 0:2], ACT.Copy).then_inc(s["hT_ready"], 1)
                for i in range(2 * TPB):
                    t, half = divmod(i, 2)
                    act.wait_ge(s["v_psum"], b * 8 + i + 1)
                    nc.scalar.activation(vv[:, t, half * S:(half + 1) * S], psum[:, 2 + i % 4], ACT.Copy).then_inc(s["v_ready"], 1)
                hi(b, 0, "q", xa, DH1 ** -0.5)
                hi(b, 0, "k", ya, 1.0)
                hi(b, 1, "q", xa, DH1 ** -0.5)
                exps(b, 0)
                exps(b, 1)
                for u in range(UNITS):
                    p, qt = divmod(u, TPB)
                    if qt == 0 and p + 1 < NP1:
                        hi(b, p + 1, "k", ya, 1.0)
                    if u + 2 < UNITS:
                        exps(b, u + 2)
                    if qt == 3 and p + 2 < NP1:
                        hi(b, p + 2, "q", xa, DH1 ** -0.5)
                    if qt == 0 and p:
                        act.wait_ge(s["pv_done"], b * UNITS + u)
                        nc.scalar.activation(attnT[:, p - 1], psum[:, 6], ACT.Copy).then_inc(s["o_read"], 1)
                act.wait_ge(s["pv_done"], b * UNITS + UNITS)
                nc.scalar.activation(attnT[:, NP1 - 1], psum[:, 6], ACT.Copy).then_inc(s["o_read"], 1)
                act.wait_ge(s["y_psum"], b * TPB + TPB)

        @block.vector
        def _(dve):
            v = nc.vector
            chain = Chain(dve, s["link"])
            dve.wait_ge(s["band_fill"], 3)
            chain.add(v.tensor_copy(ident_b[:], ident[:]))
            v.tensor_copy(band[:], band_f[:]).then_inc(s["band_ready"], 1)
            chain.close()

            def lo(b, p, name, dst, scale):
                dve.wait_ge(s[name + "_hi"], b * NP1 + p + 1)
                for a in range(2):
                    last = v.scalar_tensor_tensor(out=dst[DH1:P, p % 2, a], in0=psum[DH1 * a:DH1 * (a + 1), 7], scalar=scale,
                                                  in1=dst[0:DH1, p % 2, a].bitcast(F32), op0=ALU.mult, op1=ALU.subtract)
                last.then_inc(s[name + "_lo"], 1)

            def maxima(b, u):
                qt = u % TPB
                _, w = window(qt)
                dve.wait_ge(s["s_psum"], b * UNITS + u + 1)
                v.tensor_reduce(nmax[:, qt], psum[:, 2 * (u % 2):2 * (u % 2) + 2, 0:w], AX.X, ALU.max, negate=True).then_inc(s["max_ready"], 1)

            def invert(b, u):
                qt = u % TPB
                dve.wait_ge(s["exp_ready"], b * UNITS + u + 1)
                v.reciprocal(inv[:, qt], sums[:, qt]).then_inc(s["inv_ready"], 1)

            with dve.Fori(0, B) as b:
                chain.loop(b, layernorm_links(False))
                layernorm_steps(nc, chain, x_tok, b * TPB, hn, st, False, s["hn_ready"])
                chain.end(B)
                lo(b, 0, "q", xa, DH1 ** -0.5)
                lo(b, 0, "k", ya, 1.0)
                lo(b, 1, "q", xa, DH1 ** -0.5)
                maxima(b, 0)
                maxima(b, 1)
                invert(b, 0)
                for u in range(UNITS):
                    p, qt = divmod(u, TPB)
                    _, w = window(qt)
                    if qt == 0 and p + 1 < NP1:
                        lo(b, p + 1, "k", ya, 1.0)
                    if u + 2 < UNITS:
                        maxima(b, u + 2)
                    if qt == 3 and p + 2 < NP1:
                        lo(b, p + 2, "q", xa, DH1 ** -0.5)
                    if u + 1 < UNITS:
                        invert(b, u + 1)
                    dve.wait_ge(s["t_psum"], b * UNITS + u + 1)
                    if u >= 2:
                        dve.wait_ge(s["pv_done"], b * UNITS + u - 1)
                    v.tensor_copy(prT[:, u % 2, :, 0:w], psum[:, 4:6, 0:w]).then_inc(s["t_read"], 1)
                for i in range(TPB):
                    dve.wait_ge(s["y_psum"], b * TPB + i + 1)
                    x = x_tok[:, bass.ds(b * TPB + i, 1)].rearrange("p a d -> p (a d)")
                    v.tensor_tensor(x, x, psum[:, i, 0:D], ALU.add).then_inc(s["y_read"], 1)
                dve.wait_ge(s["y_read"], b * TPB + TPB)


FF = 768
MF = FF // P
BLK = 32
QMAX16, QMAX4 = 32767.0, 7.0
SCALE_MIN = 1e-12


def quantised_input_l1(nc, psum, x_tok, ident, wg_dram, wu_dram, wd_dram, wgT, wuT, wdT, hqT):
    with ExitStack() as ctx:
        sb, sem = scopes(nc, ctx)
        raw = {"g": sb("wg_raw", [P, MF, D]), "u": sb("wu_raw", [P, MF, D]), "d": sb("wd_raw", [P, KC, FF])}
        NBLK = MF * D // BLK
        bs, binv = sb("bs", [P, NBLK]), sb("binv", [P, NBLK])
        w16 = sb("w16", [P, MF * D], I16)
        hn = sb("hn_all", [P, NT, D])
        h16 = sb("h16", [P, NT, D], I16)
        st = layernorm_buffers(sb, "ln3")
        mx, mx1, gmax, scale, inv = sb("f_mx", [P, B]), sb("f_mx1", [P, 1]), sb("f_gmax", [P, 1]), sb("f_scale", [P, 1]), sb("f_inv", [P, 1])
        names = ("w_in", "link", "ln_done", "mx_ready", "gmax_ready", "wq_ready", "wT_psum", "wT_read", "hq_ready", "hT_psum", "hT_read")
        s = {n: sem(f"f1_{n}") for n in names}
        block = ctx.enter_context(nc.Block())

        @block.sync
        def _(sp):
            sp.dma_start(raw["g"][:], wg_dram.rearrange("(m p) c -> p m c", p=P)).then_inc(s["w_in"], 16)
            sp.dma_start(raw["u"][:], wu_dram.rearrange("(m p) c -> p m c", p=P)).then_inc(s["w_in"], 16)
            sp.dma_start(raw["d"][:], wd_dram.rearrange("(m p) c -> p m c", p=P)).then_inc(s["w_in"], 16)

        @block.gpsimd
        def _(pool):
            pool.wait_ge(s["mx_ready"], 1)
            nc.gpsimd.partition_all_reduce(gmax[:], mx1[:], P, bass.bass_isa.ReduceOp.max).then_inc(s["gmax_ready"], 1)

        @block.vector
        def _(dve):
            v = nc.vector
            chain = Chain(dve, s["link"])
            with dve.Fori(0, B) as b:
                chain.loop(b, layernorm_links(False) + 1)
                out = hn[:, bass.ds(b * TPB, TPB)]
                layernorm_steps(nc, chain, x_tok, b * TPB, out, st, False, s["ln_done"])
                dve.wait_ge(s["ln_done"], b + 1)
                chain.step(v.tensor_reduce(mx[:, bass.ds(b, 1)], out.rearrange("p t c -> p (t c)"), AX.X, ALU.max, apply_absolute_value=True))
                chain.end(B)
            v.tensor_reduce(mx1[:], mx[:], AX.X, ALU.max).then_inc(s["mx_ready"], 1)
            dve.wait_ge(s["w_in"], 48)
            for n, name in enumerate(("g", "u", "d")):
                w = raw[name][:].rearrange("p a (n k) -> p (a n) k", k=BLK)
                q = w16[:].rearrange("p (n k) -> p n k", k=BLK)
                wide = [P, NBLK, BLK]
                chain.step(v.tensor_reduce(bs[:], w, AX.X, ALU.max, apply_absolute_value=True))
                chain.step(v.tensor_scalar(bs[:], bs[:], 1.0 / QMAX4, SCALE_MIN, ALU.mult, ALU.max))
                chain.step(v.reciprocal(binv[:], bs[:]))
                chain.step(v.tensor_tensor(q, w, binv[:].unsqueeze(2).to_broadcast(wide), ALU.mult))
                chain.step(v.tensor_scalar(w, q, QMAX4, -QMAX4 - 1.0, ALU.min, ALU.max))
                chain.add(v.tensor_tensor(w, w, bs[:].unsqueeze(2).to_broadcast(wide), ALU.mult))
                chain.wait()
                v.memset(mx[:, n:n + 1], 0.0).then_inc(s["wq_ready"], 1)
            dve.wait_ge(s["gmax_ready"], 1)
            chain.step(v.tensor_scalar(scale[:], gmax[:], 1.0 / QMAX16, SCALE_MIN, ALU.mult, ALU.max))
            chain.step(v.reciprocal(inv[:], scale[:]))
            chain.step(v.tensor_scalar(h16[:], hn[:], inv[:], None, ALU.mult))
            v.tensor_scalar(hn[:], h16[:], scale[:], None, ALU.mult).then_inc(s["hq_ready"], 1)
            dve.wait_ge(s["hq_ready"], 1)

        @block.tensor
        def _(pe):
            def turned(jobs, group0, done, read):
                for g in range(0, len(jobs), 4):
                    i = group0 + g // 4
                    if i >= 8:
                        pe.wait_ge(s[read], i - 7)
                    for n, job in enumerate(jobs[g:g + 4]):
                        last = nc.tensor.transpose(psum[:, i % 8, n * P:(n + 1) * P], job, ident[:])
                    last.then_inc(s[done], 1)

            for n, name in enumerate(("g", "u", "d")):
                pe.wait_ge(s["wq_ready"], n + 1)
                rows, cols = (MF, KC) if name != "d" else (KC, MF)
                jobs = [raw[name][:, m, k * P:(k + 1) * P] for k in range(cols) for m in range(rows)]
                turned(jobs, 3 * n, "wT_psum", "wT_read")
            pe.wait_ge(s["hq_ready"], 1)
            pe.wait_ge(s["wT_read"], 9)
            turned([hn[:, t, k * P:(k + 1) * P] for k in range(KC) for t in range(NT)], 0, "hT_psum", "hT_read")

        @block.scalar
        def _(act):
            for n, dst in enumerate((wgT, wuT, wdT)):
                flat = dst[:].rearrange("p a n -> p (a n)")
                for g in range(3):
                    i = 3 * n + g
                    act.wait_ge(s["wT_psum"], i + 1)
                    nc.scalar.activation(flat[:, g * 512:(g + 1) * 512], psum[:, i % 8], ACT.Copy).then_inc(s["wT_read"], 1)
            flat = hqT[:].rearrange("p k n -> p (k n)")
            for i in range(KC * B):
                act.wait_ge(s["hT_psum"], i + 1)
                nc.scalar.activation(flat[:, i * 512:(i + 1) * 512], psum[:, i % 8], ACT.Copy).then_inc(s["hT_read"], 1)


def gated_l1(nc, psum, x_tok, wgT, wuT, wdT, hqT):
    CH = MF * S
    with ExitStack() as ctx:
        sb, sem = scopes(nc, ctx)
        gate, up = sb("gate", [P, B, CH]), sb("up", [P, B, CH])
        a16, b16 = sb("a16", [P, CH], I16), sb("b16", [P, CH], mybir.dt.uint16)
        sig = sb("sig", [P, CH])
        mx = sb("g_mx", [P, 2, B])
        mx1, gmax, k = sb("g_mx1", [P, 2]), sb("g_gmax", [P, 2]), sb("g_k", [P, 12])
        names = ("psum", "read", "mx", "gmax", "a", "sig", "link", "o", "y_psum", "y_read", "o_used")
        s = {n: sem(f"f2_{n}") for n in names}
        block = ctx.enter_context(nc.Block())
        S_G, I_G, S_U, I_U, C2, S_2, I_2, SO_IN, S_O, I_O, T0, T1 = (k[:, i:i + 1] for i in range(12))

        @block.tensor
        def _(pe):
            with pe.Fori(0, B) as c:
                for m in range(MF):
                    for n, w in enumerate((wgT, wuT)):
                        i = 2 * m + n
                        if i >= 8:
                            pe.wait_ge(s["read"], c * (2 * MF) + i - 7)
                        for kk in range(KC):
                            last = nc.tensor.matmul(psum[:, i % 8], w[:, kk, m * P:(m + 1) * P], hqT[:, kk, bass.ds(c * S, S)], start=kk == 0, stop=kk == KC - 1)
                        last.then_inc(s["psum"], 1)
                pe.wait_ge(s["read"], (c + 1) * (2 * MF))
            for c in range(B):
                pe.wait_ge(s["o"], c + 1)
                for i in range(TPB):
                    t = c * TPB + i
                    if t >= 8:
                        pe.wait_ge(s["y_read"], t - 7)
                    for m in range(MF):
                        last = nc.tensor.matmul(psum[:, t % 8, 0:D], gate[:, c, m * S + i * P:m * S + (i + 1) * P], wdT[:, m], start=m == 0, stop=m == MF - 1)
                    last.then_inc(s["y_psum"], 1)

        @block.scalar
        def _(act):
            with act.Fori(0, B) as c:
                for i in range(2 * MF):
                    m, n = divmod(i, 2)
                    act.wait_ge(s["psum"], c * (2 * MF) + i + 1)
                    dst = (gate, up)[n][:, bass.ds(c, 1), m * S:(m + 1) * S].rearrange("p a n -> p (a n)")
                    nc.scalar.activation(dst, psum[:, i % 8], ACT.Copy).then_inc(s["read"], 1)
            for c in range(B):
                act.wait_ge(s["a"], c + 1)
                nc.scalar.activation(sig[:], a16[:], ACT.Sigmoid, scale=S_G).then_inc(s["sig"], 1)
            for c in range(B):
                act.wait_ge(s["a"], B + c + 1)
                nc.scalar.activation(gate[:, c], a16[:], ACT.Copy, scale=S_O).then_inc(s["o"], 1)

        @block.gpsimd
        def _(pool):
            for n in range(3):
                pool.wait_ge(s["mx"], n + 1)
                nc.gpsimd.partition_all_reduce(gmax[:], mx1[:], P, bass.bass_isa.ReduceOp.max).then_inc(s["gmax"], 1)

        @block.vector
        def _(dve):
            v = nc.vector
            chain = Chain(dve, s["link"])

            def biggest(n):
                v.tensor_reduce(mx1[:], mx[:], AX.X, ALU.max).then_inc(s["mx"], 1)
                dve.wait_ge(s["gmax"], n)

            for c in range(B):
                dve.wait_ge(s["read"], (c + 1) * 2 * MF)
                chain.add(v.tensor_reduce(mx[:, 0, c:c + 1], gate[:, c], AX.X, ALU.max, apply_absolute_value=True))
                chain.add(v.tensor_reduce(mx[:, 1, c:c + 1], up[:, c], AX.X, ALU.max, apply_absolute_value=True))
            chain.wait()
            biggest(1)
            for out, out_i, n in ((S_G, I_G, 0), (S_U, I_U, 1)):
                chain.step(v.tensor_scalar(out, gmax[:, n:n + 1], 1.0 / QMAX16, SCALE_MIN, ALU.mult, ALU.max))
                chain.add(v.reciprocal(out_i, out))
            chain.add(v.tensor_scalar(C2, S_G, 1.0 / 65536.0, None, ALU.mult))
            chain.wait()
            for c in range(B):
                v.tensor_scalar(a16[:], gate[:, c], I_G, None, ALU.mult).then_inc(s["a"], 1)
                dve.wait_ge(s["sig"], c + 1)
                chain.step(v.tensor_scalar(b16[:], sig[:], 65536.0, None, ALU.mult))
                chain.step(v.tensor_tensor(gate[:, c], a16[:], b16[:], ALU.mult))
                chain.step(v.tensor_reduce(mx[:, 0, c:c + 1], gate[:, c], AX.X, ALU.max, apply_absolute_value=True))
            biggest(2)
            chain.step(v.tensor_tensor(T0, gmax[:, 0:1], C2, ALU.mult))
            chain.step(v.tensor_scalar(S_2, T0, 1.0 / QMAX16, SCALE_MIN, ALU.mult, ALU.max))
            chain.step(v.reciprocal(I_2, S_2))
            chain.step(v.tensor_tensor(T0, I_2, C2, ALU.mult))
            for c in range(B):
                chain.add(v.tensor_scalar(a16[:], gate[:, c], T0, None, ALU.mult))
                chain.step(v.tensor_scalar(b16[:].bitcast(I16), up[:, c], I_U, None, ALU.mult))
                chain.step(v.tensor_tensor(gate[:, c], a16[:], b16[:].bitcast(I16), ALU.mult))
                chain.step(v.tensor_reduce(mx[:, 0, c:c + 1], gate[:, c], AX.X, ALU.max, apply_absolute_value=True))
            biggest(3)
            chain.step(v.tensor_tensor(SO_IN, S_2, S_U, ALU.mult))
            chain.step(v.tensor_tensor(T1, gmax[:, 0:1], SO_IN, ALU.mult))
            chain.step(v.tensor_scalar(S_O, T1, 1.0 / QMAX16, SCALE_MIN, ALU.mult, ALU.max))
            chain.step(v.reciprocal(I_O, S_O))
            chain.step(v.tensor_tensor(T1, I_O, SO_IN, ALU.mult))
            for c in range(B):
                if c:
                    dve.wait_ge(s["o"], c)
                v.tensor_scalar(a16[:], gate[:, c], T1, None, ALU.mult).then_inc(s["a"], 1)
            for t in range(NT):
                dve.wait_ge(s["y_psum"], t + 1)
                v.tensor_tensor(x_tok[:, t], x_tok[:, t], psum[:, t % 8, 0:D], ALU.add).then_inc(s["y_read"], 1)
            dve.wait_ge(s["y_read"], NT)


def store_x(nc, x_tok, out_dram):
    with ExitStack() as ctx:
        _, sem = scopes(nc, ctx)
        stored = sem("x_stored")
        block = ctx.enter_context(nc.Block())

        @block.sync
        def _(sp):
            sp.dma_start(out_dram.rearrange("b (t p) d -> p (b t) d", p=P), x_tok[:]).then_inc(stored, 16)
            sp.wait_ge(stored, 16)


def build(nc, a, out, stages=4):
    with ExitStack() as ctx:
        sb, sem = scopes(nc, ctx)
        x_tok = sb("x_tok", [P, NT, D])
        ident = sb("ident", [P, P])
        xmask_i, xmask = sb("xmask_i", [P, NT], I32), sb("xmask", [P, NT])
        psum = ctx.enter_context(nc.psum_tensor("psum", [P, 8, 512], F32))

        def scratch(name, shape, dt=F32):
            return nc.dram_tensor(name, shape, dt, kind="Internal").ap()

        q_scr, k_scr = scratch("q_scr", (2, B, D, S)), scratch("k_scr", (2, B, D, S))
        kneg_scr, v_scr = scratch("kneg_scr", (B, NG0, 2, S)), scratch("v_scr", (B, NG0, TPB, P, P))
        sum_scr, rec_scr = scratch("sum_scr", (B * NG0, G0, S)), scratch("rec_scr", (B * NG0, G0, S))
        load_inputs(nc, a["x"], x_tok, ident, a["xmask"], xmask_i, xmask)
        project_l0(nc, psum[:], x_tok, ident, a["ctxT"], a["kvmask"], a["ln_w"], a["wq0"], a["wk0"], a["wv0"],
                   q_scr, k_scr, kneg_scr, v_scr)
        with nc.sbuf_tensor("attnT", [P, B * NG0, S], F32) as attnT:
            attend_l0(nc, psum[:], q_scr, k_scr, kneg_scr, v_scr, attnT)
            finish_l0(nc, psum[:], x_tok, attnT, sum_scr, rec_scr, a["wo0"], xmask)
        if stages >= 2:
            with nc.sbuf_tensor("hT_all", [P, KC, T], F32) as hT_all, nc.sbuf_tensor("cw", [P, NT, E0], F32) as cw:
                route_l0(nc, psum[:], x_tok, ident, a["router"], a["b2"], hT_all, cw)
                experts_l0(nc, psum[:], x_tok, hT_all, cw, a["w1"], a["b1"], a["w2"])
        if stages >= 3:
            attend_l1(nc, psum[:], x_tok, ident, a["ctxT"], a["wq1"], a["wk1"], a["wv1"], a["wo1"])
        if stages >= 4:
            with ExitStack() as ffn:
                fsb, _ = scopes(nc, ffn)
                wgT, wuT, wdT = fsb("wgT", [P, KC, FF]), fsb("wuT", [P, KC, FF]), fsb("wdT", [P, MF, D])
                hqT = fsb("hqT", [P, KC, T])
                quantised_input_l1(nc, psum[:], x_tok, ident, a["wg"], a["wu"], a["wd"], wgT, wuT, wdT, hqT)
                gated_l1(nc, psum[:], x_tok, wgT, wuT, wdT, hqT)
        store_x(nc, x_tok, out)


def layout(inputs):
    n = {k: np.asarray(v) for k, v in inputs.items()}
    c = np.ascontiguousarray
    wo0 = np.zeros((P, NG0, D), np.float32)
    wo0.reshape(G0, SLOT, NG0, D)[:, :DH0] = n["L0_xattn_Wo"].reshape(NG0, G0, DH0, D).transpose(1, 2, 0, 3)
    return {
        "x": c(n["x"]),
        "xmask": c(n["mask_BxS_ik0"].reshape(NT, P).T),
        "kvmask": c(n["mask_BxS2_ik1"].reshape(T)),
        "ctxT": c(n["ctx_1024"].transpose(0, 2, 1)),
        "ln_w": c(n["L0_xattn_ln_w"].reshape(KC, P).T),
        "wq0": c(n["L0_xattn_Wq"]),
        "wk0": c(n["L0_xattn_Wkv"][:, :D]),
        "wv0": c(n["L0_xattn_Wkv"][:, D:]),
        "wo0": wo0,
        "router": c(n["L0_ffn_router_w"].T),
        "w1": c(n["L0_ffn_w1"].transpose(0, 2, 1)),
        "b1": c(n["L0_ffn_b1"].reshape(E0, MH, P).transpose(0, 2, 1)),
        "w2": c(n["L0_ffn_w2"].transpose(0, 2, 1)),
        "b2": c(n["L0_ffn_b2"]),
        "wq1": c(n["L1_xattn_Wq"]),
        "wk1": c(n["L1_xattn_Wk"]),
        "wv1": c(n["L1_xattn_Wv"]),
        "wo1": c(n["L1_xattn_Wo"]),
        "wg": c(n["L1_ffn_w_gate"]),
        "wu": c(n["L1_ffn_w_up"]),
        "wd": c(n["L1_ffn_w_down"]),
    }


def kernel(**inputs):
    import concourse.bacc as bacc
    from concourse.bass_utils import run_bass_kernel_spmd

    arrays = layout(inputs)
    nc = bacc.Bacc("TRN2", target_bir_lowering=False, num_devices=1)
    a = {k: nc.dram_tensor(f"in_{k}", v.shape, mybir.dt.from_np(v.dtype), kind="ExternalInput").ap() for k, v in arrays.items()}
    out = nc.dram_tensor("out_x", (B, S, D), F32, kind="ExternalOutput").ap()
    build(nc, a, out)
    r = run_bass_kernel_spmd(nc, [{f"in_{k}": v for k, v in arrays.items()}], core_ids=[0])
    return r.results[0]["out_x"]
```

```python
from contextlib import ExitStack

import numpy as np

import concourse.bass as bass
from concourse import mybir

ALU = mybir.AluOpType
ACT = mybir.ActivationFunctionType
AX = mybir.AxisListType
F32 = mybir.dt.float32
F32R = mybir.dt.float32r
BF16 = mybir.dt.bfloat16
I32 = mybir.dt.int32
I16 = mybir.dt.int16
U32 = mybir.dt.uint32

P = 128
B, S, D = 4, 512, 256
T = B * S
NT = T // P
TPB = S // P
KC = D // P
LN_EPS = 1e-5
NEG = -1e9

H0, DH0 = 16, 16
G0 = 4
NG0 = H0 // G0
SLOT = P // G0


def round_f32r(v):
    bits = np.array([v], np.float32).view(np.uint32).astype(np.uint64)
    return float(((bits + 0x800) & 0xFFFFF000).astype(np.uint32).view(np.float32)[0])


class Chain:

    def __init__(self, engine, sem):
        self.engine, self.sem, self.base, self.turn, self.per, self.n = engine, sem, 0, None, 0, 0

    def loop(self, turn, per):
        self.turn, self.per, self.n = turn, per, 0

    def end(self, turns):
        assert self.n == self.per, (self.sem, self.n, self.per)
        self.base += turns * self.per
        self.turn, self.n = None, 0

    def add(self, instruction):
        instruction.then_inc(self.sem, 1)
        self.n += 1

    def wait(self):
        at = self.base + self.n
        self.engine.wait_ge(self.sem, at if self.turn is None else self.turn * self.per + at)

    def step(self, instruction):
        self.add(instruction)
        self.wait()

    def close(self):
        self.base += self.n
        self.n = 0


def rsqrt_steps(nc, chain, out, v, tmp):
    chain.step(nc.vector.tensor_scalar(out.bitcast(I32), v.bitcast(I32), -0.5, float(0x5F3759DF), ALU.mult, ALU.add))
    for _ in range(3):
        chain.step(nc.vector.scalar_tensor_tensor(out=tmp, in0=out, scalar=-0.5, in1=out, op0=ALU.mult, op1=ALU.mult))
        chain.step(nc.vector.tensor_tensor(tmp, tmp, v, ALU.mult))
        chain.step(nc.vector.scalar_tensor_tensor(out=out, in0=tmp, scalar=1.5, in1=out, op0=ALU.add, op1=ALU.mult))


RSQRT_STEPS = 10


def layernorm_steps(nc, chain, x_tok, tile0, out, st, twice, last_sem):
    v = nc.vector
    for i in range(TPB):
        chain.add(v.bn_stats(st["stats"][:, i, :], x_tok[:, bass.ds(tile0 + i, 1), :].rearrange("p a d -> p (a d)")))
    chain.wait()
    chain.add(v.memset(st["carrier"][:], 0.0))
    for i in range(TPB):
        chain.add(v.bn_aggr(st["mv"][:, i, :], st["stats"][:, i, :]))
    chain.wait()
    mean, var = st["mv"][:, :, 0], st["mv"][:, :, 1]
    chain.step(v.tensor_scalar(st["ve"][:], var, LN_EPS, None, ALU.add))
    rsqrt_steps(nc, chain, st["r"][:], st["ve"][:], st["tmp"][:])
    if twice:
        chain.step(v.tensor_tensor(st["ve"][:], st["r"][:], st["r"][:], ALU.mult))
        chain.step(v.tensor_tensor(st["ve"][:], st["ve"][:], var, ALU.mult))
        chain.step(v.tensor_scalar(st["ve"][:], st["ve"][:], LN_EPS, None, ALU.add))
        rsqrt_steps(nc, chain, st["r2"][:], st["ve"][:], st["tmp"][:])
        chain.step(v.tensor_tensor(st["r"][:], st["r"][:], st["r2"][:], ALU.mult))
    chain.step(v.scalar_tensor_tensor(out=st["nm"][:], in0=mean, scalar=-1.0, in1=st["r"][:], op0=ALU.mult, op1=ALU.mult))
    for i in range(TPB):
        ins = v.tensor_scalar(out[:, i, :], x_tok[:, bass.ds(tile0 + i, 1), :].rearrange("p a d -> p (a d)"),
                              st["r"][:, i:i + 1], st["nm"][:, i:i + 1], ALU.mult, ALU.add)
        if i == TPB - 1:
            ins.then_inc(last_sem, 1)


def layernorm_links(twice):
    return 2 * TPB + 2 + RSQRT_STEPS + 1 + (4 + RSQRT_STEPS if twice else 0)


def layernorm_buffers(sb, tag):
    return {"stats": sb(f"{tag}_stats", [P, TPB, 6], F32), "mv": sb(f"{tag}_mv", [P, TPB, 2], F32), "carrier": sb(f"{tag}_carrier", [P, 1], F32),
            **{n: sb(f"{tag}_{n}", [P, TPB], F32) for n in ("ve", "r", "r2", "tmp", "nm")}}


def scopes(nc, ctx):
    def sb(name, shape, dt=F32):
        return ctx.enter_context(nc.sbuf_tensor(name, shape, dt))

    def sem(name):
        return ctx.enter_context(nc.semaphore(name))

    return sb, sem


def load_inputs(nc, x_dram, x_tok, ident, xmask_dram, xmask_i, xmask):
    with ExitStack() as ctx:
        sb, sem = scopes(nc, ctx)
        loaded, stored, built = sem("x_loaded"), sem("xmask_ready"), sem("ident_built")
        block = ctx.enter_context(nc.Block())

        @block.sync
        def _(sp):
            sp.dma_start(x_tok[:], x_dram.rearrange("b (t p) d -> p (b t) d", p=P)).then_inc(loaded, 16)
            sp.dma_start(xmask_i[:], xmask_dram).then_inc(loaded, 16)
            sp.wait_ge(loaded, 32)

        @block.gpsimd
        def _(pool):
            pool.memset(ident[:], 0.0).then_inc(built, 1)
            pool.wait_ge(built, 1)
            pool.affine_select(out=ident[:], in_=ident[:], compare_op=ALU.not_equal, fill=1.0, base=0,
                               pattern=[[-1, P]], channel_multiplier=1).then_inc(built, 1)
            pool.wait_ge(built, 2)

        @block.vector
        def _(dve):
            dve.wait_ge(loaded, 32)
            nc.vector.tensor_copy(xmask[:], xmask_i[:]).then_inc(stored, 1)
            dve.wait_ge(stored, 1)


def project_l0(nc, psum, x_tok, ident, ctxT_dram, kvmask_dram, ln_w_dram, wq_dram, wk_dram, wv_dram,
               q_scr, k_scr, kneg_scr, v_scr):
    HI, LO = 0, 1
    MG = P // (G0 * DH0)
    with ExitStack() as ctx:
        sb, sem = scopes(nc, ctx)
        wq, wk, wv = (sb(n, [P, KC, D]) for n in ("wq0", "wk0", "wv0"))
        lnw = sb("lnw", [P, KC])
        ctxT = sb("ctxT", [P, KC, S])
        kv_i = sb("kv_i", [P, T], I32)
        kv = sb("kv", [P, T])
        sc_mul, sc_add = sb("sc_mul", [2, 1]), sb("sc_add", [2, 1])
        kneg = sb("kneg", [2, T], F32R)
        hn = sb("hn", [P, TPB, D])
        hT = sb("hT", [P, KC, S])
        km = sb("km", [P, KC, S])
        parts = {n: sb(n, [P, KC, S], F32R) for n in ("q_hi", "q_lo", "k_hi", "k_lo")}
        vaug = sb("vaug", [P, TPB, H0 * SLOT])
        st = layernorm_buffers(sb, "ln0")
        ps_t, ps_q, ps_k, ps_v = psum[:, 0:2], psum[:, 2:4], psum[:, 4:6], psum[:, 6:8]

        w_in, kv_in, ctx_in = sem("w_in"), sem("kv_in"), sem("ctx_in")
        link = sem("dve_link")
        hn_ready, hT_psum, hT_ready = sem("hn_ready"), sem("hT_psum"), sem("hT_ready")
        q_psum, k_psum, v_psum = sem("q_psum"), sem("k_psum"), sem("v_psum")
        km_ready, kneg_ready, ones_ready = sem("km_ready"), sem("kneg_ready"), sem("ones_ready")
        k_hi_ready, q_hi_ready, k_lo_ready, q_lo_ready = (sem(n) for n in ("k_hi_ready", "q_hi_ready", "k_lo_ready", "q_lo_ready"))
        v_ready = sem("v_ready")
        k_out, v_out, q_out, kneg_out = sem("k_out"), sem("v_out"), sem("q_out"), sem("kneg_out")
        block = ctx.enter_context(nc.Block())

        def rows(scr, part, b):
            return scr[part, bass.ds(b, 1)].rearrange("a (k p) n -> p (a k) n", p=P)

        @block.sync
        def _(sp):
            sp.dma_start(ctxT[:], ctxT_dram[0].rearrange("(k p) n -> p k n", p=P)).then_inc(ctx_in, 16)
            for w, dram in ((wk, wk_dram), (wv, wv_dram), (wq, wq_dram)):
                sp.dma_start(w[:], dram.rearrange("(k p) n -> p k n", p=P)).then_inc(w_in, 16)
            sp.dma_start(lnw[:], ln_w_dram).then_inc(w_in, 16)
            sp.dma_start(kv_i[:], kvmask_dram.partition_broadcast(P)).then_inc(kv_in, 16)

            def turn(b, more):
                if more:
                    sp.wait_ge(v_psum, b + 1)
                    sp.dma_start(ctxT[:], ctxT_dram[bass.ds(b + 1, 1)].rearrange("a (k p) n -> p (a k) n", p=P)).then_inc(ctx_in, 16)
                sp.wait_ge(k_lo_ready, b + 1)
                sp.dma_start(rows(k_scr, HI, b), parts["k_hi"][:].bitcast(F32)).then_inc(k_out, 16)
                sp.dma_start(rows(k_scr, LO, b), parts["k_lo"][:].bitcast(F32)).then_inc(k_out, 16)
                sp.wait_ge(v_ready, 2 * b + 2)
                for g in range(NG0):
                    sp.dma_start(v_scr[bass.ds(b, 1), g].rearrange("a t p n -> p (a t) n"),
                                 vaug[:, :, g * P:(g + 1) * P]).then_inc(v_out, 16)
                sp.wait_ge(q_lo_ready, b + 1)
                sp.dma_start(rows(q_scr, HI, b), parts["q_hi"][:].bitcast(F32)).then_inc(q_out, 16)
                sp.dma_start(rows(q_scr, LO, b), parts["q_lo"][:].bitcast(F32)).then_inc(q_out, 16)

            with sp.Fori(0, B - 1) as b:
                turn(b, True)
            turn(B - 1, False)
            sp.wait_ge(kneg_ready, 1)
            for g in range(NG0):
                sp.dma_start(kneg_scr[:, g].rearrange("b r n -> r b n"),
                             kneg[:].bitcast(F32).rearrange("r (b n) -> r b n", b=B)).then_inc(kneg_out, 16)
            sp.wait_ge(kneg_out, 16 * NG0)
            sp.wait_ge(k_out, 32 * B)
            sp.wait_ge(v_out, 16 * NG0 * B)
            sp.wait_ge(q_out, 32 * B)

        @block.tensor
        def _(pe):
            pe.wait_ge(w_in, 64)
            with pe.Fori(0, B) as b:
                pe.wait_ge(ctx_in, 16 * b + 16)
                for m in range(KC):
                    for k in range(KC):
                        last = nc.tensor.matmul(ps_k[:, m], wk[:, k, m * P:(m + 1) * P], ctxT[:, k], start=k == 0, stop=k == KC - 1)
                last.then_inc(k_psum, 1)
                for t in range(TPB):
                    for k in range(KC):
                        last = nc.tensor.matmul(ps_v[:, t // 2, (t % 2) * D:(t % 2 + 1) * D], ctxT[:, k, t * P:(t + 1) * P],
                                                wv[:, k], start=k == 0, stop=k == KC - 1)
                last.then_inc(v_psum, 1)
                pe.wait_ge(hn_ready, b + 1)
                for k in range(KC):
                    for t in range(TPB):
                        last = nc.tensor.transpose(ps_t[:, k, t * P:(t + 1) * P], hn[:, t, k * P:(k + 1) * P], ident[:])
                last.then_inc(hT_psum, 1)
                pe.wait_ge(hT_ready, KC * b + KC)
                for m in range(KC):
                    for k in range(KC):
                        last = nc.tensor.matmul(ps_q[:, m], wq[:, k, m * P:(m + 1) * P], hT[:, k], start=k == 0, stop=k == KC - 1)
                last.then_inc(q_psum, 1)
                pe.wait_ge(km_ready, b + 1)
                pe.wait_ge(v_ready, 2 * b + 2)
                pe.wait_ge(q_lo_ready, b + 1)

        @block.scalar
        def _(act):
            act.wait_ge(w_in, 64)
            act.wait_ge(ones_ready, 1)
            with act.Fori(0, B) as b:
                act.wait_ge(km_ready, b + 1)
                nc.scalar.activation(parts["k_hi"][:], km[:], ACT.Copy).then_inc(k_hi_ready, 1)
                act.wait_ge(v_psum, b + 1)
                for half in range(2):
                    out = vaug[:, 2 * half:2 * half + 2].rearrange("p t (h e) -> p (t h) e", e=SLOT)[:, :, 0:DH0]
                    nc.scalar.activation(out, ps_v[:, half].rearrange("p (h e) -> p h e", e=DH0), ACT.Copy).then_inc(v_ready, 1)
                act.wait_ge(hT_psum, b + 1)
                for k in range(KC):
                    nc.scalar.activation(hT[:, k], ps_t[:, k], ACT.Copy, scale=lnw[:, k:k + 1]).then_inc(hT_ready, 1)
                act.wait_ge(q_psum, b + 1)
                nc.scalar.activation(parts["q_hi"][:], ps_q, ACT.Copy, scale=DH0 ** -0.5).then_inc(q_hi_ready, 1)
                act.wait_ge(k_out, 32 * b + 32)
                act.wait_ge(v_out, 16 * NG0 * b + 16 * NG0)
                act.wait_ge(q_out, 32 * b + 32)

        @block.vector
        def _(dve):
            v = nc.vector
            chain = Chain(dve, link)
            v.memset(vaug[:], 1.0).then_inc(ones_ready, 1)
            hi = round_f32r(NEG)
            chain.add(v.memset(sc_mul[:], -(NEG - hi)))
            chain.step(v.memset(sc_add[:], NEG - hi))
            chain.add(v.memset(sc_mul[0:1], -hi))
            chain.step(v.memset(sc_add[0:1], hi))
            dve.wait_ge(kv_in, 16)
            chain.step(v.tensor_scalar(kv[:], kv_i[:], 0.0, None, ALU.is_gt))
            v.tensor_scalar(kneg[:], kv[0:2], sc_mul[:, 0:1], sc_add[:, 0:1], ALU.mult, ALU.add).then_inc(kneg_ready, 1)
            chain.close()
            with dve.Fori(0, B) as b:
                chain.loop(b, layernorm_links(True))
                layernorm_steps(nc, chain, x_tok, b * TPB, hn, st, True, hn_ready)
                chain.end(B)
                dve.wait_ge(k_psum, b + 1)
                for m in range(KC):
                    ins = v.tensor_tensor(km[:, m], ps_k[:, m], kv[:, bass.ds(b * S, S)], ALU.mult)
                ins.then_inc(km_ready, 1)
                dve.wait_ge(k_hi_ready, b + 1)
                v.tensor_tensor(parts["k_lo"][:], km[:], parts["k_hi"][:].bitcast(F32), ALU.subtract).then_inc(k_lo_ready, 1)
                dve.wait_ge(q_hi_ready, b + 1)
                v.scalar_tensor_tensor(out=parts["q_lo"][:], in0=ps_q, scalar=DH0 ** -0.5,
                                       in1=parts["q_hi"][:].bitcast(F32), op0=ALU.mult, op1=ALU.subtract).then_inc(q_lo_ready, 1)
                dve.wait_ge(k_out, 32 * b + 32)
                dve.wait_ge(q_out, 32 * b + 32)


def attend_l0(nc, psum, q_scr, k_scr, kneg_scr, v_scr, attnT, w1_dram, w1_all, w1_in, xs_scr):
    NGRP = B * NG0
    AHEAD, NBUF = 2, 4
    R_MASK, R_MAX, R_ALL = 4 * DH0, 4 * DH0 + 2, 4 * DH0 + 4
    LOADS = 2 * 4 + 1 + 1
    MAX_IN = 16 * 2 * 4
    with ExitStack() as ctx:
        sb, sem = scopes(nc, ctx)
        qs = [sb(f"qs{n}", [R_ALL, G0, S], F32R) for n in range(NBUF)]
        ks = [sb(f"ks{n}", [R_ALL, G0, S], F32R) for n in range(NBUF)]
        vs = [sb(f"vs{n}", [P, TPB, G0 * SLOT]) for n in range(NBUF)]
        nmax = sb("nmax", [P, NBUF, G0 * TPB])
        mparts = sb("mparts", [P, 2 * G0 * TPB])
        mpartsT = sb("mpartsT", [P, NBUF, 2 * G0 * TPB], F32)
        mhi = sb("mhi", [P, G0 * TPB], F32R)
        probs = sb("probs", [P, 2, G0, S])
        marks = sb("marks", [P, 2 * 2])
        ZEROS = 3 * D
        zeros = sb("zeros", [P, ZEROS])
        ps_s1, ps_s2, ps_o = psum[:, 0:2], psum[:, 2:6], psum[:, 6:8]

        loaded = [sem(f"grp_loaded{n}") for n in range(NBUF)]
        rows_set, link = sem("rows_set"), sem("a0_link")
        s1_psum, s1_max, maxT_ready = sem("s1_psum"), sem("s1_max"), sem("maxT_ready")
        max_in = [sem(f"max_in{n}") for n in range(NBUF)]
        zeros_ready, zeroed = sem("zeros_ready"), sem("xs_zeroed")
        s2_psum, probs_ready, pv_done, o_read = sem("s2_psum"), sem("probs_ready"), sem("pv_done"), sem("o_read")
        block = ctx.enter_context(nc.Block())

        FREE = 2

        def turns(engine, body):
            with engine.Fori(0, NGRP // NBUF - 1) as t:
                body(t * NBUF, True)
            body(NGRP - NBUF, False)

        @block.sync
        def _(sp):
            def load(i, n):
                for dst, scr, order in ((qs[n], q_scr, (0, 0, 1, 1)), (ks[n], k_scr, (0, 1, 0, 1))):
                    for r, part in enumerate(order):
                        sp.dma_start(dst[r * DH0:(r + 1) * DH0].bitcast(F32),
                                     scr[part].rearrange("b (g j d) n -> d (b g) j n", j=G0, d=DH0)[:, bass.ds(i, 1)]
                                     .rearrange("d a j n -> d (a j) n")).then_inc(loaded[n], 16)
                neg = kneg_scr.rearrange("b g r n -> r (b g) n")[:, bass.ds(i, 1)]
                sp.dma_start(ks[n][R_MASK:R_MASK + 2].bitcast(F32), neg.to_broadcast([2, G0, S])).then_inc(loaded[n], 16)
                sp.dma_start(vs[n][:], v_scr.rearrange("b g t p n -> p (b g) t n")[:, bass.ds(i, 1)]
                             .rearrange("p a t n -> p (a t) n")).then_inc(loaded[n], 16)

            def put_max(i, n):
                sp.wait_ge(maxT_ready, i + 1)
                for part in range(2):
                    dst = qs[n][R_MAX + part:R_MAX + part + 1].bitcast(F32).rearrange("r j (t c q) -> r c (j t) q", c=4, q=32)
                    for c in range(4):
                        sp.dma_start(dst[:, c], mpartsT[32 * c + 16 * part:32 * c + 16 * part + 16, n, :]).then_inc(max_in[n], 16)

            sp.wait_ge(rows_set, 1)
            for i in range(AHEAD + 1):
                load(i, i)
            put_max(0, 0)

            def body(i0, more):
                for n in range(NBUF):
                    i = i0 + n
                    if more or n < NBUF - 1:
                        put_max(i + 1, (n + 1) % NBUF)
                    if more or n + AHEAD + 1 < NBUF:
                        sp.wait_ge(pv_done, i * TPB + FREE)
                        load(i + AHEAD + 1, (n + AHEAD + 1) % NBUF)

            turns(sp, body)

        @block.gpsimd
        def _(pool):
            pool.memset(zeros[:], 0.0).then_inc(zeros_ready, 1)
            pool.wait_ge(zeros_ready, 1)
            rows = NS * P * D // (P * ZEROS)
            pool.wait_ge(pv_done, TPB + FREE)
            pool.dma_start(xs_scr.rearrange("n d -> (n d)").rearrange("(p a z) -> p a z", p=P, z=ZEROS),
                           zeros[:].unsqueeze(1).to_broadcast([P, rows, ZEROS])).then_inc(zeroed, 16)
            with pool.Fori(0, E0) as e:
                pool.wait_ge(pv_done, e * (NGRP // E0 * TPB) + 2 * TPB + FREE)
                pool.dma_start(w1_all[:, bass.ds(e, 1)].rearrange("p a k h -> p (a k) h"),
                               w1_dram[bass.ds(e, 1)].rearrange("a (k p) h -> p (a k) h", p=P)).then_inc(w1_in, 16)
            pool.wait_ge(zeroed, 16)

        @block.tensor
        def _(pe):
            def s1(i, n, s0, s1_, wait_bank):
                for s in range(s0, s1_):
                    j, t = divmod(s, TPB)
                    if wait_bank or s >= 2:
                        pe.wait_ge(s1_max, i * 16 + s - 1)
                    nc.tensor.matmul(ps_s1[:, s % 2], qs[n][0:R_MAX, j, t * P:(t + 1) * P], ks[n][0:R_MAX, j, :],
                                     start=True, stop=True).then_inc(s1_psum, 1)

            def s2(i, n, c, half):
                if c == half == 0:
                    pe.wait_ge(max_in[n], (i - n) * (MAX_IN // NBUF) + MAX_IN)
                for j in (2 * half, 2 * half + 1):
                    ins = nc.tensor.matmul(ps_s2[:, j], ks[n][:, j, c * P:(c + 1) * P], qs[n][:, j, :], start=True, stop=True)
                ins.then_inc(s2_psum, 1)

            for i in range(AHEAD):
                pe.wait_ge(loaded[i], 16 * LOADS)
                s1(i, i, 0, 16, i > 0)
            s2(0, 0, 0, 0)
            s2(0, 0, 0, 1)

            def body(i0, more):
                for n in range(NBUF):
                    i, na = i0 + n, (n + AHEAD) % NBUF
                    ahead = more or n + AHEAD < NBUF
                    if ahead:
                        pe.wait_ge(loaded[na], (i + AHEAD - na) * (16 * LOADS // NBUF) + 16 * LOADS)
                    for c in range(TPB):
                        step = i * TPB + c
                        i2, n2, c2 = (i, n, c + 1) if c + 1 < TPB else (i + 1, (n + 1) % NBUF, 0)
                        for half in range(2):
                            pe.wait_ge(probs_ready, step * 2 + half + 1)
                            if more or n2 or c2:
                                s2(i2, n2, c2, half)
                            if half == 1:
                                if c == 0:
                                    pe.wait_ge(o_read, i - 1 + FREE)
                                for j in range(G0):
                                    ins = nc.tensor.matmul(ps_o[SLOT * j:SLOT * (j + 1), n % 2], vs[n][:, c, SLOT * j:SLOT * (j + 1)],
                                                           probs[:, c % 2, j, :], start=c == 0, stop=c == TPB - 1)
                                ins.then_inc(pv_done, 1)
                            if ahead:
                                s1(i + AHEAD, na, 4 * c + 2 * half, 4 * c + 2 * half + 2, True)

            turns(pe, body)

        @block.scalar
        def _(act):
            def exps(step, c):
                for half in range(2):
                    act.wait_ge(s2_psum, step * 2 + half + 1)
                    if half == 0:
                        act.wait_ge(pv_done, step - 1 + FREE)
                    nc.scalar.activation(probs[:, c % 2, 2 * half:2 * half + 2], ps_s2[:, 2 * half:2 * half + 2],
                                         ACT.Exp).then_inc(probs_ready, 1)

            exps(0, 0)
            exps(1, 1)

            def body(i0, more):
                for n in range(NBUF):
                    i = i0 + n
                    exps(i * TPB + 2, 2)
                    exps(i * TPB + 3, 3)
                    if more or n < NBUF - 1:
                        exps(i * TPB + 4, 0)
                        exps(i * TPB + 5, 1)
                    act.wait_ge(pv_done, (i + 1) * TPB + FREE)
                    nc.scalar.activation(attnT[:, bass.ds(i, 1)].rearrange("p a n -> p (a n)"), ps_o[:, n % 2], ACT.Copy).then_inc(o_read, 1)

            turns(act, body)

        @block.vector
        def _(dve):
            v = nc.vector
            chain = Chain(dve, link)
            for f in range(FREE):
                v.memset(marks[:, 2 * f:2 * f + 1], 0.0).then_inc(pv_done, 1)
                v.memset(marks[:, 2 * f + 1:2 * f + 2], 0.0).then_inc(o_read, 1)
            dve.wait_ge(o_read, FREE)
            for n in range(NBUF):
                v.memset(qs[n][R_MASK:R_ALL].bitcast(F32), 1.0)
                ins = v.memset(ks[n][R_MASK:R_ALL].bitcast(F32), 1.0)
            ins.then_inc(rows_set, 1)

            def maxima(i, n, s0, s1_):
                for s in range(s0, s1_):
                    dve.wait_ge(s1_psum, i * 16 + s + 1)
                    v.tensor_reduce(nmax[:, n, s:s + 1], ps_s1[:, s % 2], AX.X, ALU.max, negate=True).then_inc(s1_max, 1)

            def split_max(i, n):
                dve.wait_ge(s1_max, i * 16 + 16)
                chain.step(v.tensor_copy(mhi[:], nmax[:, n]))
                chain.add(v.tensor_copy(mparts[:, 0:16], mhi[:].bitcast(F32)))
                chain.step(v.tensor_tensor(mparts[:, 16:32], nmax[:, n], mhi[:].bitcast(F32), ALU.subtract))
                v.transpose(mpartsT[:, n], mparts[:]).then_inc(maxT_ready, 1)
                dve.wait_ge(maxT_ready, i + 1)

            for i in range(AHEAD):
                maxima(i, i, 0, 16)
            split_max(0, 0)
            chain.close()

            def body(i0, more):
                for n in range(NBUF):
                    i = i0 + n
                    ahead = more or n + AHEAD < NBUF
                    if more or n < NBUF - 1:
                        split_max(i + 1, (n + 1) % NBUF)
                    if ahead:
                        maxima(i + AHEAD, (n + AHEAD) % NBUF, 0, 16)

            with dve.Fori(0, NGRP // NBUF - 1) as t:
                chain.loop(t, NBUF * 3)
                body(t * NBUF, True)
                chain.end(NGRP // NBUF - 1)
            body(NGRP - NBUF, False)


def finish_l0(nc, psum, x_tok, attnT, sum_scr, rec_scr, wo_dram, xmask):
    NGRP = B * NG0
    with ExitStack() as ctx:
        sb, sem = scopes(nc, ctx)
        wo = sb("wo0", [P, NG0, D])
        sums, inv = sb("sums", [P, NGRP * G0 * S // P]), sb("inv", [P, NGRP * G0 * S // P])
        scale = sb("scale", [P, 2, NG0, S])
        at = sb("at", [P, 2, NG0, S])
        w_in, sums_out, sums_in, inv_ready, inv_out = sem("wo_in"), sem("sums_out"), sem("sums_in"), sem("inv_ready"), sem("inv_out")
        scale_in = [sem(f"scale_in{n}") for n in range(2)]
        at_ready, y_psum, y_read = sem("at_ready"), sem("y_psum"), sem("y_read")
        block = ctx.enter_context(nc.Block())

        @block.sync
        def _(sp):
            sp.dma_start(wo[:], wo_dram).then_inc(w_in, 16)
            for j in range(G0):
                sp.dma_start(sum_scr[:, j].unsqueeze(0), attnT[SLOT * j + DH0:SLOT * j + DH0 + 1]).then_inc(sums_out, 16)
            sp.wait_ge(sums_out, 16 * G0)
            sp.dma_start(sums[:], sum_scr.rearrange("g j (a m) -> (g j a) m", a=P // (NGRP * G0))).then_inc(sums_in, 16)
            sp.wait_ge(inv_ready, 1)
            sp.dma_start(rec_scr.rearrange("g j (a m) -> (g j a) m", a=P // (NGRP * G0)), inv[:]).then_inc(inv_out, 16)
            sp.wait_ge(inv_out, 16)

            def spread(b, n):
                for j in range(G0):
                    src = rec_scr[bass.ds(b * NG0, NG0), j].unsqueeze(0).to_broadcast([SLOT, NG0, S])
                    sp.dma_start(scale[SLOT * j:SLOT * (j + 1), n], src).then_inc(scale_in[n], 16)

            spread(0, 0)
            spread(1, 1)
            with sp.Fori(1, B // 2) as t:
                for n in range(2):
                    sp.wait_ge(at_ready, 2 * t + n - 1)
                    spread(2 * t + n, n)

        @block.gpsimd
        def _(pool):
            with pool.Fori(0, B // 2) as t:
                for n in range(2):
                    pool.wait_ge(scale_in[n], 16 * G0 * t + 16 * G0)
                    nc.gpsimd.tensor_tensor(at[:, n], attnT[:, bass.ds((2 * t + n) * NG0, NG0)], scale[:, n], ALU.mult).then_inc(at_ready, 1)
                for n in range(2):
                    pool.wait_ge(y_psum, (2 * t + n + 1) * TPB)

        @block.tensor
        def _(pe):
            pe.wait_ge(w_in, 16)
            with pe.Fori(0, B // 2) as t:
                for n in range(2):
                    pe.wait_ge(at_ready, 2 * t + n + 1)
                    for i in range(TPB):
                        for g in range(NG0):
                            last = nc.tensor.matmul(psum[:, 4 * n + i, 0:D], at[:, n, g, i * P:(i + 1) * P], wo[:, g], start=g == 0, stop=g == NG0 - 1)
                        last.then_inc(y_psum, 1)
                pe.wait_ge(y_read, (2 * t + 2) * TPB)

        @block.vector
        def _(dve):
            dve.wait_ge(sums_in, 16)
            nc.vector.reciprocal(inv[:], sums[:]).then_inc(inv_ready, 1)
            with dve.Fori(0, B // 2) as t:
                for n in range(2):
                    for i in range(TPB):
                        tile = (2 * t + n) * TPB + i
                        dve.wait_ge(y_psum, tile + 1)
                        x = x_tok[:, bass.ds(tile, 1)].rearrange("p a d -> p (a d)")
                        nc.vector.scalar_tensor_tensor(out=x, in0=psum[:, 4 * n + i, 0:D], scalar=xmask[:, bass.ds(tile, 1)], in1=x,
                                                       op0=ALU.mult, op1=ALU.add).then_inc(y_read, 1)
            dve.wait_ge(y_read, NT)


E0, HID, TOP = 8, 1024, 2
MH = HID // P
NS = (TOP * T + E0 * (P - 1)) // P


def route_l0(nc, psum, x_tok, ident, router_dram, w2_dram, w2_all, w2_in, xs_scr, gate_w, slot, expert):
    with ExitStack() as ctx:
        sb, sem = scopes(nc, ctx)
        wr = sb("wr", [P, KC, E0])
        hn = sb("hn1", [P, NT, D])
        hT = sb("hT1", [P, KC, S])
        st = layernorm_buffers(sb, "ln1")
        logits, probs, top = sb("logits", [P, NT, E0]), sb("rprobs", [P, NT, E0]), sb("top", [P, NT, E0])
        idx, idx_f = sb("idx", [P, NT, E0], U32), sb("idx_f", [P, NT, E0])
        iota_i, iota = sb("iota_i", [P, NS], I32), sb("iota", [P, NS])
        hot = [sb(f"hot{n}", [P, NT, E0]) for n in range(TOP)]
        picked, before_b, ones_b = sb("picked", [P, NT, E0], BF16), sb("before_b", [P, P], BF16), sb("ones_b", [P, P], BF16)
        before = sb("before", [P, P])
        col, col2 = sb("col", [P, NT]), sb("col2", [P, NT])
        tiles_i, tiles, first, end = sb("tiles_i", [P, E0], I32), sb("tiles", [P, E0]), sb("first", [P, E0]), sb("end", [P, E0])
        below = sb("below", [P, E0, E0])
        passed, expert_f = sb("passed", [1, NS, E0]), sb("expert_f", [1, NS])
        ps_t, ps_l, ps_rank, ps_count = psum[:, 0:2], psum[:, 2], psum[:, 3, 0:NT * E0], psum[:, 4, 0:E0]
        w_in, link, hn_ready, hT_psum, hT_ready = sem("r_in"), sem("r_link"), sem("r_hn"), sem("r_hT_psum"), sem("r_hT")
        l_psum, iota_ready, before_ready, e_ready, shifted, picked_ready, rank_psum, slot_ready, scattered = (
            sem(f"r_{n}") for n in ("logits", "iota", "before", "exp", "shifted", "picked", "rank", "slot", "scattered"))
        block = ctx.enter_context(nc.Block())

        @block.sync
        def _(sp):
            sp.dma_start(wr[:], router_dram.rearrange("(k p) e -> p k e", p=P)).then_inc(w_in, 16)
            with sp.Fori(0, E0) as e:
                sp.dma_start(w2_all[:, bass.ds(e, 1)].rearrange("p a m c -> p (a m) c"),
                             w2_dram[bass.ds(e, 1)].rearrange("a (m p) c -> p (a m) c", p=P)).then_inc(w2_in, 16)

        @block.gpsimd
        def _(pool):
            pool.iota(iota_i[:], pattern=[[1, NS]], base=0, channel_multiplier=0).then_inc(iota_ready, 1)
            pool.memset(before[:], 1.0).then_inc(before_ready, 1)
            pool.wait_ge(before_ready, 1)
            pool.affine_select(out=before[:], in_=before[:], compare_op=ALU.is_gt, fill=0.0, base=0,
                               pattern=[[1, P]], channel_multiplier=-1).then_inc(before_ready, 1)
            pool.wait_ge(slot_ready, 1)
            for t in range(NT):
                for n in range(TOP):
                    pool.indirect_dma_start(out=xs_scr, out_offset=bass.IndirectOffsetOnAxis(ap=slot[:, n, t:t + 1], axis=0),
                                            in_=hn[:, t], in_offset=None).then_inc(scattered, 16)
            pool.wait_ge(scattered, 16 * TOP * NT)

        @block.tensor
        def _(pe):
            pe.wait_ge(w_in, 16)
            for b in range(B):
                pe.wait_ge(hn_ready, b + 1)
                for k in range(KC):
                    for t in range(TPB):
                        last = nc.tensor.transpose(ps_t[:, k, t * P:(t + 1) * P], hn[:, b * TPB + t, k * P:(k + 1) * P], ident[:])
                last.then_inc(hT_psum, 1)
                pe.wait_ge(hT_ready, b + 1)
                for t in range(TPB):
                    for k in range(KC):
                        at = (b * TPB + t) * E0
                        last = nc.tensor.matmul(ps_l[:, at:at + E0], hT[:, k, t * P:(t + 1) * P], wr[:, k], start=k == 0, stop=k == KC - 1)
                last.then_inc(l_psum, 1)
            pe.wait_ge(picked_ready, 1)
            nc.tensor.matmul(ps_rank, before_b[:], picked[:].rearrange("p t e -> p (t e)"), start=True, stop=False)
            for t in range(NT - 1):
                nc.tensor.matmul(ps_rank[:, (t + 1) * E0:].rearrange("p (t e) -> p t e", e=E0), ones_b[:],
                                 picked[:, t:t + 1].to_broadcast([P, NT - 1 - t, E0]), start=False, stop=t == NT - 2)
            for t in range(NT):
                last = nc.tensor.matmul(ps_count, ones_b[:], picked[:, t], start=t == 0, stop=t == NT - 1)
            last.then_inc(rank_psum, 1)

        @block.scalar
        def _(act):
            with act.Fori(0, B) as b:
                act.wait_ge(hT_psum, b + 1)
                nc.scalar.activation(hT[:], ps_t, ACT.Copy).then_inc(hT_ready, 1)
                act.wait_ge(l_psum, b + 1)
            act.wait_ge(shifted, 1)
            nc.scalar.activation(probs[:], logits[:], ACT.Exp).then_inc(e_ready, 1)

        @block.vector
        def _(dve):
            v = nc.vector
            chain = Chain(dve, link)
            with dve.Fori(0, B) as b:
                chain.loop(b, layernorm_links(False))
                layernorm_steps(nc, chain, x_tok, b * TPB, hn[:, bass.ds(b * TPB, TPB)], st, False, hn_ready)
                chain.end(B)
            wide = [P, NT, E0]
            dve.wait_ge(iota_ready, 1)
            chain.add(v.memset(ones_b[:], 1.0))
            chain.step(v.tensor_copy(iota[:], iota_i[:]))
            iota_e = iota[:, 0:E0]
            chain.add(v.tensor_tensor(below[:], iota_e.unsqueeze(1).to_broadcast([P, E0, E0]), iota_e.unsqueeze(2).to_broadcast([P, E0, E0]), ALU.is_lt))
            dve.wait_ge(before_ready, 2)
            chain.add(v.tensor_copy(before_b[:], before[:]))
            dve.wait_ge(l_psum, B)
            lg = ps_l[:, 0:NT * E0].rearrange("p (t e) -> p t e", e=E0)
            chain.step(v.tensor_reduce(col[:], lg, AX.X, ALU.max))
            v.tensor_tensor(logits[:], lg, col[:].unsqueeze(2).to_broadcast(wide), ALU.subtract).then_inc(shifted, 1)
            dve.wait_ge(e_ready, 1)
            chain.step(v.tensor_reduce(col[:], probs[:], AX.X, ALU.add))
            chain.step(v.reciprocal(col2[:], col[:]))
            chain.step(v.tensor_tensor(logits[:], probs[:], col2[:].unsqueeze(2).to_broadcast(wide), ALU.mult))
            for t in range(NT):
                chain.add(v.max(top[:, t], logits[:, t]))
            chain.wait()
            for t in range(NT):
                chain.add(v.max_index(idx[:, t], top[:, t], logits[:, t]))
            chain.wait()
            chain.step(v.tensor_copy(idx_f[:], idx[:]))
            iota_w = iota_e.unsqueeze(1).to_broadcast(wide)
            for n in range(TOP):
                chain.add(v.tensor_tensor(hot[n][:], iota_w, idx_f[:, :, n:n + 1].to_broadcast(wide), ALU.is_equal))
            chain.wait()
            v.tensor_tensor(picked[:], hot[0][:], hot[1][:], ALU.add).then_inc(picked_ready, 1)
            chain.step(v.tensor_tensor(col[:], top[:, :, 0], top[:, :, 1], ALU.add))
            chain.step(v.tensor_scalar(col[:], col[:], 1e-8, None, ALU.add))
            chain.step(v.reciprocal(col2[:], col[:]))
            chain.add(v.tensor_tensor(gate_w[:], top[:, :, 0:TOP], col2[:].unsqueeze(2).to_broadcast([P, NT, TOP]), ALU.mult))
            dve.wait_ge(rank_psum, 1)
            chain.step(v.tensor_scalar(tiles_i[:], ps_count, 1.0 / P, (P - 1) / (2.0 * P), ALU.mult, ALU.add))
            chain.step(v.tensor_copy(tiles[:], tiles_i[:]))
            chain.step(v.tensor_tensor(below[:], below[:], tiles[:].unsqueeze(1).to_broadcast([P, E0, E0]), ALU.mult))
            chain.step(v.tensor_reduce(first[:], below[:], AX.X, ALU.add))
            chain.add(v.tensor_tensor(end[:], first[:], tiles[:], ALU.add))
            rank = ps_rank.rearrange("p (t e) -> p t e", e=E0)
            chain.step(v.scalar_tensor_tensor(out=logits[:], in0=first[:].unsqueeze(1).to_broadcast(wide), scalar=float(P), in1=rank, op0=ALU.mult, op1=ALU.add))
            for n in range(TOP):
                chain.add(v.tensor_tensor(hot[n][:], hot[n][:], logits[:], ALU.mult))
            chain.wait()
            chain.add(v.tensor_reduce(col[:], hot[0][:], AX.X, ALU.add))
            chain.step(v.tensor_reduce(col2[:], hot[1][:], AX.X, ALU.add))
            chain.add(v.tensor_copy(slot[:, 0], col[:]))
            chain.add(v.tensor_copy(slot[:, 1], col2[:]))
            chain.wait()
            v.tensor_tensor(passed[:], end[0:1].unsqueeze(1).to_broadcast([1, NS, E0]), iota[0:1].unsqueeze(2).to_broadcast([1, NS, E0]),
                            ALU.is_le).then_inc(slot_ready, 1)
            dve.wait_ge(slot_ready, 1)
            chain.step(v.tensor_reduce(expert_f[:], passed[:], AX.X, ALU.add))
            chain.step(v.tensor_scalar(expert[:], expert_f[:], float(E0 - 1), None, ALU.min))


def experts_l0(nc, psum, ident, xs_scr, ys_scr, expert, w1_all, w1_in, w2_all, w2_in, b1_dram, b2_dram):
    HALF = HID // 2
    with ExitStack() as ctx:
        sb, sem = scopes(nc, ctx)
        b1, b2 = sb("b1", [P, E0, HID]), sb("b2", [P, E0, D])
        xs, xT = sb("xs", [P, D]), sb("xT", [P, KC, P])
        hid, hidT, y = sb("hid", [P, 2, HALF]), sb("hidT", [P, MH, P]), sb("y", [P, D])
        ps_h, ps_T, ps_x, ps_y = psum[:, 0:2], psum[:, 2:4], psum[:, 4, 0:D], psum[:, 5, 0:D]
        b_in, xs_in, x_psum, xT_ready, h_psum, hid_ready, T_psum, T_ready, y_psum, y_ready, y_out = (
            sem(f"e_{n}") for n in ("b_in", "xs_in", "x_psum", "xT", "h_psum", "hid", "T_psum", "hidT", "y_psum", "y", "y_out"))
        block = ctx.enter_context(nc.Block())
        FREE = 1

        def expert_of(engine, j):
            at = expert[0:1, j:j + 1] if isinstance(j, int) else expert[0:1, bass.ds(j, 1)]
            return engine.value_load(at, min_val=0, max_val=E0 - 1)

        def rows(scr, j):
            return scr[j * P:(j + 1) * P] if isinstance(j, int) else scr[bass.ds(j * P, P)]

        @block.sync
        def _(sp):
            sp.dma_start(xs[:], rows(xs_scr, 0)).then_inc(xs_in, 16)
            for e in range(0, E0, 2):
                sp.dma_start(b1[:, e:e + 2], b1_dram[e:e + 2].partition_broadcast(P)).then_inc(b_in, 16)
            sp.dma_start(b2[:], b2_dram.partition_broadcast(P)).then_inc(b_in, 16)
            with sp.Fori(1, NS) as j:
                sp.wait_ge(x_psum, j)
                sp.dma_start(xs[:], rows(xs_scr, j)).then_inc(xs_in, 16)

        @block.gpsimd
        def _(pool):
            with pool.Fori(0, NS) as j:
                pool.wait_ge(y_ready, j + 1 + FREE)
                pool.dma_start(rows(ys_scr, j), y[:]).then_inc(y_out, 16)
            pool.wait_ge(y_out, 16 * NS)

        @block.tensor
        def _(pe):
            def turn_x(j):
                pe.wait_ge(xs_in, 16 * j + 16)
                for k in range(KC):
                    last = nc.tensor.transpose(ps_x[:, k * P:(k + 1) * P], xs[:, k * P:(k + 1) * P], ident[:])
                last.then_inc(x_psum, 1)

            def first_product(j):
                e = expert_of(pe, j)
                pe.wait_ge(xT_ready, j + 1)
                for half in range(2):
                    for k in range(KC):
                        w = w1_all[:, bass.ds(e, 1), k, half * HALF:(half + 1) * HALF].rearrange("p a n -> p (a n)")
                        last = nc.tensor.matmul(ps_h[:, half], xT[:, k], w, start=k == 0, stop=k == KC - 1)
                    last.then_inc(h_psum, 1)

            def turn_hidden(j):
                for half in range(2):
                    pe.wait_ge(hid_ready, 2 * j + half + 1)
                    for i in range(MH // 2):
                        last = nc.tensor.transpose(ps_T[:, half, i * P:(i + 1) * P], hid[:, half, i * P:(i + 1) * P], ident[:])
                    last.then_inc(T_psum, 1)

            def second_product(j):
                e = expert_of(pe, j)
                pe.wait_ge(y_ready, j + FREE)
                for m in range(MH):
                    if m % (MH // 2) == 0:
                        pe.wait_ge(T_ready, 2 * j + 2 * m // MH + 1)
                    w = w2_all[:, bass.ds(e, 1), m].rearrange("p a n -> p (a n)")
                    last = nc.tensor.matmul(ps_y, hidT[:, m], w, start=m == 0, stop=m == MH - 1)
                last.then_inc(y_psum, 1)

            turn_x(0)
            pe.wait_ge(w1_in, 16 * E0)
            first_product(0)
            turn_x(1)
            pe.wait_ge(w2_in, 16 * E0)
            with pe.Fori(0, NS - 2) as j:
                turn_hidden(j)
                first_product(j + 1)
                turn_x(j + 2)
                second_product(j)
            turn_hidden(NS - 2)
            first_product(NS - 1)
            second_product(NS - 2)
            turn_hidden(NS - 1)
            second_product(NS - 1)

        @block.scalar
        def _(act):
            def evacuate_x(j):
                act.wait_ge(x_psum, j + 1)
                nc.scalar.activation(xT[:].rearrange("p k n -> p (k n)"), ps_x, ACT.Copy).then_inc(xT_ready, 1)

            def gelu(j):
                for half in range(2):
                    act.wait_ge(T_psum, 2 * j + half + 1)
                    out = hidT[:, half * (MH // 2):(half + 1) * (MH // 2)].rearrange("p m n -> p (m n)")
                    nc.scalar.activation(out, ps_T[:, half], ACT.Gelu_apprx_tanh).then_inc(T_ready, 1)

            evacuate_x(0)
            evacuate_x(1)
            with act.Fori(0, NS - 2) as j:
                gelu(j)
                evacuate_x(j + 2)
            gelu(NS - 2)
            gelu(NS - 1)

        @block.vector
        def _(dve):
            v = nc.vector

            def add_bias(j):
                e = expert_of(dve, j)
                for half in range(2):
                    dve.wait_ge(h_psum, 2 * j + half + 1)
                    bias = b1[:, bass.ds(e, 1), half * HALF:(half + 1) * HALF].rearrange("p a n -> p (a n)")
                    v.tensor_tensor(hid[:, half], ps_h[:, half], bias, ALU.add).then_inc(hid_ready, 1)

            def read_y(j):
                e = expert_of(dve, j)
                dve.wait_ge(y_psum, j + 1)
                if not (isinstance(j, int) and j == 0):
                    dve.wait_ge(y_out, 16 * j)
                v.tensor_tensor(y[:], ps_y, b2[:, bass.ds(e, 1)].rearrange("p a n -> p (a n)"), ALU.add).then_inc(y_ready, 1)

            v.memset(y[:], 0.0).then_inc(y_ready, FREE)
            dve.wait_ge(y_ready, FREE)
            dve.wait_ge(b_in, 16 * (E0 // 2 + 1))
            add_bias(0)
            add_bias(1)
            read_y(0)
            with dve.Fori(1, NS - 1) as j:
                add_bias(j + 1)
                read_y(j)
            read_y(NS - 1)


def combine_l0(nc, x_tok, ys_scr, gate_w, slot):
    with ExitStack() as ctx:
        sb, sem = scopes(nc, ctx)
        got = sb("got", [P, NT * TOP, D])
        got_in = [sem(f"c_in{b}") for b in range(B)]
        first_done = sem("c_first")
        done = sem("c_done")
        block = ctx.enter_context(nc.Block())

        @block.gpsimd
        def _(pool):
            for t in range(NT):
                for n in range(TOP):
                    pool.indirect_dma_start(out=got[:, t * TOP + n], out_offset=None, in_=ys_scr,
                                            in_offset=bass.IndirectOffsetOnAxis(ap=slot[:, n, t:t + 1], axis=0)).then_inc(got_in[t // TPB], 16)

        @block.vector
        def _(dve):
            v = nc.vector
            for b in range(B):
                dve.wait_ge(got_in[b], 16 * TOP * TPB)
                for n in range(TOP):
                    if n:
                        dve.wait_ge(first_done, (b + 1) * TPB)
                    for t in range(b * TPB, (b + 1) * TPB):
                        v.scalar_tensor_tensor(out=x_tok[:, t], in0=got[:, t * TOP + n], scalar=gate_w[:, t, n:n + 1], in1=x_tok[:, t],
                                               op0=ALU.mult, op1=ALU.add).then_inc((first_done, done)[n], 1)
            dve.wait_ge(done, NT)


H1, DH1 = 16, 64
NP1 = H1 // 2
E1 = H1 * DH1
W3 = 3 * P
MASKED = -1e30


def attend_l1(nc, psum, x_tok, ident, ctxT_dram, wq_dram, wk_dram, wv_dram, wo_dram):
    UNITS = NP1 * TPB
    with ExitStack() as ctx:
        sb, sem = scopes(nc, ctx)
        wq, wk, wv = (sb(n, [P, KC, E1]) for n in ("wq1", "wk1", "wv1"))
        wo = sb("wo1", [P, NP1, D])
        ctxT, hn, hT = sb("ctxT1", [P, KC, S]), sb("hn2", [P, TPB, D]), sb("hT2", [P, KC, S])
        vv = sb("v1", [P, TPB, E1])
        attnT = sb("attnT1", [P, NP1, S])
        xa, xb, ya = (sb(n, [P, 2, 2, S], F32R) for n in ("q_hilo", "q_lohi", "k_hilo"))
        band_f, band, ident_b = sb("band_f", [P, 3, P]), sb("band", [P, 3, P], BF16), sb("ident_b", [P, P], BF16)
        pr = sb("pr", [P, TPB, 2, W3])
        prT = sb("prT", [P, 2, 2, W3])
        nmax, sums, inv = (sb(n, [P, TPB, 2]) for n in ("nmax1", "sums1", "inv1"))
        st = layernorm_buffers(sb, "ln2")
        names = ("w_in", "ctx_in", "band_fill", "band_ready", "link", "hn_ready", "hT_psum", "hT_ready", "v_psum", "v_ready",
                 "q_psum", "q_hi", "q_lo", "k_psum", "k_hi", "k_lo", "s_psum", "max_ready", "exp_ready", "inv_ready",
                 "p_ready", "t_psum", "t_read", "pv_done", "o_read", "y_psum", "y_read")
        s = {n: sem(f"l1_{n}") for n in names}
        xb_in = [sem(f"l1_xb_in{n}") for n in range(2)]
        block = ctx.enter_context(nc.Block())

        def window(qt):
            k0, k1 = max(0, qt - 1), min(TPB - 1, qt + 1)
            return k0, (k1 - k0 + 1) * P

        @block.sync
        def _(sp):
            for w, dram in ((wq, wq_dram), (wk, wk_dram), (wv, wv_dram)):
                sp.dma_start(w[:], dram.rearrange("(k p) n -> p k n", p=P)).then_inc(s["w_in"], 16)
            sp.dma_start(wo[:], wo_dram.rearrange("(m p) n -> p m n", p=P)).then_inc(s["w_in"], 16)

            def load_ctx(b):
                sp.dma_start(ctxT[:], ctxT_dram[bass.ds(b, 1)].rearrange("a (k p) n -> p (a k) n", p=P)).then_inc(s["ctx_in"], 16)

            def turn(b, more):
                for p in range(NP1):
                    n = p % 2
                    sp.wait_ge(s["q_lo"], b * NP1 + p + 1)
                    sp.dma_start(xb[0:DH1, n].bitcast(F32), xa[DH1:P, n].bitcast(F32)).then_inc(xb_in[n], 16)
                    sp.dma_start(xb[DH1:P, n].bitcast(F32), xa[0:DH1, n].bitcast(F32)).then_inc(xb_in[n], 16)
                if more:
                    sp.wait_ge(s["k_lo"], b * NP1 + NP1)
                    load_ctx(b + 1)

            load_ctx(0)
            with sp.Fori(0, B - 1) as b:
                turn(b, True)
            turn(B - 1, False)

        @block.gpsimd
        def _(pool):
            pool.memset(band_f[:], 0.0).then_inc(s["band_fill"], 1)
            pool.wait_ge(s["band_fill"], 1)
            pool.affine_select(out=band_f[:, 0], in_=band_f[:, 0], compare_op=ALU.is_ge, fill=MASKED, base=0, pattern=[[1, P]], channel_multiplier=-1).then_inc(s["band_fill"], 1)
            pool.affine_select(out=band_f[:, 2], in_=band_f[:, 2], compare_op=ALU.is_ge, fill=MASKED, base=0, pattern=[[-1, P]], channel_multiplier=1).then_inc(s["band_fill"], 1)
            with pool.Fori(0, B) as b:
                for u in range(UNITS):
                    qt = u % TPB
                    _, w = window(qt)
                    pool.wait_ge(s["inv_ready"], b * UNITS + u + 1)
                    nc.gpsimd.tensor_tensor(pr[:, qt, :, 0:w], pr[:, qt, :, 0:w], inv[:, qt].unsqueeze(2).to_broadcast([P, 2, w]),
                                            ALU.mult).then_inc(s["p_ready"], 1)

        @block.tensor
        def _(pe):
            mm = nc.tensor.matmul

            def project(b, p, w, src, done, prev, prev_n):
                if prev_n is not None:
                    pe.wait_ge(s[prev], prev_n)
                for k in range(KC):
                    last = mm(psum[:, 7], w[:, k, p * P:(p + 1) * P], src[:, k], start=k == 0, stop=k == KC - 1)
                last.then_inc(s[done], 1)

            def q_of(b, p):
                project(b, p, wq, hT, "q_psum", "k_lo", b * NP1 + p if p else None)

            def k_of(b, p):
                project(b, p, wk, ctxT, "k_psum", "q_lo", b * NP1 + p + 1)

            def scores(b, u):
                p, qt = divmod(u, TPB)
                n, (k0, w) = p % 2, window(qt)
                if qt == 0:
                    pe.wait_ge(s["k_lo"], b * NP1 + p + 1)
                    pe.wait_ge(xb_in[n], b * (NP1 * 16) + (p // 2 + 1) * 32)
                if u >= 2:
                    pe.wait_ge(s["exp_ready"], b * UNITS + u - 1)
                for a in range(2):
                    out = psum[:, 2 * (u % 2) + a, 0:w]
                    mm(out, xa[:, n, a, qt * P:(qt + 1) * P], ya[:, n, a, k0 * P:k0 * P + w], start=True, stop=False)
                    mm(out, xb[:, n, a, qt * P:(qt + 1) * P], ya[:, n, a, k0 * P:k0 * P + w], start=False, stop=False)
                    off = P if qt == 0 else 0
                    last = mm(out, ident_b[:], band[:].rearrange("p c n -> p (c n)")[:, off:off + w], start=False, stop=True)
                last.then_inc(s["s_psum"], 1)

            def turn_probs(b, u):
                qt = u % TPB
                _, w = window(qt)
                pe.wait_ge(s["p_ready"], b * UNITS + u + 1)
                if u:
                    pe.wait_ge(s["t_read"], b * UNITS + u)
                for a in range(2):
                    for c in range(w // P):
                        last = nc.tensor.transpose(psum[:, 4 + a, c * P:(c + 1) * P], pr[:, qt, a, c * P:(c + 1) * P], ident[:])
                last.then_inc(s["t_psum"], 1)

            def product(b, u):
                p, qt = divmod(u, TPB)
                k0, w = window(qt)
                pe.wait_ge(s["t_read"], b * UNITS + u + 1)
                if qt == 0 and p:
                    pe.wait_ge(s["o_read"], b * NP1 + p)
                for c in range(w // P):
                    for a in range(2):
                        last = mm(psum[DH1 * a:DH1 * (a + 1), 6, qt * P:(qt + 1) * P], vv[:, k0 + c, p * P + a * DH1:p * P + (a + 1) * DH1],
                                  prT[:, u % 2, a, c * P:(c + 1) * P], start=c == 0, stop=c == w // P - 1)
                last.then_inc(s["pv_done"], 1)

            pe.wait_ge(s["w_in"], 64)
            pe.wait_ge(s["band_ready"], 1)
            with pe.Fori(0, B) as b:
                pe.wait_ge(s["hn_ready"], b + 1)
                for k in range(KC):
                    for t in range(TPB):
                        last = nc.tensor.transpose(psum[:, k, t * P:(t + 1) * P], hn[:, t, k * P:(k + 1) * P], ident[:])
                last.then_inc(s["hT_psum"], 1)
                pe.wait_ge(s["ctx_in"], b * 16 + 16)
                for i in range(2 * TPB):
                    t, half = divmod(i, 2)
                    if i >= 4:
                        pe.wait_ge(s["v_ready"], b * 8 + i - 3)
                    for k in range(KC):
                        last = mm(psum[:, 2 + i % 4], ctxT[:, k, t * P:(t + 1) * P], wv[:, k, half * S:(half + 1) * S], start=k == 0, stop=k == KC - 1)
                    last.then_inc(s["v_psum"], 1)
                pe.wait_ge(s["hT_ready"], b + 1)
                q_of(b, 0)
                k_of(b, 0)
                q_of(b, 1)
                pe.wait_ge(s["v_ready"], b * 8 + 8)
                scores(b, 0)
                scores(b, 1)
                for u in range(UNITS):
                    p, qt = divmod(u, TPB)
                    if qt == 0 and p + 1 < NP1:
                        k_of(b, p + 1)
                    if u + 2 < UNITS:
                        scores(b, u + 2)
                    if qt == 3 and p + 2 < NP1:
                        q_of(b, p + 2)
                    turn_probs(b, u)
                    if u:
                        product(b, u - 1)
                product(b, UNITS - 1)
                pe.wait_ge(s["o_read"], b * NP1 + NP1)
                for i in range(TPB):
                    for p in range(NP1):
                        last = mm(psum[:, i, 0:D], attnT[:, p, i * P:(i + 1) * P], wo[:, p], start=p == 0, stop=p == NP1 - 1)
                    last.then_inc(s["y_psum"], 1)
                pe.wait_ge(s["y_read"], b * TPB + TPB)

        @block.scalar
        def _(act):
            def hi(b, p, name, dst, scale):
                act.wait_ge(s[name + "_psum"], b * NP1 + p + 1)
                for a in range(2):
                    last = nc.scalar.activation(dst[0:DH1, p % 2, a], psum[DH1 * a:DH1 * (a + 1), 7], ACT.Copy, scale=scale)
                last.then_inc(s[name + "_hi"], 1)

            def exps(b, u):
                qt = u % TPB
                _, w = window(qt)
                act.wait_ge(s["max_ready"], b * UNITS + u + 1)
                if u >= 4:
                    act.wait_ge(s["t_psum"], b * UNITS + u - 3)
                for a in range(2):
                    last = nc.scalar.activation(pr[:, qt, a, 0:w], psum[:, 2 * (u % 2) + a, 0:w], ACT.Exp, bias=nmax[:, qt, a:a + 1],
                                                accum_out=sums[:, qt, a:a + 1])
                last.then_inc(s["exp_ready"], 1)

            with act.Fori(0, B) as b:
                act.wait_ge(s["hT_psum"], b + 1)
                nc.scalar.activation(hT[:], psum[:, 0:2], ACT.Copy).then_inc(s["hT_ready"], 1)
                for i in range(2 * TPB):
                    t, half = divmod(i, 2)
                    act.wait_ge(s["v_psum"], b * 8 + i + 1)
                    nc.scalar.activation(vv[:, t, half * S:(half + 1) * S], psum[:, 2 + i % 4], ACT.Copy).then_inc(s["v_ready"], 1)
                hi(b, 0, "q", xa, DH1 ** -0.5)
                hi(b, 0, "k", ya, 1.0)
                hi(b, 1, "q", xa, DH1 ** -0.5)
                exps(b, 0)
                exps(b, 1)
                for u in range(UNITS):
                    p, qt = divmod(u, TPB)
                    if qt == 0 and p + 1 < NP1:
                        hi(b, p + 1, "k", ya, 1.0)
                    if u + 2 < UNITS:
                        exps(b, u + 2)
                    if qt == 3 and p + 2 < NP1:
                        hi(b, p + 2, "q", xa, DH1 ** -0.5)
                    if qt == 0 and p:
                        act.wait_ge(s["pv_done"], b * UNITS + u)
                        nc.scalar.activation(attnT[:, p - 1], psum[:, 6], ACT.Copy).then_inc(s["o_read"], 1)
                act.wait_ge(s["pv_done"], b * UNITS + UNITS)
                nc.scalar.activation(attnT[:, NP1 - 1], psum[:, 6], ACT.Copy).then_inc(s["o_read"], 1)
                act.wait_ge(s["y_psum"], b * TPB + TPB)

        @block.vector
        def _(dve):
            v = nc.vector
            chain = Chain(dve, s["link"])
            dve.wait_ge(s["band_fill"], 3)
            chain.add(v.tensor_copy(ident_b[:], ident[:]))
            v.tensor_copy(band[:], band_f[:]).then_inc(s["band_ready"], 1)
            chain.close()

            def lo(b, p, name, dst, scale):
                dve.wait_ge(s[name + "_hi"], b * NP1 + p + 1)
                for a in range(2):
                    last = v.scalar_tensor_tensor(out=dst[DH1:P, p % 2, a], in0=psum[DH1 * a:DH1 * (a + 1), 7], scalar=scale,
                                                  in1=dst[0:DH1, p % 2, a].bitcast(F32), op0=ALU.mult, op1=ALU.subtract)
                last.then_inc(s[name + "_lo"], 1)

            def maxima(b, u):
                qt = u % TPB
                _, w = window(qt)
                dve.wait_ge(s["s_psum"], b * UNITS + u + 1)
                v.tensor_reduce(nmax[:, qt], psum[:, 2 * (u % 2):2 * (u % 2) + 2, 0:w], AX.X, ALU.max, negate=True).then_inc(s["max_ready"], 1)

            def invert(b, u):
                qt = u % TPB
                dve.wait_ge(s["exp_ready"], b * UNITS + u + 1)
                v.reciprocal(inv[:, qt], sums[:, qt]).then_inc(s["inv_ready"], 1)

            with dve.Fori(0, B) as b:
                chain.loop(b, layernorm_links(False))
                layernorm_steps(nc, chain, x_tok, b * TPB, hn, st, False, s["hn_ready"])
                chain.end(B)
                lo(b, 0, "q", xa, DH1 ** -0.5)
                lo(b, 0, "k", ya, 1.0)
                lo(b, 1, "q", xa, DH1 ** -0.5)
                maxima(b, 0)
                maxima(b, 1)
                invert(b, 0)
                for u in range(UNITS):
                    p, qt = divmod(u, TPB)
                    _, w = window(qt)
                    if qt == 0 and p + 1 < NP1:
                        lo(b, p + 1, "k", ya, 1.0)
                    if u + 2 < UNITS:
                        maxima(b, u + 2)
                    if qt == 3 and p + 2 < NP1:
                        lo(b, p + 2, "q", xa, DH1 ** -0.5)
                    if u + 1 < UNITS:
                        invert(b, u + 1)
                    dve.wait_ge(s["t_psum"], b * UNITS + u + 1)
                    if u >= 2:
                        dve.wait_ge(s["pv_done"], b * UNITS + u - 1)
                    v.tensor_copy(prT[:, u % 2, :, 0:w], psum[:, 4:6, 0:w]).then_inc(s["t_read"], 1)
                for i in range(TPB):
                    dve.wait_ge(s["y_psum"], b * TPB + i + 1)
                    x = x_tok[:, bass.ds(b * TPB + i, 1)].rearrange("p a d -> p (a d)")
                    v.tensor_tensor(x, x, psum[:, i, 0:D], ALU.add).then_inc(s["y_read"], 1)
                dve.wait_ge(s["y_read"], b * TPB + TPB)


FF = 768
MF = FF // P
BLK = 32
QMAX16, QMAX4 = 32767.0, 7.0
SCALE_MIN = 1e-12


def quantised_input_l1(nc, psum, x_tok, ident, wg_dram, wu_dram, wd_dram, wgT, wuT, wdT, hqT):
    with ExitStack() as ctx:
        sb, sem = scopes(nc, ctx)
        raw = {"g": sb("wg_raw", [P, MF, D]), "u": sb("wu_raw", [P, MF, D]), "d": sb("wd_raw", [P, KC, FF])}
        NBLK = MF * D // BLK
        bs, binv = sb("bs", [P, NBLK]), sb("binv", [P, NBLK])
        w16 = sb("w16", [P, MF * D], I16)
        hn = sb("hn_all", [P, NT, D])
        h16 = sb("h16", [P, NT, D], I16)
        st = layernorm_buffers(sb, "ln3")
        mx, mx1, gmax, scale, inv = sb("f_mx", [P, B]), sb("f_mx1", [P, 1]), sb("f_gmax", [P, 1]), sb("f_scale", [P, 1]), sb("f_inv", [P, 1])
        names = ("w_in", "link", "ln_done", "mx_ready", "gmax_ready", "wq_ready", "wT_psum", "wT_read", "hq_ready", "hT_psum", "hT_read")
        s = {n: sem(f"f1_{n}") for n in names}
        block = ctx.enter_context(nc.Block())

        @block.sync
        def _(sp):
            sp.dma_start(raw["g"][:], wg_dram.rearrange("(m p) c -> p m c", p=P)).then_inc(s["w_in"], 16)
            sp.dma_start(raw["u"][:], wu_dram.rearrange("(m p) c -> p m c", p=P)).then_inc(s["w_in"], 16)
            sp.dma_start(raw["d"][:], wd_dram.rearrange("(m p) c -> p m c", p=P)).then_inc(s["w_in"], 16)

        @block.gpsimd
        def _(pool):
            pool.wait_ge(s["mx_ready"], 1)
            nc.gpsimd.partition_all_reduce(gmax[:], mx1[:], P, bass.bass_isa.ReduceOp.max).then_inc(s["gmax_ready"], 1)

        @block.vector
        def _(dve):
            v = nc.vector
            chain = Chain(dve, s["link"])
            with dve.Fori(0, B) as b:
                chain.loop(b, layernorm_links(False) + 1)
                out = hn[:, bass.ds(b * TPB, TPB)]
                layernorm_steps(nc, chain, x_tok, b * TPB, out, st, False, s["ln_done"])
                dve.wait_ge(s["ln_done"], b + 1)
                chain.step(v.tensor_reduce(mx[:, bass.ds(b, 1)], out.rearrange("p t c -> p (t c)"), AX.X, ALU.max, apply_absolute_value=True))
                chain.end(B)
            v.tensor_reduce(mx1[:], mx[:], AX.X, ALU.max).then_inc(s["mx_ready"], 1)
            dve.wait_ge(s["w_in"], 48)
            for n, name in enumerate(("g", "u", "d")):
                w = raw[name][:].rearrange("p a (n k) -> p (a n) k", k=BLK)
                q = w16[:].rearrange("p (n k) -> p n k", k=BLK)
                wide = [P, NBLK, BLK]
                chain.step(v.tensor_reduce(bs[:], w, AX.X, ALU.max, apply_absolute_value=True))
                chain.step(v.tensor_scalar(bs[:], bs[:], 1.0 / QMAX4, SCALE_MIN, ALU.mult, ALU.max))
                chain.step(v.reciprocal(binv[:], bs[:]))
                chain.step(v.tensor_tensor(q, w, binv[:].unsqueeze(2).to_broadcast(wide), ALU.mult))
                chain.step(v.tensor_scalar(w, q, QMAX4, -QMAX4 - 1.0, ALU.min, ALU.max))
                chain.add(v.tensor_tensor(w, w, bs[:].unsqueeze(2).to_broadcast(wide), ALU.mult))
                chain.wait()
                v.memset(mx[:, n:n + 1], 0.0).then_inc(s["wq_ready"], 1)
            dve.wait_ge(s["gmax_ready"], 1)
            chain.step(v.tensor_scalar(scale[:], gmax[:], 1.0 / QMAX16, SCALE_MIN, ALU.mult, ALU.max))
            chain.step(v.reciprocal(inv[:], scale[:]))
            chain.step(v.tensor_scalar(h16[:], hn[:], inv[:], None, ALU.mult))
            v.tensor_scalar(hn[:], h16[:], scale[:], None, ALU.mult).then_inc(s["hq_ready"], 1)
            dve.wait_ge(s["hq_ready"], 1)

        @block.tensor
        def _(pe):
            def turned(jobs, group0, done, read):
                for g in range(0, len(jobs), 4):
                    i = group0 + g // 4
                    if i >= 8:
                        pe.wait_ge(s[read], i - 7)
                    for n, job in enumerate(jobs[g:g + 4]):
                        last = nc.tensor.transpose(psum[:, i % 8, n * P:(n + 1) * P], job, ident[:])
                    last.then_inc(s[done], 1)

            for n, name in enumerate(("g", "u", "d")):
                pe.wait_ge(s["wq_ready"], n + 1)
                rows, cols = (MF, KC) if name != "d" else (KC, MF)
                jobs = [raw[name][:, m, k * P:(k + 1) * P] for k in range(cols) for m in range(rows)]
                turned(jobs, 3 * n, "wT_psum", "wT_read")
            pe.wait_ge(s["hq_ready"], 1)
            pe.wait_ge(s["wT_read"], 9)
            turned([hn[:, t, k * P:(k + 1) * P] for k in range(KC) for t in range(NT)], 0, "hT_psum", "hT_read")

        @block.scalar
        def _(act):
            for n, dst in enumerate((wgT, wuT, wdT)):
                flat = dst[:].rearrange("p a n -> p (a n)")
                for g in range(3):
                    i = 3 * n + g
                    act.wait_ge(s["wT_psum"], i + 1)
                    nc.scalar.activation(flat[:, g * 512:(g + 1) * 512], psum[:, i % 8], ACT.Copy).then_inc(s["wT_read"], 1)
            flat = hqT[:].rearrange("p k n -> p (k n)")
            for i in range(KC * B):
                act.wait_ge(s["hT_psum"], i + 1)
                nc.scalar.activation(flat[:, i * 512:(i + 1) * 512], psum[:, i % 8], ACT.Copy).then_inc(s["hT_read"], 1)


def gated_l1(nc, psum, x_tok, wgT, wuT, wdT, hqT):
    CH = MF * S
    with ExitStack() as ctx:
        sb, sem = scopes(nc, ctx)
        gate, up = sb("gate", [P, B, CH]), sb("up", [P, B, CH])
        a16, b16 = sb("a16", [P, CH], I16), sb("b16", [P, CH], mybir.dt.uint16)
        sig = sb("sig", [P, CH])
        mx = sb("g_mx", [P, 2, B])
        mx1, gmax, k = sb("g_mx1", [P, 2]), sb("g_gmax", [P, 2]), sb("g_k", [P, 12])
        names = ("psum", "read", "mx", "gmax", "a", "sig", "link", "o", "y_psum", "y_read", "o_used")
        s = {n: sem(f"f2_{n}") for n in names}
        block = ctx.enter_context(nc.Block())
        S_G, I_G, S_U, I_U, C2, S_2, I_2, SO_IN, S_O, I_O, T0, T1 = (k[:, i:i + 1] for i in range(12))

        @block.tensor
        def _(pe):
            with pe.Fori(0, B) as c:
                for m in range(MF):
                    for n, w in enumerate((wgT, wuT)):
                        i = 2 * m + n
                        if i >= 8:
                            pe.wait_ge(s["read"], c * (2 * MF) + i - 7)
                        for kk in range(KC):
                            last = nc.tensor.matmul(psum[:, i % 8], w[:, kk, m * P:(m + 1) * P], hqT[:, kk, bass.ds(c * S, S)], start=kk == 0, stop=kk == KC - 1)
                        last.then_inc(s["psum"], 1)
                pe.wait_ge(s["read"], (c + 1) * (2 * MF))
            for c in range(B):
                pe.wait_ge(s["o"], c + 1)
                for i in range(TPB):
                    t = c * TPB + i
                    if t >= 8:
                        pe.wait_ge(s["y_read"], t - 7)
                    for m in range(MF):
                        last = nc.tensor.matmul(psum[:, t % 8, 0:D], gate[:, c, m * S + i * P:m * S + (i + 1) * P], wdT[:, m], start=m == 0, stop=m == MF - 1)
                    last.then_inc(s["y_psum"], 1)

        @block.scalar
        def _(act):
            with act.Fori(0, B) as c:
                for i in range(2 * MF):
                    m, n = divmod(i, 2)
                    act.wait_ge(s["psum"], c * (2 * MF) + i + 1)
                    dst = (gate, up)[n][:, bass.ds(c, 1), m * S:(m + 1) * S].rearrange("p a n -> p (a n)")
                    nc.scalar.activation(dst, psum[:, i % 8], ACT.Copy).then_inc(s["read"], 1)
            for c in range(B):
                act.wait_ge(s["a"], c + 1)
                nc.scalar.activation(sig[:], a16[:], ACT.Sigmoid, scale=S_G).then_inc(s["sig"], 1)
            for c in range(B):
                act.wait_ge(s["a"], B + c + 1)
                nc.scalar.activation(gate[:, c], a16[:], ACT.Copy, scale=S_O).then_inc(s["o"], 1)

        @block.gpsimd
        def _(pool):
            for n in range(3):
                pool.wait_ge(s["mx"], n + 1)
                nc.gpsimd.partition_all_reduce(gmax[:], mx1[:], P, bass.bass_isa.ReduceOp.max).then_inc(s["gmax"], 1)

        @block.vector
        def _(dve):
            v = nc.vector
            chain = Chain(dve, s["link"])

            def biggest(n):
                v.tensor_reduce(mx1[:], mx[:], AX.X, ALU.max).then_inc(s["mx"], 1)
                dve.wait_ge(s["gmax"], n)

            for c in range(B):
                dve.wait_ge(s["read"], (c + 1) * 2 * MF)
                chain.add(v.tensor_reduce(mx[:, 0, c:c + 1], gate[:, c], AX.X, ALU.max, apply_absolute_value=True))
                chain.add(v.tensor_reduce(mx[:, 1, c:c + 1], up[:, c], AX.X, ALU.max, apply_absolute_value=True))
            chain.wait()
            biggest(1)
            for out, out_i, n in ((S_G, I_G, 0), (S_U, I_U, 1)):
                chain.step(v.tensor_scalar(out, gmax[:, n:n + 1], 1.0 / QMAX16, SCALE_MIN, ALU.mult, ALU.max))
                chain.add(v.reciprocal(out_i, out))
            chain.add(v.tensor_scalar(C2, S_G, 1.0 / 65536.0, None, ALU.mult))
            chain.wait()
            for c in range(B):
                v.tensor_scalar(a16[:], gate[:, c], I_G, None, ALU.mult).then_inc(s["a"], 1)
                dve.wait_ge(s["sig"], c + 1)
                chain.step(v.tensor_scalar(b16[:], sig[:], 65536.0, None, ALU.mult))
                chain.step(v.tensor_tensor(gate[:, c], a16[:], b16[:], ALU.mult))
                chain.step(v.tensor_reduce(mx[:, 0, c:c + 1], gate[:, c], AX.X, ALU.max, apply_absolute_value=True))
            biggest(2)
            chain.step(v.tensor_tensor(T0, gmax[:, 0:1], C2, ALU.mult))
            chain.step(v.tensor_scalar(S_2, T0, 1.0 / QMAX16, SCALE_MIN, ALU.mult, ALU.max))
            chain.step(v.reciprocal(I_2, S_2))
            chain.step(v.tensor_tensor(T0, I_2, C2, ALU.mult))
            for c in range(B):
                chain.add(v.tensor_scalar(a16[:], gate[:, c], T0, None, ALU.mult))
                chain.step(v.tensor_scalar(b16[:].bitcast(I16), up[:, c], I_U, None, ALU.mult))
                chain.step(v.tensor_tensor(gate[:, c], a16[:], b16[:].bitcast(I16), ALU.mult))
                chain.step(v.tensor_reduce(mx[:, 0, c:c + 1], gate[:, c], AX.X, ALU.max, apply_absolute_value=True))
            biggest(3)
            chain.step(v.tensor_tensor(SO_IN, S_2, S_U, ALU.mult))
            chain.step(v.tensor_tensor(T1, gmax[:, 0:1], SO_IN, ALU.mult))
            chain.step(v.tensor_scalar(S_O, T1, 1.0 / QMAX16, SCALE_MIN, ALU.mult, ALU.max))
            chain.step(v.reciprocal(I_O, S_O))
            chain.step(v.tensor_tensor(T1, I_O, SO_IN, ALU.mult))
            for c in range(B):
                if c:
                    dve.wait_ge(s["o"], c)
                v.tensor_scalar(a16[:], gate[:, c], T1, None, ALU.mult).then_inc(s["a"], 1)
            for t in range(NT):
                dve.wait_ge(s["y_psum"], t + 1)
                v.tensor_tensor(x_tok[:, t], x_tok[:, t], psum[:, t % 8, 0:D], ALU.add).then_inc(s["y_read"], 1)
            dve.wait_ge(s["y_read"], NT)


def store_x(nc, x_tok, out_dram):
    with ExitStack() as ctx:
        _, sem = scopes(nc, ctx)
        stored = sem("x_stored")
        block = ctx.enter_context(nc.Block())

        @block.sync
        def _(sp):
            sp.dma_start(out_dram.rearrange("b (t p) d -> p (b t) d", p=P), x_tok[:]).then_inc(stored, 16)
            sp.wait_ge(stored, 16)


def build(nc, a, out, stages=4):
    with ExitStack() as ctx:
        sb, sem = scopes(nc, ctx)
        x_tok = sb("x_tok", [P, NT, D])
        ident = sb("ident", [P, P])
        xmask_i, xmask = sb("xmask_i", [P, NT], I32), sb("xmask", [P, NT])
        psum = ctx.enter_context(nc.psum_tensor("psum", [P, 8, 512], F32))

        def scratch(name, shape, dt=F32):
            return nc.dram_tensor(name, shape, dt, kind="Internal").ap()

        q_scr, k_scr = scratch("q_scr", (2, B, D, S)), scratch("k_scr", (2, B, D, S))
        kneg_scr, v_scr = scratch("kneg_scr", (B, NG0, 2, S)), scratch("v_scr", (B, NG0, TPB, P, P))
        sum_scr, rec_scr = scratch("sum_scr", (B * NG0, G0, S)), scratch("rec_scr", (B * NG0, G0, S))
        load_inputs(nc, a["x"], x_tok, ident, a["xmask"], xmask_i, xmask)
        project_l0(nc, psum[:], x_tok, ident, a["ctxT"], a["kvmask"], a["ln_w"], a["wq0"], a["wk0"], a["wv0"],
                   q_scr, k_scr, kneg_scr, v_scr)
        xs_scr, ys_scr = scratch("xs_scr", (NS * P, D)), scratch("ys_scr", (NS * P, D))
        with ExitStack() as moe:
            msb, msem = scopes(nc, moe)
            w1_in, w2_in = msem("w1_in"), msem("w2_in")
            gate_w, slot, expert = msb("gate_w", [P, NT, TOP]), msb("slot", [P, TOP, NT], U32), msb("expert", [1, NS], I32)
            with nc.sbuf_tensor("w1_all", [P, E0, KC, HID], F32) as w1_all:
                with nc.sbuf_tensor("attnT", [P, B * NG0, S], F32) as attnT:
                    attend_l0(nc, psum[:], q_scr, k_scr, kneg_scr, v_scr, attnT, a["w1"], w1_all, w1_in, xs_scr)
                    finish_l0(nc, psum[:], x_tok, attnT, sum_scr, rec_scr, a["wo0"], xmask)
                if stages >= 2:
                    with nc.sbuf_tensor("w2_all", [P, E0, MH, D], F32) as w2_all:
                        route_l0(nc, psum[:], x_tok, ident, a["router"], a["w2"], w2_all, w2_in, xs_scr, gate_w, slot, expert)
                        experts_l0(nc, psum[:], ident, xs_scr, ys_scr, expert, w1_all, w1_in, w2_all, w2_in, a["b1"], a["b2"])
            if stages >= 2:
                combine_l0(nc, x_tok, ys_scr, gate_w, slot)
        if stages >= 3:
            attend_l1(nc, psum[:], x_tok, ident, a["ctxT"], a["wq1"], a["wk1"], a["wv1"], a["wo1"])
        if stages >= 4:
            with ExitStack() as ffn:
                fsb, _ = scopes(nc, ffn)
                wgT, wuT, wdT = fsb("wgT", [P, KC, FF]), fsb("wuT", [P, KC, FF]), fsb("wdT", [P, MF, D])
                hqT = fsb("hqT", [P, KC, T])
                quantised_input_l1(nc, psum[:], x_tok, ident, a["wg"], a["wu"], a["wd"], wgT, wuT, wdT, hqT)
                gated_l1(nc, psum[:], x_tok, wgT, wuT, wdT, hqT)
        store_x(nc, x_tok, out)


def layout(inputs):
    n = {k: np.asarray(v) for k, v in inputs.items()}
    c = np.ascontiguousarray
    wo0 = np.zeros((P, NG0, D), np.float32)
    wo0.reshape(G0, SLOT, NG0, D)[:, :DH0] = n["L0_xattn_Wo"].reshape(NG0, G0, DH0, D).transpose(1, 2, 0, 3)
    return {
        "x": c(n["x"]),
        "xmask": c(n["mask_BxS_ik0"].reshape(NT, P).T),
        "kvmask": c(n["mask_BxS2_ik1"].reshape(T)),
        "ctxT": c(n["ctx_1024"].transpose(0, 2, 1)),
        "ln_w": c(n["L0_xattn_ln_w"].reshape(KC, P).T),
        "wq0": c(n["L0_xattn_Wq"]),
        "wk0": c(n["L0_xattn_Wkv"][:, :D]),
        "wv0": c(n["L0_xattn_Wkv"][:, D:]),
        "wo0": wo0,
        "router": c(n["L0_ffn_router_w"].T),
        "w1": c(n["L0_ffn_w1"].transpose(0, 2, 1)),
        "b1": c(n["L0_ffn_b1"]),
        "w2": c(n["L0_ffn_w2"].transpose(0, 2, 1)),
        "b2": c(n["L0_ffn_b2"]),
        "wq1": c(n["L1_xattn_Wq"]),
        "wk1": c(n["L1_xattn_Wk"]),
        "wv1": c(n["L1_xattn_Wv"]),
        "wo1": c(n["L1_xattn_Wo"]),
        "wg": c(n["L1_ffn_w_gate"]),
        "wu": c(n["L1_ffn_w_up"]),
        "wd": c(n["L1_ffn_w_down"]),
    }


def kernel(**inputs):
    import concourse.bacc as bacc
    from concourse.bass_utils import run_bass_kernel_spmd

    arrays = layout(inputs)
    nc = bacc.Bacc("TRN2", target_bir_lowering=False, num_devices=1)
    a = {k: nc.dram_tensor(f"in_{k}", v.shape, mybir.dt.from_np(v.dtype), kind="ExternalInput").ap() for k, v in arrays.items()}
    out = nc.dram_tensor("out_x", (B, S, D), F32, kind="ExternalOutput").ap()
    build(nc, a, out)
    r = run_bass_kernel_spmd(nc, [{f"in_{k}": v for k, v in arrays.items()}], core_ids=[0])
    return r.results[0]["out_x"]
```

```python
from contextlib import ExitStack

import numpy as np

import concourse.bass as bass
from concourse import mybir

ALU = mybir.AluOpType
ACT = mybir.ActivationFunctionType
AX = mybir.AxisListType
F32 = mybir.dt.float32
F32R = mybir.dt.float32r
BF16 = mybir.dt.bfloat16
I32 = mybir.dt.int32
I16 = mybir.dt.int16
U32 = mybir.dt.uint32

P = 128
B, S, D = 4, 512, 256
T = B * S
NT = T // P
TPB = S // P
KC = D // P
LN_EPS = 1e-5
NEG = -1e9

H0, DH0 = 16, 16
G0 = 4
NG0 = H0 // G0
SLOT = P // G0


def round_f32r(v):
    bits = np.array([v], np.float32).view(np.uint32).astype(np.uint64)
    return float(((bits + 0x800) & 0xFFFFF000).astype(np.uint32).view(np.float32)[0])


class Chain:

    def __init__(self, engine, sem):
        self.engine, self.sem, self.base, self.turn, self.per, self.n = engine, sem, 0, None, 0, 0

    def loop(self, turn, per):
        self.turn, self.per, self.n = turn, per, 0

    def end(self, turns):
        assert self.n == self.per, (self.sem, self.n, self.per)
        self.base += turns * self.per
        self.turn, self.n = None, 0

    def add(self, instruction):
        instruction.then_inc(self.sem, 1)
        self.n += 1

    def wait(self):
        at = self.base + self.n
        self.engine.wait_ge(self.sem, at if self.turn is None else self.turn * self.per + at)

    def step(self, instruction):
        self.add(instruction)
        self.wait()

    def close(self):
        self.base += self.n
        self.n = 0


def rsqrt_steps(nc, chain, out, v, tmp):
    chain.step(nc.vector.tensor_scalar(out.bitcast(I32), v.bitcast(I32), -0.5, float(0x5F3759DF), ALU.mult, ALU.add))
    for _ in range(3):
        chain.step(nc.vector.scalar_tensor_tensor(out=tmp, in0=out, scalar=-0.5, in1=out, op0=ALU.mult, op1=ALU.mult))
        chain.step(nc.vector.tensor_tensor(tmp, tmp, v, ALU.mult))
        chain.step(nc.vector.scalar_tensor_tensor(out=out, in0=tmp, scalar=1.5, in1=out, op0=ALU.add, op1=ALU.mult))


RSQRT_STEPS = 10


def layernorm_steps(nc, chain, x_tok, tile0, out, st, twice, last_sem, tiles=TPB):
    v = nc.vector
    for i in range(tiles):
        chain.add(v.bn_stats(st["stats"][:, i, :], x_tok[:, bass.ds(tile0 + i, 1), :].rearrange("p a d -> p (a d)")))
    chain.wait()
    chain.add(v.memset(st["carrier"][:], 0.0))
    for i in range(tiles):
        chain.add(v.bn_aggr(st["mv"][:, i, :], st["stats"][:, i, :]))
    chain.wait()
    mean, var = st["mv"][:, :, 0], st["mv"][:, :, 1]
    chain.step(v.tensor_scalar(st["ve"][:], var, LN_EPS, None, ALU.add))
    rsqrt_steps(nc, chain, st["r"][:], st["ve"][:], st["tmp"][:])
    if twice:
        chain.step(v.tensor_tensor(st["ve"][:], st["r"][:], st["r"][:], ALU.mult))
        chain.step(v.tensor_tensor(st["ve"][:], st["ve"][:], var, ALU.mult))
        chain.step(v.tensor_scalar(st["ve"][:], st["ve"][:], LN_EPS, None, ALU.add))
        rsqrt_steps(nc, chain, st["r2"][:], st["ve"][:], st["tmp"][:])
        chain.step(v.tensor_tensor(st["r"][:], st["r"][:], st["r2"][:], ALU.mult))
    chain.step(v.scalar_tensor_tensor(out=st["nm"][:], in0=mean, scalar=-1.0, in1=st["r"][:], op0=ALU.mult, op1=ALU.mult))
    for i in range(tiles):
        ins = v.tensor_scalar(out[:, i, :], x_tok[:, bass.ds(tile0 + i, 1), :].rearrange("p a d -> p (a d)"),
                              st["r"][:, i:i + 1], st["nm"][:, i:i + 1], ALU.mult, ALU.add)
        if i % TPB == TPB - 1:
            ins.then_inc(last_sem, 1)


def layernorm_links(twice):
    return 2 * TPB + 2 + RSQRT_STEPS + 1 + (4 + RSQRT_STEPS if twice else 0)


def layernorm_buffers(sb, tag, tiles=TPB):
    return {"stats": sb(f"{tag}_stats", [P, tiles, 6], F32), "mv": sb(f"{tag}_mv", [P, tiles, 2], F32), "carrier": sb(f"{tag}_carrier", [P, 1], F32),
            **{n: sb(f"{tag}_{n}", [P, tiles], F32) for n in ("ve", "r", "r2", "tmp", "nm")}}


def scopes(nc, ctx):
    def sb(name, shape, dt=F32):
        return ctx.enter_context(nc.sbuf_tensor(name, shape, dt))

    def sem(name):
        return ctx.enter_context(nc.semaphore(name))

    return sb, sem


def load_inputs(nc, x_dram, x_tok, ident, xmask_dram, xmask_i, xmask):
    with ExitStack() as ctx:
        _, sem = scopes(nc, ctx)
        loaded, stored, built = sem("x_loaded"), sem("xmask_ready"), sem("ident_built")
        block = ctx.enter_context(nc.Block())

        @block.sync
        def _(sp):
            sp.dma_start(x_tok[:], x_dram.rearrange("b (t p) d -> p (b t) d", p=P)).then_inc(loaded, 16)
            sp.dma_start(xmask_i[:], xmask_dram).then_inc(loaded, 16)
            sp.wait_ge(loaded, 32)

        @block.gpsimd
        def _(pool):
            pool.memset(ident[:], 0.0).then_inc(built, 1)
            pool.wait_ge(built, 1)
            pool.affine_select(out=ident[:], in_=ident[:], compare_op=ALU.not_equal, fill=1.0, base=0,
                               pattern=[[-1, P]], channel_multiplier=1).then_inc(built, 1)
            pool.wait_ge(built, 2)

        @block.vector
        def _(dve):
            dve.wait_ge(loaded, 32)
            nc.vector.tensor_copy(xmask[:], xmask_i[:]).then_inc(stored, 1)
            dve.wait_ge(stored, 1)


def project_l0(nc, psum, x_tok, ident, ctxT_dram, kvmask_dram, ln_w_dram, wq_dram, wk_dram, wv_dram,
               q_scr, k_scr, kneg_scr, v_scr):
    HI, LO = 0, 1
    with ExitStack() as ctx:
        sb, sem = scopes(nc, ctx)
        wq, wk, wv = (sb(n, [P, KC, D]) for n in ("wq0", "wk0", "wv0"))
        lnw = sb("lnw", [P, KC])
        ctxT = sb("ctxT", [P, KC, S])
        kv_i = sb("kv_i", [P, T], I32)
        kv = sb("kv", [P, T])
        sc_mul, sc_add = sb("sc_mul", [2, 1]), sb("sc_add", [2, 1])
        kneg = sb("kneg", [2, T], F32R)
        hn = sb("hn", [P, NT, D])
        hT = sb("hT", [P, KC, S])
        km = sb("km", [P, KC, S])
        parts = {n: sb(n, [P, KC, S], F32R) for n in ("q_hi", "q_lo", "k_hi", "k_lo")}
        vaug = sb("vaug", [P, TPB, H0 * SLOT])
        st = layernorm_buffers(sb, "ln0", NT)
        ps_t, ps_q, ps_k, ps_v = psum[:, 0:2], psum[:, 2:4], psum[:, 4:6], psum[:, 6:8]

        w_in, kv_in, ctx_in = sem("w_in"), sem("kv_in"), sem("ctx_in")
        link = sem("dve_link")
        hn_ready, hT_psum, hT_ready = sem("hn_ready"), sem("hT_psum"), sem("hT_ready")
        q_psum, k_psum, v_psum = sem("q_psum"), sem("k_psum"), sem("v_psum")
        km_ready, kneg_ready, ones_ready = sem("km_ready"), sem("kneg_ready"), sem("ones_ready")
        k_hi_ready, q_hi_ready, k_lo_ready, q_lo_ready = (sem(n) for n in ("k_hi_ready", "q_hi_ready", "k_lo_ready", "q_lo_ready"))
        v_ready = sem("v_ready")
        k_out, v_out, q_out, kneg_out = sem("k_out"), sem("v_out"), sem("q_out"), sem("kneg_out")
        block = ctx.enter_context(nc.Block())

        def rows(scr, part, b):
            return scr[part, bass.ds(b, 1)].rearrange("a (k p) n -> p (a k) n", p=P)

        @block.sync
        def _(sp):
            sp.dma_start(ctxT[:], ctxT_dram[0].rearrange("(k p) n -> p k n", p=P)).then_inc(ctx_in, 16)
            for w, dram in ((wk, wk_dram), (wv, wv_dram), (wq, wq_dram)):
                sp.dma_start(w[:], dram.rearrange("(k p) n -> p k n", p=P)).then_inc(w_in, 16)
            sp.dma_start(lnw[:], ln_w_dram).then_inc(w_in, 16)
            sp.dma_start(kv_i[:], kvmask_dram.partition_broadcast(P)).then_inc(kv_in, 16)

            def turn(b, more):
                if more:
                    sp.wait_ge(v_psum, b + 1)
                    sp.dma_start(ctxT[:], ctxT_dram[bass.ds(b + 1, 1)].rearrange("a (k p) n -> p (a k) n", p=P)).then_inc(ctx_in, 16)
                sp.wait_ge(k_lo_ready, b + 1)
                sp.dma_start(rows(k_scr, HI, b), parts["k_hi"][:].bitcast(F32)).then_inc(k_out, 16)
                sp.dma_start(rows(k_scr, LO, b), parts["k_lo"][:].bitcast(F32)).then_inc(k_out, 16)
                sp.wait_ge(v_ready, 2 * b + 2)
                for g in range(NG0):
                    sp.dma_start(v_scr[bass.ds(b, 1), g].rearrange("a t p n -> p (a t) n"),
                                 vaug[:, :, g * P:(g + 1) * P]).then_inc(v_out, 16)
                sp.wait_ge(q_lo_ready, b + 1)
                sp.dma_start(rows(q_scr, HI, b), parts["q_hi"][:].bitcast(F32)).then_inc(q_out, 16)
                sp.dma_start(rows(q_scr, LO, b), parts["q_lo"][:].bitcast(F32)).then_inc(q_out, 16)

            with sp.Fori(0, B - 1) as b:
                turn(b, True)
            turn(B - 1, False)
            sp.wait_ge(kneg_ready, 1)
            for g in range(NG0):
                sp.dma_start(kneg_scr[:, g].rearrange("b r n -> r b n"),
                             kneg[:].bitcast(F32).rearrange("r (b n) -> r b n", b=B)).then_inc(kneg_out, 16)
            sp.wait_ge(kneg_out, 16 * NG0)
            sp.wait_ge(k_out, 32 * B)
            sp.wait_ge(v_out, 16 * NG0 * B)
            sp.wait_ge(q_out, 32 * B)

        @block.tensor
        def _(pe):
            pe.wait_ge(w_in, 64)
            for b in range(B):
                pe.wait_ge(ctx_in, 16 * b + 16)
                if b:
                    pe.wait_ge(km_ready, b)
                for m in range(KC):
                    for k in range(KC):
                        last = nc.tensor.matmul(ps_k[:, m], wk[:, k, m * P:(m + 1) * P], ctxT[:, k], start=k == 0, stop=k == KC - 1)
                last.then_inc(k_psum, 1)
                if b:
                    pe.wait_ge(v_ready, 2 * b)
                for t in range(TPB):
                    for k in range(KC):
                        last = nc.tensor.matmul(ps_v[:, t // 2, (t % 2) * D:(t % 2 + 1) * D], ctxT[:, k, t * P:(t + 1) * P],
                                                wv[:, k], start=k == 0, stop=k == KC - 1)
                last.then_inc(v_psum, 1)
                pe.wait_ge(hn_ready, b + 1)
                if b:
                    pe.wait_ge(hT_ready, KC * b)
                for k in range(KC):
                    for t in range(TPB):
                        last = nc.tensor.transpose(ps_t[:, k, t * P:(t + 1) * P], hn[:, b * TPB + t, k * P:(k + 1) * P], ident[:])
                last.then_inc(hT_psum, 1)
                pe.wait_ge(hT_ready, KC * b + KC)
                if b:
                    pe.wait_ge(q_lo_ready, b)
                for m in range(KC):
                    for k in range(KC):
                        last = nc.tensor.matmul(ps_q[:, m], wq[:, k, m * P:(m + 1) * P], hT[:, k], start=k == 0, stop=k == KC - 1)
                last.then_inc(q_psum, 1)

        @block.scalar
        def _(act):
            act.wait_ge(w_in, 64)
            act.wait_ge(ones_ready, 1)

            def turn(b, again):
                act.wait_ge(km_ready, b + 1)
                if again:
                    act.wait_ge(k_out, 32 * b)
                nc.scalar.activation(parts["k_hi"][:], km[:], ACT.Copy).then_inc(k_hi_ready, 1)
                act.wait_ge(v_psum, b + 1)
                if again:
                    act.wait_ge(v_out, 16 * NG0 * b)
                for half in range(2):
                    out = vaug[:, 2 * half:2 * half + 2].rearrange("p t (h e) -> p (t h) e", e=SLOT)[:, :, 0:DH0]
                    nc.scalar.activation(out, ps_v[:, half].rearrange("p (h e) -> p h e", e=DH0), ACT.Copy).then_inc(v_ready, 1)
                act.wait_ge(hT_psum, b + 1)
                for k in range(KC):
                    nc.scalar.activation(hT[:, k], ps_t[:, k], ACT.Copy, scale=lnw[:, k:k + 1]).then_inc(hT_ready, 1)
                act.wait_ge(q_psum, b + 1)
                if again:
                    act.wait_ge(q_out, 32 * b)
                nc.scalar.activation(parts["q_hi"][:], ps_q, ACT.Copy, scale=DH0 ** -0.5).then_inc(q_hi_ready, 1)

            turn(0, False)
            with act.Fori(1, B) as b:
                turn(b, True)

        @block.vector
        def _(dve):
            v = nc.vector
            chain = Chain(dve, link)
            v.memset(vaug[:], 1.0).then_inc(ones_ready, 1)
            layernorm_steps(nc, chain, x_tok, 0, hn, st, True, hn_ready, NT)
            hi = round_f32r(NEG)
            chain.add(v.memset(sc_mul[:], -(NEG - hi)))
            chain.step(v.memset(sc_add[:], NEG - hi))
            chain.add(v.memset(sc_mul[0:1], -hi))
            chain.step(v.memset(sc_add[0:1], hi))
            dve.wait_ge(kv_in, 16)
            chain.step(v.tensor_scalar(kv[:], kv_i[:], 0.0, None, ALU.is_gt))
            v.tensor_scalar(kneg[:], kv[0:2], sc_mul[:, 0:1], sc_add[:, 0:1], ALU.mult, ALU.add).then_inc(kneg_ready, 1)

            def turn(b, again):
                dve.wait_ge(k_psum, b + 1)
                if again:
                    dve.wait_ge(k_lo_ready, b)
                for m in range(KC):
                    cols = kv[:, bass.ds(b * S, S)] if again else kv[:, 0:S]
                    ins = v.tensor_tensor(km[:, m], ps_k[:, m], cols, ALU.mult)
                ins.then_inc(km_ready, 1)
                dve.wait_ge(k_hi_ready, b + 1)
                if again:
                    dve.wait_ge(k_out, 32 * b)
                v.tensor_tensor(parts["k_lo"][:], km[:], parts["k_hi"][:].bitcast(F32), ALU.subtract).then_inc(k_lo_ready, 1)
                dve.wait_ge(q_hi_ready, b + 1)
                if again:
                    dve.wait_ge(q_out, 32 * b)
                v.scalar_tensor_tensor(out=parts["q_lo"][:], in0=ps_q, scalar=DH0 ** -0.5,
                                       in1=parts["q_hi"][:].bitcast(F32), op0=ALU.mult, op1=ALU.subtract).then_inc(q_lo_ready, 1)

            turn(0, False)
            with dve.Fori(1, B) as b:
                turn(b, True)


def attend_l0(nc, psum, q_scr, k_scr, kneg_scr, v_scr, attnT, w1_dram, w1_all, w1_in, xs_scr):
    NGRP = B * NG0
    AHEAD, NBUF = 2, 4
    R_MASK, R_MAX, R_ALL = 4 * DH0, P - 2, P
    LOADS = 2 * 4 + 1 + 1
    MAX_IN = 16 * 2 * 4
    with ExitStack() as ctx:
        sb, sem = scopes(nc, ctx)
        qs = [sb(f"qs{n}", [R_ALL, G0, S], F32R) for n in range(NBUF)]
        ks = [sb(f"ks{n}", [R_ALL, G0, S], F32R) for n in range(NBUF)]
        vs = [sb(f"vs{n}", [P, TPB, G0 * SLOT]) for n in range(NBUF)]
        nmax = sb("nmax", [P, NBUF, G0 * TPB])
        mparts = sb("mparts", [P, 2 * G0 * TPB])
        mpartsT = sb("mpartsT", [P, NBUF, 2 * G0 * TPB], F32)
        mhi = sb("mhi", [P, G0 * TPB], F32R)
        probs = sb("probs", [P, 2, G0, S])
        marks = sb("marks", [P, 2 * 2])
        ZEROS = NS * D // E0
        zeros = sb("zeros", [P, ZEROS])
        ps_s1, ps_s2, ps_o = psum[:, 0:2], psum[:, 2:6], psum[:, 6:8]

        loaded = [sem(f"grp_loaded{n}") for n in range(NBUF)]
        rows_set = [sem(f"rows_set{n}") for n in range(NBUF)]
        pool_set, link = sem("pool_set"), sem("a0_link")
        s1_psum, s1_max, maxT_ready = sem("s1_psum"), sem("s1_max"), sem("maxT_ready")
        max_in = [sem(f"max_in{n}") for n in range(NBUF)]
        zeroed = sem("xs_zeroed")
        s2_psum, probs_ready, pv_done, o_read = sem("s2_psum"), sem("probs_ready"), sem("pv_done"), sem("o_read")
        block = ctx.enter_context(nc.Block())

        FREE = 2

        def turns(engine, body):
            with engine.Fori(0, NGRP // NBUF - 1) as t:
                body(t * NBUF, True)
            body(NGRP - NBUF, False)

        @block.sync
        def _(sp):
            def load(i, n):
                load_rows(i, n)
                load_mask_v(i, n)

            def load_rows(i, n):
                for dst, scr, order in ((qs[n], q_scr, (0, 0, 1, 1)), (ks[n], k_scr, (0, 1, 0, 1))):
                    for r, part in enumerate(order):
                        sp.dma_start(dst[r * DH0:(r + 1) * DH0].bitcast(F32),
                                     scr[part].rearrange("b (g j d) n -> d (b g) j n", j=G0, d=DH0)[:, bass.ds(i, 1)]
                                     .rearrange("d a j n -> d (a j) n")).then_inc(loaded[n], 16)

            def load_mask_v(i, n):
                neg = kneg_scr.rearrange("b g r n -> r (b g) n")[:, bass.ds(i, 1)]
                sp.dma_start(ks[n][R_MASK:R_MASK + 2].bitcast(F32), neg.to_broadcast([2, G0, S])).then_inc(loaded[n], 16)
                sp.dma_start(vs[n][:], v_scr.rearrange("b g t p n -> p (b g) t n")[:, bass.ds(i, 1)]
                             .rearrange("p a t n -> p (a t) n")).then_inc(loaded[n], 16)

            def put_max(i, n):
                sp.wait_ge(maxT_ready, i + 1)
                for part in range(2):
                    dst = qs[n][R_MAX + part:R_MAX + part + 1].bitcast(F32).rearrange("r j (t c q) -> r c (j t) q", c=4, q=32)
                    for c in range(4):
                        sp.dma_start(dst[:, c], mpartsT[32 * c + 16 * part:32 * c + 16 * part + 16, n, :]).then_inc(max_in[n], 16)

            for i in range(AHEAD + 1):
                load_rows(i, i)
            for i in range(AHEAD + 1):
                sp.wait_ge(rows_set[i], 2)
                sp.wait_ge(pool_set, i + 1)
                load_mask_v(i, i)
            sp.wait_ge(rows_set[NBUF - 1], 2)
            sp.wait_ge(pool_set, NBUF)
            put_max(0, 0)


            def body(i0, more):
                for n in range(NBUF):
                    i = i0 + n
                    if more or n < NBUF - 1:
                        put_max(i + 1, (n + 1) % NBUF)
                    if more or n + AHEAD + 1 < NBUF:
                        sp.wait_ge(pv_done, i * TPB + FREE)
                        load(i + AHEAD + 1, (n + AHEAD + 1) % NBUF)

            turns(sp, body)

        @block.gpsimd
        def _(pool):
            for n in range(NBUF):
                pool.memset(ks[n][R_MASK:R_ALL].bitcast(F32), 1.0).then_inc(pool_set, 1)
                pool.wait_ge(pool_set, n + 1)
            for n in range(NBUF // 2, NBUF):
                pool.memset(qs[n][R_MASK:R_ALL].bitcast(F32), 0.0).then_inc(rows_set[n], 1)
                pool.wait_ge(rows_set[n], 1)
                pool.memset(qs[n][R_MASK:R_MASK + 2].bitcast(F32), 1.0).then_inc(rows_set[n], 1)
                pool.wait_ge(rows_set[n], 2)
            pool.memset(zeros[:], 0.0).then_inc(pool_set, 1)
            pool.wait_ge(pool_set, NBUF + 1)
            xs_parts = xs_scr.rearrange("n d -> (n d)").rearrange("(e p z) -> p e z", e=E0, p=P)
            with pool.Fori(0, E0) as e:
                pool.wait_ge(pv_done, e * (NGRP // E0 * TPB) + 2 * TPB + FREE)
                pool.dma_start(w1_all[:, bass.ds(e, 1)].rearrange("p a k h -> p (a k) h"),
                               w1_dram[bass.ds(e, 1)].rearrange("a (k p) h -> p (a k) h", p=P)).then_inc(w1_in, 16)
                pool.dma_start(xs_parts[:, bass.ds(e, 1)].rearrange("p a z -> p (a z)"), zeros[:]).then_inc(zeroed, 16)
            pool.wait_ge(zeroed, 16 * E0)

        @block.tensor
        def _(pe):
            def s1(i, n, s0, s1_, wait_bank):
                for s in range(s0, s1_):
                    j, t = divmod(s, TPB)
                    if wait_bank or s >= 2:
                        pe.wait_ge(s1_max, i * 16 + s - 1)
                    nc.tensor.matmul(ps_s1[:, s % 2], qs[n][0:R_MAX, j, t * P:(t + 1) * P], ks[n][0:R_MAX, j, :],
                                     start=True, stop=True).then_inc(s1_psum, 1)

            def s2(i, n, c, half):
                if c == half == 0:
                    pe.wait_ge(max_in[n], (i - n) * (MAX_IN // NBUF) + MAX_IN)
                for j in (2 * half, 2 * half + 1):
                    ins = nc.tensor.matmul(ps_s2[:, j], ks[n][:, j, c * P:(c + 1) * P], qs[n][:, j, :], start=True, stop=True)
                ins.then_inc(s2_psum, 1)

            for i in range(AHEAD):
                pe.wait_ge(loaded[i], 16 * LOADS)
                s1(i, i, 0, 16, i > 0)
            s2(0, 0, 0, 0)
            s2(0, 0, 0, 1)

            def body(i0, more):
                for n in range(NBUF):
                    i, na = i0 + n, (n + AHEAD) % NBUF
                    ahead = more or n + AHEAD < NBUF
                    if ahead:
                        pe.wait_ge(loaded[na], (i + AHEAD - na) * (16 * LOADS // NBUF) + 16 * LOADS)
                    for c in range(TPB):
                        step = i * TPB + c
                        i2, n2, c2 = (i, n, c + 1) if c + 1 < TPB else (i + 1, (n + 1) % NBUF, 0)
                        for half in range(2):
                            pe.wait_ge(probs_ready, step * 2 + half + 1)
                            if more or n2 or c2:
                                s2(i2, n2, c2, half)
                            if half == 1:
                                if c == 0:
                                    pe.wait_ge(o_read, i - 1 + FREE)
                                for j in range(G0):
                                    ins = nc.tensor.matmul(ps_o[SLOT * j:SLOT * (j + 1), n % 2], vs[n][:, c, SLOT * j:SLOT * (j + 1)],
                                                           probs[:, c % 2, j, :], start=c == 0, stop=c == TPB - 1)
                                ins.then_inc(pv_done, 1)
                            if ahead:
                                s1(i + AHEAD, na, 4 * c + 2 * half, 4 * c + 2 * half + 2, True)

            turns(pe, body)

        @block.scalar
        def _(act):
            def exps(step, c):
                for half in range(2):
                    act.wait_ge(s2_psum, step * 2 + half + 1)
                    if half == 0:
                        act.wait_ge(pv_done, step - 1 + FREE)
                    nc.scalar.activation(probs[:, c % 2, 2 * half:2 * half + 2], ps_s2[:, 2 * half:2 * half + 2],
                                         ACT.Exp).then_inc(probs_ready, 1)

            exps(0, 0)
            exps(1, 1)

            def body(i0, more):
                for n in range(NBUF):
                    i = i0 + n
                    exps(i * TPB + 2, 2)
                    exps(i * TPB + 3, 3)
                    if more or n < NBUF - 1:
                        exps(i * TPB + 4, 0)
                        exps(i * TPB + 5, 1)
                    act.wait_ge(pv_done, (i + 1) * TPB + FREE)
                    nc.scalar.activation(attnT[:, bass.ds(i, 1)].rearrange("p a n -> p (a n)"), ps_o[:, n % 2], ACT.Copy).then_inc(o_read, 1)

            turns(act, body)

        @block.vector
        def _(dve):
            v = nc.vector
            chain = Chain(dve, link)
            for f in range(FREE):
                v.memset(marks[:, 2 * f:2 * f + 1], 0.0).then_inc(pv_done, 1)
                v.memset(marks[:, 2 * f + 1:2 * f + 2], 0.0).then_inc(o_read, 1)
            dve.wait_ge(o_read, FREE)
            for n in range(NBUF // 2):
                v.memset(qs[n][R_MASK:R_ALL].bitcast(F32), 0.0).then_inc(rows_set[n], 1)
            for n in range(NBUF // 2):
                dve.wait_ge(rows_set[n], 1)
                v.memset(qs[n][R_MASK:R_MASK + 2].bitcast(F32), 1.0).then_inc(rows_set[n], 1)

            def maxima(i, n, s0, s1_):
                for s in range(s0, s1_):
                    dve.wait_ge(s1_psum, i * 16 + s + 1)
                    v.tensor_reduce(nmax[:, n, s:s + 1], ps_s1[:, s % 2], AX.X, ALU.max, negate=True).then_inc(s1_max, 1)

            def split_max(i, n):
                dve.wait_ge(s1_max, i * 16 + 16)
                chain.step(v.tensor_copy(mhi[:], nmax[:, n]))
                chain.add(v.tensor_copy(mparts[:, 0:16], mhi[:].bitcast(F32)))
                chain.step(v.tensor_tensor(mparts[:, 16:32], nmax[:, n], mhi[:].bitcast(F32), ALU.subtract))
                v.transpose(mpartsT[:, n], mparts[:]).then_inc(maxT_ready, 1)
                dve.wait_ge(maxT_ready, i + 1)

            maxima(0, 0, 0, 16)
            split_max(0, 0)
            chain.close()
            for i in range(1, AHEAD):
                maxima(i, i, 0, 16)

            def body(i0, more):
                for n in range(NBUF):
                    i = i0 + n
                    ahead = more or n + AHEAD < NBUF
                    if more or n < NBUF - 1:
                        split_max(i + 1, (n + 1) % NBUF)
                    if ahead:
                        maxima(i + AHEAD, (n + AHEAD) % NBUF, 0, 16)

            with dve.Fori(0, NGRP // NBUF - 1) as t:
                chain.loop(t, NBUF * 3)
                body(t * NBUF, True)
                chain.end(NGRP // NBUF - 1)
            body(NGRP - NBUF, False)


def finish_l0(nc, psum, x_tok, attnT, rec_scr, wo_dram, xmask):
    NGRP = B * NG0
    with ExitStack() as ctx:
        sb, sem = scopes(nc, ctx)
        wo = sb("wo0", [P, NG0, D])
        sums, inv = sb("sums", [P, NGRP * G0 * S // P]), sb("inv", [P, NGRP * G0 * S // P])
        scale = sb("scale", [P, NGRP, S])
        w_in, sums_in, inv_ready, inv_out = sem("wo_in"), sem("sums_in"), sem("inv_ready"), sem("inv_out")
        scale_in = [sem(f"scale_in{b}") for b in range(B)]
        at_ready, y_psum, y_read = sem("at_ready"), sem("y_psum"), sem("y_read")
        block = ctx.enter_context(nc.Block())

        @block.sync
        def _(sp):
            for j in range(G0):
                sp.dma_start(sums[P // G0 * j:P // G0 * (j + 1)], attnT[SLOT * j + DH0:SLOT * j + DH0 + 1]).then_inc(sums_in, 16)
            sp.dma_start(wo[:], wo_dram).then_inc(w_in, 16)
            sp.wait_ge(inv_ready, 1)
            sp.dma_start(rec_scr.rearrange("j g (a m) -> (j g a) m", a=P // (NGRP * G0)), inv[:]).then_inc(inv_out, 16)
            sp.wait_ge(inv_out, 16)
            for b in range(B):
                for j in range(G0):
                    src = rec_scr[j, b * NG0:(b + 1) * NG0].unsqueeze(0).to_broadcast([SLOT, NG0, S])
                    sp.dma_start(scale[SLOT * j:SLOT * (j + 1), b * NG0:(b + 1) * NG0], src).then_inc(scale_in[b], 16)

        @block.tensor
        def _(pe):
            pe.wait_ge(w_in, 16)
            for t in range(NT):
                b, i = divmod(t, TPB)
                pe.wait_ge(at_ready, b + 1)
                if t >= 8:
                    pe.wait_ge(y_read, t - 7)
                for g in range(NG0):
                    last = nc.tensor.matmul(psum[:, t % 8, 0:D], attnT[:, b * NG0 + g, i * P:(i + 1) * P], wo[:, g], start=g == 0, stop=g == NG0 - 1)
                last.then_inc(y_psum, 1)

        @block.vector
        def _(dve):
            v = nc.vector
            dve.wait_ge(sums_in, 16 * G0)
            v.reciprocal(inv[:], sums[:]).then_inc(inv_ready, 1)

            def divide(b):
                dve.wait_ge(scale_in[b], 16 * G0)
                part = attnT[:, b * NG0:(b + 1) * NG0]
                v.tensor_tensor(part, part, scale[:, b * NG0:(b + 1) * NG0], ALU.mult).then_inc(at_ready, 1)

            divide(0)
            for b in range(B):
                if b + 1 < B:
                    divide(b + 1)
                for t in range(b * TPB, (b + 1) * TPB):
                    dve.wait_ge(y_psum, t + 1)
                    v.scalar_tensor_tensor(out=x_tok[:, t], in0=psum[:, t % 8, 0:D], scalar=xmask[:, t:t + 1], in1=x_tok[:, t],
                                           op0=ALU.mult, op1=ALU.add).then_inc(y_read, 1)
            dve.wait_ge(y_read, NT)


FF = 768
MF = FF // P
BLK = 32
QMAX16, QMAX4 = 32767.0, 7.0
SCALE_MIN = 1e-12

E0, HID, TOP = 8, 1024, 2
MH = HID // P
NS = (TOP * T + E0 * (P - 1)) // P


def route_l0(nc, psum, x_tok, ident, router_dram, w2_dram, b1_dram, w2_all, b1_all, w2_in, b1_in, xs_scr, gate_w, slot, expert):
    with ExitStack() as ctx:
        sb, sem = scopes(nc, ctx)
        wr = sb("wr", [P, KC, E0])
        hn = sb("hn1", [P, NT, D])
        TPH = 2
        hT = sb("hT1", [P, 2, KC, TPH * P])
        st = layernorm_buffers(sb, "ln1", NT)
        logits, probs, top = sb("logits", [P, NT, E0]), sb("rprobs", [P, NT, E0]), sb("top", [P, NT, E0])
        idx, idx_f = sb("idx", [P, NT, E0], U32), sb("idx_f", [P, NT, E0])
        iota_i, iota = sb("iota_i", [P, NS], I32), sb("iota", [P, NS])
        hot = [sb(f"hot{n}", [P, NT, E0]) for n in range(TOP)]
        picked, before_b, ones_b = sb("picked", [P, NT, E0], BF16), sb("before_b", [P, P], BF16), sb("ones_b", [P, P], BF16)
        before = sb("before", [P, P])
        col, col2 = sb("col", [P, NT]), sb("col2", [P, NT])
        tiles_i, tiles, first, end = sb("tiles_i", [P, E0], I32), sb("tiles", [P, E0]), sb("first", [P, E0]), sb("end", [P, E0])
        below = sb("below", [P, E0, E0])
        passed, expert_f = sb("passed", [1, NS, E0]), sb("expert_f", [1, NS])
        ps_t = [psum[:, n].rearrange("p (k n) -> p k n", k=KC) for n in range(2)]
        ps_l, ps_rank, ps_count = psum[:, 2], psum[:, 3, 0:NT * E0], psum[:, 4, 0:E0]
        w_in, link, hn_ready, hT_psum, hT_ready = sem("r_in"), sem("r_link"), sem("r_hn"), sem("r_hT_psum"), sem("r_hT")
        l_psum, iota_ready, before_ready, e_ready, shifted, picked_ready, rank_psum, slot_ready, scattered = (
            sem(f"r_{n}") for n in ("logits", "iota", "before", "exp", "shifted", "picked", "rank", "slot", "scattered"))
        block = ctx.enter_context(nc.Block())

        @block.sync
        def _(sp):
            sp.dma_start(wr[:], router_dram.rearrange("(k p) e -> p k e", p=P)).then_inc(w_in, 16)
            with sp.Fori(0, E0) as e:
                sp.dma_start(w2_all[:, bass.ds(e, 1)].rearrange("p a m c -> p (a m) c"),
                             w2_dram[bass.ds(e, 1)].rearrange("a (m p) c -> p (a m) c", p=P)).then_inc(w2_in, 16)
            for e in range(0, E0, 2):
                sp.dma_start(b1_all[:, e:e + 2], b1_dram[e:e + 2].partition_broadcast(P)).then_inc(b1_in, 16)

        @block.gpsimd
        def _(pool):
            pool.iota(iota_i[:], pattern=[[1, NS]], base=0, channel_multiplier=0).then_inc(iota_ready, 1)
            pool.memset(before[:], 1.0).then_inc(before_ready, 1)
            pool.wait_ge(before_ready, 1)
            pool.affine_select(out=before[:], in_=before[:], compare_op=ALU.is_gt, fill=0.0, base=0,
                               pattern=[[1, P]], channel_multiplier=-1).then_inc(before_ready, 1)
            pool.wait_ge(slot_ready, 1)
            for t in range(NT):
                for n in range(TOP):
                    pool.indirect_dma_start(out=xs_scr, out_offset=bass.IndirectOffsetOnAxis(ap=slot[:, n, t:t + 1], axis=0),
                                            in_=hn[:, t], in_offset=None).then_inc(scattered, 16)
            pool.wait_ge(scattered, 16 * TOP * NT)

        @block.tensor
        def _(pe):
            def turn(i):
                pe.wait_ge(hn_ready, i * TPH // TPB + 1)
                for k in range(KC):
                    for t in range(TPH):
                        last = nc.tensor.transpose(ps_t[i % 2][:, k, t * P:(t + 1) * P], hn[:, i * TPH + t, k * P:(k + 1) * P], ident[:])
                last.then_inc(hT_psum, 1)

            turn(0)
            pe.wait_ge(w_in, 16)
            for i in range(NT // TPH):
                if i + 1 < NT // TPH:
                    turn(i + 1)
                pe.wait_ge(hT_ready, i + 1)
                for t in range(TPH):
                    for k in range(KC):
                        at = (i * TPH + t) * E0
                        last = nc.tensor.matmul(ps_l[:, at:at + E0], hT[:, i % 2, k, t * P:(t + 1) * P], wr[:, k], start=k == 0, stop=k == KC - 1)
                last.then_inc(l_psum, 1)
            pe.wait_ge(picked_ready, 1)
            nc.tensor.matmul(ps_rank, before_b[:], picked[:].rearrange("p t e -> p (t e)"), start=True, stop=False)
            for t in range(NT - 1):
                nc.tensor.matmul(ps_rank[:, (t + 1) * E0:].rearrange("p (t e) -> p t e", e=E0), ones_b[:],
                                 picked[:, t:t + 1].to_broadcast([P, NT - 1 - t, E0]), start=False, stop=t == NT - 2)
            for t in range(NT):
                last = nc.tensor.matmul(ps_count, ones_b[:], picked[:, t], start=t == 0, stop=t == NT - 1)
            last.then_inc(rank_psum, 1)

        @block.scalar
        def _(act):
            for i in range(NT // TPH):
                act.wait_ge(hT_psum, i + 1)
                if i >= 2:
                    act.wait_ge(l_psum, i - 1)
                nc.scalar.activation(hT[:, i % 2], ps_t[i % 2], ACT.Copy).then_inc(hT_ready, 1)
            act.wait_ge(shifted, 1)
            nc.scalar.activation(probs[:], logits[:], ACT.Exp).then_inc(e_ready, 1)

        @block.vector
        def _(dve):
            v = nc.vector
            chain = Chain(dve, link)
            layernorm_steps(nc, chain, x_tok, 0, hn, st, False, hn_ready, NT)
            wide = [P, NT, E0]
            dve.wait_ge(iota_ready, 1)
            chain.add(v.memset(ones_b[:], 1.0))
            chain.step(v.tensor_copy(iota[:], iota_i[:]))
            iota_e = iota[:, 0:E0]
            chain.add(v.tensor_tensor(below[:], iota_e.unsqueeze(1).to_broadcast([P, E0, E0]), iota_e.unsqueeze(2).to_broadcast([P, E0, E0]), ALU.is_lt))
            dve.wait_ge(before_ready, 2)
            chain.add(v.tensor_copy(before_b[:], before[:]))
            dve.wait_ge(l_psum, NT // TPH)
            lg = ps_l[:, 0:NT * E0].rearrange("p (t e) -> p t e", e=E0)
            chain.step(v.tensor_reduce(col[:], lg, AX.X, ALU.max))
            v.tensor_tensor(logits[:], lg, col[:].unsqueeze(2).to_broadcast(wide), ALU.subtract).then_inc(shifted, 1)
            dve.wait_ge(e_ready, 1)
            chain.step(v.tensor_reduce(col[:], probs[:], AX.X, ALU.add))
            chain.step(v.reciprocal(col2[:], col[:]))
            chain.step(v.tensor_tensor(logits[:], probs[:], col2[:].unsqueeze(2).to_broadcast(wide), ALU.mult))
            for t in range(NT):
                chain.add(v.max(top[:, t], logits[:, t]))
            chain.wait()
            for t in range(NT):
                chain.add(v.max_index(idx[:, t], top[:, t], logits[:, t]))
            chain.wait()
            chain.step(v.tensor_copy(idx_f[:], idx[:]))
            iota_w = iota_e.unsqueeze(1).to_broadcast(wide)
            for n in range(TOP):
                chain.add(v.tensor_tensor(hot[n][:], iota_w, idx_f[:, :, n:n + 1].to_broadcast(wide), ALU.is_equal))
            chain.wait()
            v.tensor_tensor(picked[:], hot[0][:], hot[1][:], ALU.add).then_inc(picked_ready, 1)
            chain.step(v.tensor_tensor(col[:], top[:, :, 0], top[:, :, 1], ALU.add))
            chain.step(v.tensor_scalar(col[:], col[:], 1e-8, None, ALU.add))
            chain.step(v.reciprocal(col2[:], col[:]))
            chain.add(v.tensor_tensor(gate_w[:], top[:, :, 0:TOP], col2[:].unsqueeze(2).to_broadcast([P, NT, TOP]), ALU.mult))
            dve.wait_ge(rank_psum, 1)
            chain.step(v.tensor_scalar(tiles_i[:], ps_count, 1.0 / P, (P - 1) / (2.0 * P), ALU.mult, ALU.add))
            chain.step(v.tensor_copy(tiles[:], tiles_i[:]))
            chain.step(v.tensor_tensor(below[:], below[:], tiles[:].unsqueeze(1).to_broadcast([P, E0, E0]), ALU.mult))
            chain.step(v.tensor_reduce(first[:], below[:], AX.X, ALU.add))
            chain.add(v.tensor_tensor(end[:], first[:], tiles[:], ALU.add))
            rank = ps_rank.rearrange("p (t e) -> p t e", e=E0)
            chain.step(v.scalar_tensor_tensor(out=logits[:], in0=first[:].unsqueeze(1).to_broadcast(wide), scalar=float(P), in1=rank, op0=ALU.mult, op1=ALU.add))
            for n in range(TOP):
                chain.add(v.tensor_tensor(hot[n][:], hot[n][:], logits[:], ALU.mult))
            chain.wait()
            chain.add(v.tensor_reduce(col[:], hot[0][:], AX.X, ALU.add))
            chain.step(v.tensor_reduce(col2[:], hot[1][:], AX.X, ALU.add))
            chain.add(v.tensor_copy(slot[:, 0], col[:]))
            chain.add(v.tensor_copy(slot[:, 1], col2[:]))
            chain.wait()
            v.tensor_tensor(passed[:], end[0:1].unsqueeze(1).to_broadcast([1, NS, E0]), iota[0:1].unsqueeze(2).to_broadcast([1, NS, E0]),
                            ALU.is_le).then_inc(slot_ready, 1)
            dve.wait_ge(slot_ready, 1)
            chain.step(v.tensor_reduce(expert_f[:], passed[:], AX.X, ALU.add))
            chain.step(v.tensor_scalar(expert[:], expert_f[:], float(E0 - 1), None, ALU.min))


def experts_l0(nc, psum, ident, xs_scr, ys_scr, expert, w1_all, w1_in, w2_all, w2_in, b1_all, b1_in, b2_dram):
    HALF = HID // 2
    with ExitStack() as ctx:
        sb, sem = scopes(nc, ctx)
        b2 = sb("b2", [P, E0, D])
        xs, xT = sb("xs", [P, D]), sb("xT", [P, KC, P])
        hid, hidT, y = sb("hid", [P, 2, HALF]), sb("hidT", [P, MH, P]), sb("y", [P, D])
        ps_h, ps_T, ps_x, ps_y = psum[:, 0:2], psum[:, 2:4], psum[:, 4, 0:D], psum[:, 5, 0:D]
        b_in, xs_in, x_psum, xT_ready, h_psum, hid_ready, T_psum, T_ready, y_psum, y_ready, y_out = (
            sem(f"e_{n}") for n in ("b_in", "xs_in", "x_psum", "xT", "h_psum", "hid", "T_psum", "hidT", "y_psum", "y", "y_out"))
        block = ctx.enter_context(nc.Block())
        FREE = 1

        def expert_of(engine, j):
            at = expert[0:1, j:j + 1] if isinstance(j, int) else expert[0:1, bass.ds(j, 1)]
            return engine.value_load(at, min_val=0, max_val=E0 - 1)

        def rows(scr, j):
            return scr[j * P:(j + 1) * P] if isinstance(j, int) else scr[bass.ds(j * P, P)]

        @block.sync
        def _(sp):
            sp.dma_start(xs[:], rows(xs_scr, 0)).then_inc(xs_in, 16)
            sp.dma_start(b2[:], b2_dram.partition_broadcast(P)).then_inc(b_in, 16)
            with sp.Fori(1, NS) as j:
                sp.wait_ge(x_psum, j)
                sp.dma_start(xs[:], rows(xs_scr, j)).then_inc(xs_in, 16)

        @block.gpsimd
        def _(pool):
            with pool.Fori(0, NS) as j:
                pool.wait_ge(y_ready, j + 1 + FREE)
                pool.dma_start(rows(ys_scr, j), y[:]).then_inc(y_out, 16)
            pool.wait_ge(y_out, 16 * NS)

        @block.tensor
        def _(pe):
            def turn_x(j):
                pe.wait_ge(xs_in, 16 * j + 16)
                for k in range(KC):
                    last = nc.tensor.transpose(ps_x[:, k * P:(k + 1) * P], xs[:, k * P:(k + 1) * P], ident[:])
                last.then_inc(x_psum, 1)

            def first_product(j):
                e = expert_of(pe, j)
                pe.wait_ge(xT_ready, j + 1)
                for half in range(2):
                    for k in range(KC):
                        w = w1_all[:, bass.ds(e, 1), k, half * HALF:(half + 1) * HALF].rearrange("p a n -> p (a n)")
                        last = nc.tensor.matmul(ps_h[:, half], xT[:, k], w, start=k == 0, stop=k == KC - 1)
                    last.then_inc(h_psum, 1)

            def turn_hidden(j):
                for half in range(2):
                    pe.wait_ge(hid_ready, 2 * j + half + 1)
                    for i in range(MH // 2):
                        last = nc.tensor.transpose(ps_T[:, half, i * P:(i + 1) * P], hid[:, half, i * P:(i + 1) * P], ident[:])
                    last.then_inc(T_psum, 1)

            def second_product(j):
                e = expert_of(pe, j)
                pe.wait_ge(y_ready, j + FREE)
                for m in range(MH):
                    if m % (MH // 2) == 0:
                        pe.wait_ge(T_ready, 2 * j + 2 * m // MH + 1)
                    w = w2_all[:, bass.ds(e, 1), m].rearrange("p a n -> p (a n)")
                    last = nc.tensor.matmul(ps_y, hidT[:, m], w, start=m == 0, stop=m == MH - 1)
                last.then_inc(y_psum, 1)

            turn_x(0)
            pe.wait_ge(w1_in, 16 * E0)
            first_product(0)
            turn_x(1)
            pe.wait_ge(w2_in, 16 * E0)
            with pe.Fori(0, NS - 2) as j:
                turn_hidden(j)
                first_product(j + 1)
                turn_x(j + 2)
                second_product(j)
            turn_hidden(NS - 2)
            first_product(NS - 1)
            second_product(NS - 2)
            turn_hidden(NS - 1)
            second_product(NS - 1)

        @block.scalar
        def _(act):
            def gelu(j):
                for half in range(2):
                    act.wait_ge(T_psum, 2 * j + half + 1)
                    out = hidT[:, half * (MH // 2):(half + 1) * (MH // 2)].rearrange("p m n -> p (m n)")
                    nc.scalar.activation(out, ps_T[:, half], ACT.Gelu_apprx_tanh).then_inc(T_ready, 1)

            with act.Fori(0, NS) as j:
                gelu(j)

        @block.vector
        def _(dve):
            v = nc.vector

            def evacuate_x(j):
                dve.wait_ge(x_psum, j + 1)
                v.tensor_copy(xT[:].rearrange("p k n -> p (k n)"), ps_x).then_inc(xT_ready, 1)

            def add_bias(j):
                e = expert_of(dve, j)
                for half in range(2):
                    dve.wait_ge(h_psum, 2 * j + half + 1)
                    bias = b1_all[:, bass.ds(e, 1), half * HALF:(half + 1) * HALF].rearrange("p a n -> p (a n)")
                    v.tensor_tensor(hid[:, half], ps_h[:, half], bias, ALU.add).then_inc(hid_ready, 1)

            def read_y(j):
                e = expert_of(dve, j)
                dve.wait_ge(y_psum, j + 1)
                if not (isinstance(j, int) and j == 0):
                    dve.wait_ge(y_out, 16 * j)
                v.tensor_tensor(y[:], ps_y, b2[:, bass.ds(e, 1)].rearrange("p a n -> p (a n)"), ALU.add).then_inc(y_ready, 1)

            v.memset(y[:], 0.0).then_inc(y_ready, FREE)
            dve.wait_ge(y_ready, FREE)
            evacuate_x(0)
            dve.wait_ge(b1_in, 16 * (E0 // 2))
            add_bias(0)
            evacuate_x(1)
            add_bias(1)
            evacuate_x(2)
            dve.wait_ge(b_in, 16)
            read_y(0)
            with dve.Fori(1, NS - 2) as j:
                add_bias(j + 1)
                evacuate_x(j + 2)
                read_y(j)
            add_bias(NS - 1)
            read_y(NS - 2)
            read_y(NS - 1)


def combine_l0(nc, psum, x_tok, ident, ys_scr, gate_w, slot, wg_dram, wu_dram, wd_dram, wgT, wuT, wdT, qkv_drams, qkv_hi, qkv_lo, wo_dram, wo):
    with ExitStack() as ctx:
        sb, sem = scopes(nc, ctx)
        got = sb("got", [P, NT * TOP, D])
        got_in = [sem(f"c_in{b}") for b in range(B)]
        first_done = sem("c_first")
        done = sem("c_done")
        raw = {"g": sb("wg_raw", [P, MF, D]), "u": sb("wu_raw", [P, MF, D]), "d": sb("wd_raw", [P, KC, FF])}
        NBLK = MF * D // BLK
        bs, binv = sb("bs", [P, NBLK]), sb("binv", [P, NBLK])
        w16 = sb("w16", [P, MF * D], I16)
        mark = sb("c_mark", [P, 1])
        qkv_raw = [sb(f"w{n}1_raw", [P, KC, E1]) for n in "qkv"]
        w_in, link, wq_ready, wT_psum, wT_read, qkv_in, hi_ready, lo_ready = (
            sem(f"c_{n}") for n in ("w_in", "link", "wq", "wT_psum", "wT_read", "qkv_in", "hi", "lo"))
        block = ctx.enter_context(nc.Block())

        @block.sync
        def _(sp):
            for name, dram in (("g", wg_dram), ("u", wu_dram), ("d", wd_dram)):
                sp.dma_start(raw[name][:], dram.rearrange("(m p) c -> p m c", p=P)).then_inc(w_in, 16)
            sp.wait_ge(w_in, 48)
            for w, dram in zip(qkv_raw, qkv_drams):
                sp.dma_start(w[:], dram.rearrange("(k p) n -> p k n", p=P)).then_inc(qkv_in, 16)
            sp.dma_start(wo[:], wo_dram.rearrange("(m p) n -> p m n", p=P)).then_inc(qkv_in, 16)
            sp.wait_ge(qkv_in, 16 * 4)

        @block.gpsimd
        def _(pool):
            pool.wait_ge(w_in, 48)
            for t in range(NT):
                for n in range(TOP):
                    pool.indirect_dma_start(out=got[:, t * TOP + n], out_offset=None, in_=ys_scr,
                                            in_offset=bass.IndirectOffsetOnAxis(ap=slot[:, n, t:t + 1], axis=0)).then_inc(got_in[t // TPB], 16)
            for n in range(3):
                pool.wait_ge(hi_ready, n + 1)
                nc.gpsimd.tensor_tensor(qkv_lo[n][:], qkv_raw[n][:], qkv_hi[n][:].bitcast(F32), ALU.subtract).then_inc(lo_ready, 1)
            pool.wait_ge(lo_ready, 3)

        @block.vector
        def _(dve):
            v = nc.vector
            chain = Chain(dve, link)

            def add_outputs(b):
                dve.wait_ge(got_in[b], 16 * TOP * TPB)
                for n in range(TOP):
                    if n:
                        dve.wait_ge(first_done, (b + 1) * TPB)
                    for t in range(b * TPB, (b + 1) * TPB):
                        v.scalar_tensor_tensor(out=x_tok[:, t], in0=got[:, t * TOP + n], scalar=gate_w[:, t, n:n + 1], in1=x_tok[:, t],
                                               op0=ALU.mult, op1=ALU.add).then_inc((first_done, done)[n], 1)

            dve.wait_ge(w_in, 48)
            for n, name in enumerate(("g", "u", "d")):
                w = raw[name][:].rearrange("p a (n k) -> p (a n) k", k=BLK)
                q = w16[:].rearrange("p (n k) -> p n k", k=BLK)
                wide = [P, NBLK, BLK]
                chain.step(v.tensor_reduce(bs[:], w, AX.X, ALU.max, apply_absolute_value=True))
                chain.step(v.tensor_scalar(bs[:], bs[:], 1.0 / QMAX4, SCALE_MIN, ALU.mult, ALU.max))
                chain.step(v.reciprocal(binv[:], bs[:]))
                chain.step(v.tensor_tensor(q, w, binv[:].unsqueeze(2).to_broadcast(wide), ALU.mult))
                chain.step(v.tensor_scalar(w, q, QMAX4, -QMAX4 - 1.0, ALU.min, ALU.max))
                chain.add(v.tensor_tensor(w, w, bs[:].unsqueeze(2).to_broadcast(wide), ALU.mult))
                chain.wait()
                v.memset(mark[:], 0.0).then_inc(wq_ready, 1)
                if n:
                    add_outputs(n - 1)
                dve.wait_ge(wq_ready, n + 1)
                if n < 2:
                    high, low = (w[:].rearrange("p a n -> p (a n)") for w in (wgT, wuT)[n])
                    dve.wait_ge(wT_read, 3 * n + 3)
                    for g in range(3):
                        part = slice(g * 512, (g + 1) * 512)
                        chain.add(v.tensor_tensor(low[:, part], psum[:, 3 * n + g], high[:, part].bitcast(F32), ALU.subtract))
            add_outputs(B - 2)
            add_outputs(B - 1)
            dve.wait_ge(done, NT)

        @block.tensor
        def _(pe):
            for n, name in enumerate(("g", "u", "d")):
                pe.wait_ge(wq_ready, n + 1)
                rows, cols = (MF, KC) if name != "d" else (KC, MF)
                blocks = [(k, m) for k in range(cols) for m in range(rows)]
                for g in range(3):
                    i = 3 * n + g
                    if i >= 8:
                        pe.wait_ge(wT_read, i - 7)
                    for c, (k, m) in enumerate(blocks[4 * g:4 * g + 4]):
                        last = nc.tensor.transpose(psum[:, i % 8, c * P:(c + 1) * P], raw[name][:, m, k * P:(k + 1) * P], ident[:])
                    last.then_inc(wT_psum, 1)

        @block.scalar
        def _(act):
            for n, dst in enumerate((wgT[0], wuT[0], wdT)):
                flat = dst[:].rearrange("p a n -> p (a n)")
                for g in range(3):
                    i = 3 * n + g
                    act.wait_ge(wT_psum, i + 1)
                    nc.scalar.activation(flat[:, g * 512:(g + 1) * 512], psum[:, i % 8], ACT.Copy).then_inc(wT_read, 1)
                if n == 0:
                    act.wait_ge(qkv_in, 16 * 4)
                nc.scalar.activation(qkv_hi[n][:], qkv_raw[n][:], ACT.Copy).then_inc(hi_ready, 1)


H1, DH1 = 16, 64
NP1 = H1 // 2
E1 = H1 * DH1
W3 = 3 * P
MASKED = -1e30


def attend_l1(nc, psum, x_tok, ident, ctxT_dram, qkv_hi, qkv_lo, wo):
    UNITS = NP1 * TPB
    Y_BANKS = (0, 1, 6, 7)
    V_BEFORE = 6
    with ExitStack() as ctx:
        sb, sem = scopes(nc, ctx)
        wq, wk, wv = zip(qkv_hi, qkv_lo)
        ctx_raw, ctx_hi, ctx_lo = sb("ctx_raw", [P, KC, S]), sb("ctx_hi", [P, KC, S], F32R), sb("ctx_lo", [P, KC, S], F32R)
        hn, hT_hi, hT_lo = sb("hn2", [P, TPB, D]), sb("hT_hi", [P, KC, S], F32R), sb("hT_lo", [P, KC, S], F32R)
        vv = sb("v1", [P, TPB, E1])
        attnT = sb("attnT1", [P, NP1, S])
        xa, xb, ya = (sb(n, [P, 2, 2, S], F32R) for n in ("q_hilo", "q_lohi", "k_hilo"))
        band_f, band, ident_b = sb("band_f", [P, 3, P]), sb("band", [P, 3, P], BF16), sb("ident_b", [P, P], BF16)
        pr = sb("pr", [P, TPB, 2, W3])
        prT = sb("prT", [P, 2, 2, W3])
        nmax, sums, inv = (sb(n, [P, TPB, 2]) for n in ("nmax1", "sums1", "inv1"))
        st = layernorm_buffers(sb, "ln2")
        names = ("ctx_in", "ctx_hi", "ctx_lo", "hT_hi", "band_fill", "band_ready", "link", "hn_ready", "hT_psum", "hT_ready", "v_psum", "v_ready",
                 "q_psum", "q_hi", "q_lo", "k_psum", "k_hi", "k_lo", "s_psum", "max_ready", "exp_ready", "inv_ready",
                 "p_ready", "t_psum", "t_read", "pv_done", "o_read", "y_psum", "y_read")
        s = {n: sem(f"l1_{n}") for n in names}
        xb_in = [sem(f"l1_xb_in{n}") for n in range(2)]
        block = ctx.enter_context(nc.Block())

        def bank(p, name):
            return 6 if (p, name) == (0, "k") else 7

        def window(qt):
            k0, k1 = max(0, qt - 1), min(TPB - 1, qt + 1)
            return k0, (k1 - k0 + 1) * P

        @block.sync
        def _(sp):
            def load_ctx(b):
                sp.dma_start(ctx_raw[:], ctxT_dram[bass.ds(b, 1)].rearrange("a (k p) n -> p (a k) n", p=P)).then_inc(s["ctx_in"], 16)

            def turn(b, more):
                for p in range(NP1):
                    n = p % 2
                    sp.wait_ge(s["q_lo"], b * NP1 + p + 1)
                    sp.dma_start(xb[0:DH1, n].bitcast(F32), xa[DH1:P, n].bitcast(F32)).then_inc(xb_in[n], 16)
                    sp.dma_start(xb[DH1:P, n].bitcast(F32), xa[0:DH1, n].bitcast(F32)).then_inc(xb_in[n], 16)
                if more:
                    sp.wait_ge(s["ctx_lo"], b + 1)
                    load_ctx(b + 1)

            load_ctx(0)
            with sp.Fori(0, B - 1) as b:
                turn(b, True)
            turn(B - 1, False)

        @block.gpsimd
        def _(pool):
            pool.memset(band_f[:], 0.0).then_inc(s["band_fill"], 1)
            pool.wait_ge(s["band_fill"], 1)
            pool.affine_select(out=band_f[:, 0], in_=band_f[:, 0], compare_op=ALU.is_ge, fill=MASKED, base=0, pattern=[[1, P]], channel_multiplier=-1).then_inc(s["band_fill"], 1)
            pool.affine_select(out=band_f[:, 2], in_=band_f[:, 2], compare_op=ALU.is_ge, fill=MASKED, base=0, pattern=[[-1, P]], channel_multiplier=1).then_inc(s["band_fill"], 1)
            with pool.Fori(0, B) as b:
                pool.wait_ge(s["ctx_hi"], b + 1)
                nc.gpsimd.tensor_tensor(ctx_lo[:], ctx_raw[:], ctx_hi[:].bitcast(F32), ALU.subtract).then_inc(s["ctx_lo"], 1)
                for u in range(UNITS):
                    qt = u % TPB
                    _, w = window(qt)
                    pool.wait_ge(s["inv_ready"], b * UNITS + u + 1)
                    nc.gpsimd.tensor_tensor(pr[:, qt, :, 0:w], pr[:, qt, :, 0:w], inv[:, qt].unsqueeze(2).to_broadcast([P, 2, w]),
                                            ALU.mult).then_inc(s["p_ready"], 1)

        @block.tensor
        def _(pe):
            mm = nc.tensor.matmul

            def split_product(out, lhs, rhs, lhs_cols, rhs_cols):
                passes = [(k, i, j) for k in range(KC) for i, j in ((0, 0), (0, 1), (1, 0))]
                for n, (k, i, j) in enumerate(passes):
                    last = mm(out, lhs[i][:, k, lhs_cols[0]:lhs_cols[1]], rhs[j][:, k, rhs_cols[0]:rhs_cols[1]],
                              start=n == 0, stop=n == len(passes) - 1)
                return last

            def project(b, p, w, src, done, prev, prev_n):
                if prev_n is not None:
                    pe.wait_ge(s[prev], prev_n)
                split_product(psum[:, bank(p, done[0])], w, src, (p * P, (p + 1) * P), (0, S)).then_inc(s[done], 1)

            def q_of(b, p):
                prev, n = ("q_lo" if p == 1 else "k_lo"), b * NP1 + p
                project(b, p, wq, (hT_hi, hT_lo), "q_psum", prev, n if p else None)

            def k_of(b, p):
                project(b, p, wk, (ctx_hi, ctx_lo), "k_psum", "q_lo", b * NP1 + p + 1 if p else None)

            def v_of(b, i):
                t, half = divmod(i, 2)
                if i >= 4:
                    pe.wait_ge(s["v_ready"], b * 8 + i - 3)
                split_product(psum[:, 2 + i % 4], (ctx_hi, ctx_lo), wv, (t * P, (t + 1) * P), (half * S, (half + 1) * S)).then_inc(s["v_psum"], 1)

            def scores(b, u):
                p, qt = divmod(u, TPB)
                n, (k0, w) = p % 2, window(qt)
                if qt == 0:
                    pe.wait_ge(s["k_lo"], b * NP1 + p + 1)
                    pe.wait_ge(xb_in[n], b * (NP1 * 16) + (p // 2 + 1) * 32)
                if u >= 2:
                    pe.wait_ge(s["exp_ready"], b * UNITS + u - 1)
                for a in range(2):
                    out = psum[:, 2 * (u % 2) + a, 0:w]
                    mm(out, xa[:, n, a, qt * P:(qt + 1) * P], ya[:, n, a, k0 * P:k0 * P + w], start=True, stop=False)
                    mm(out, xb[:, n, a, qt * P:(qt + 1) * P], ya[:, n, a, k0 * P:k0 * P + w], start=False, stop=False)
                    off = P if qt == 0 else 0
                    last = mm(out, ident_b[:], band[:].rearrange("p c n -> p (c n)")[:, off:off + w], start=False, stop=True)
                last.then_inc(s["s_psum"], 1)

            def turn_probs(b, u):
                qt = u % TPB
                _, w = window(qt)
                pe.wait_ge(s["p_ready"], b * UNITS + u + 1)
                if u:
                    pe.wait_ge(s["t_read"], b * UNITS + u)
                for a in range(2):
                    for c in range(w // P):
                        last = nc.tensor.transpose(psum[:, 4 + a, c * P:(c + 1) * P], pr[:, qt, a, c * P:(c + 1) * P], ident[:])
                last.then_inc(s["t_psum"], 1)

            def product(b, u):
                p, qt = divmod(u, TPB)
                k0, w = window(qt)
                pe.wait_ge(s["t_read"], b * UNITS + u + 1)
                if qt == 0 and p:
                    pe.wait_ge(s["o_read"], b * NP1 + p)
                for c in range(w // P):
                    for a in range(2):
                        last = mm(psum[DH1 * a:DH1 * (a + 1), 6, qt * P:(qt + 1) * P], vv[:, k0 + c, p * P + a * DH1:p * P + (a + 1) * DH1],
                                  prT[:, u % 2, a, c * P:(c + 1) * P], start=c == 0, stop=c == w // P - 1)
                last.then_inc(s["pv_done"], 1)

            pe.wait_ge(s["band_ready"], 1)
            with pe.Fori(0, B) as b:
                pe.wait_ge(s["ctx_lo"], b + 1)
                for i in range(V_BEFORE):
                    v_of(b, i)
                pe.wait_ge(s["hn_ready"], b + 1)
                for k in range(KC):
                    for t in range(TPB):
                        last = nc.tensor.transpose(psum[:, k, t * P:(t + 1) * P], hn[:, t, k * P:(k + 1) * P], ident[:])
                last.then_inc(s["hT_psum"], 1)
                k_of(b, 0)
                pe.wait_ge(s["hT_ready"], b + 1)
                q_of(b, 0)
                v_of(b, V_BEFORE)
                q_of(b, 1)
                for i in range(V_BEFORE + 1, 2 * TPB):
                    v_of(b, i)
                pe.wait_ge(s["v_ready"], b * 8 + 8)
                scores(b, 0)
                scores(b, 1)
                for u in range(UNITS):
                    p, qt = divmod(u, TPB)
                    if qt == 0 and p + 1 < NP1:
                        k_of(b, p + 1)
                    if u + 2 < UNITS:
                        scores(b, u + 2)
                    if qt == 2 and p + 2 < NP1:
                        q_of(b, p + 2)
                    if u >= 1:
                        turn_probs(b, u - 1)
                    if u >= 2:
                        product(b, u - 2)
                turn_probs(b, UNITS - 1)
                product(b, UNITS - 2)
                product(b, UNITS - 1)
                pe.wait_ge(s["o_read"], b * NP1 + NP1)
                for i in range(TPB):
                    for p in range(NP1):
                        last = mm(psum[:, Y_BANKS[i], 0:D], attnT[:, p, i * P:(i + 1) * P], wo[:, p], start=p == 0, stop=p == NP1 - 1)
                    last.then_inc(s["y_psum"], 1)

        @block.scalar
        def _(act):
            def hi(b, p, name, dst, scale):
                act.wait_ge(s[name + "_psum"], b * NP1 + p + 1)
                for a in range(2):
                    last = nc.scalar.activation(dst[0:DH1, p % 2, a], psum[DH1 * a:DH1 * (a + 1), bank(p, name)], ACT.Copy, scale=scale)
                last.then_inc(s[name + "_hi"], 1)

            def exps(b, u):
                qt = u % TPB
                _, w = window(qt)
                act.wait_ge(s["max_ready"], b * UNITS + u + 1)
                if u >= 4:
                    act.wait_ge(s["t_psum"], b * UNITS + u - 3)
                for a in range(2):
                    last = nc.scalar.activation(pr[:, qt, a, 0:w], psum[:, 2 * (u % 2) + a, 0:w], ACT.Exp, bias=nmax[:, qt, a:a + 1],
                                                accum_out=sums[:, qt, a:a + 1])
                last.then_inc(s["exp_ready"], 1)

            def keep_v(b, i):
                t, half = divmod(i, 2)
                act.wait_ge(s["v_psum"], b * 8 + i + 1)
                nc.scalar.activation(vv[:, t, half * S:(half + 1) * S], psum[:, 2 + i % 4], ACT.Copy).then_inc(s["v_ready"], 1)

            with act.Fori(0, B) as b:
                act.wait_ge(s["ctx_in"], b * 16 + 16)
                nc.scalar.activation(ctx_hi[:], ctx_raw[:], ACT.Copy).then_inc(s["ctx_hi"], 1)
                for i in range(V_BEFORE):
                    keep_v(b, i)
                act.wait_ge(s["hT_psum"], b + 1)
                nc.scalar.activation(hT_hi[:], psum[:, 0:2], ACT.Copy).then_inc(s["hT_hi"], 1)
                hi(b, 0, "k", ya, 1.0)
                hi(b, 0, "q", xa, DH1 ** -0.5)
                keep_v(b, V_BEFORE)
                hi(b, 1, "q", xa, DH1 ** -0.5)
                for i in range(V_BEFORE + 1, 2 * TPB):
                    keep_v(b, i)
                exps(b, 0)
                exps(b, 1)
                for u in range(UNITS):
                    p, qt = divmod(u, TPB)
                    if u + 2 < UNITS:
                        exps(b, u + 2)
                    if qt == 0 and p + 1 < NP1:
                        hi(b, p + 1, "k", ya, 1.0)
                    if qt == 2 and p + 2 < NP1:
                        hi(b, p + 2, "q", xa, DH1 ** -0.5)
                    if qt == 1 and p:
                        act.wait_ge(s["pv_done"], b * UNITS + u - 1)
                        nc.scalar.activation(attnT[:, p - 1], psum[:, 6], ACT.Copy).then_inc(s["o_read"], 1)
                act.wait_ge(s["pv_done"], b * UNITS + UNITS)
                nc.scalar.activation(attnT[:, NP1 - 1], psum[:, 6], ACT.Copy).then_inc(s["o_read"], 1)

        @block.vector
        def _(dve):
            v = nc.vector
            chain = Chain(dve, s["link"])
            dve.wait_ge(s["band_fill"], 3)
            chain.add(v.tensor_copy(ident_b[:], ident[:]))
            v.tensor_copy(band[:], band_f[:]).then_inc(s["band_ready"], 1)
            chain.close()

            def lo(b, p, name, dst, scale):
                dve.wait_ge(s[name + "_hi"], b * NP1 + p + 1)
                for a in range(2):
                    last = v.scalar_tensor_tensor(out=dst[DH1:P, p % 2, a], in0=psum[DH1 * a:DH1 * (a + 1), bank(p, name)], scalar=scale,
                                                  in1=dst[0:DH1, p % 2, a].bitcast(F32), op0=ALU.mult, op1=ALU.subtract)
                last.then_inc(s[name + "_lo"], 1)

            def maxima(b, u):
                qt = u % TPB
                _, w = window(qt)
                dve.wait_ge(s["s_psum"], b * UNITS + u + 1)
                v.tensor_reduce(nmax[:, qt], psum[:, 2 * (u % 2):2 * (u % 2) + 2, 0:w], AX.X, ALU.max, negate=True).then_inc(s["max_ready"], 1)

            def invert(b, u):
                qt = u % TPB
                dve.wait_ge(s["exp_ready"], b * UNITS + u + 1)
                v.reciprocal(inv[:, qt], sums[:, qt]).then_inc(s["inv_ready"], 1)

            with dve.Fori(0, B) as b:
                chain.loop(b, layernorm_links(False))
                layernorm_steps(nc, chain, x_tok, b * TPB, hn, st, False, s["hn_ready"])
                chain.end(B)
                dve.wait_ge(s["hT_hi"], b + 1)
                v.tensor_tensor(hT_lo[:], psum[:, 0:2], hT_hi[:].bitcast(F32), ALU.subtract).then_inc(s["hT_ready"], 1)
                lo(b, 0, "k", ya, 1.0)
                lo(b, 0, "q", xa, DH1 ** -0.5)
                lo(b, 1, "q", xa, DH1 ** -0.5)
                maxima(b, 0)
                maxima(b, 1)
                invert(b, 0)

                def keep_turned(u):
                    _, w = window(u % TPB)
                    dve.wait_ge(s["t_psum"], b * UNITS + u + 1)
                    if u >= 2:
                        dve.wait_ge(s["pv_done"], b * UNITS + u - 1)
                    v.tensor_copy(prT[:, u % 2, :, 0:w], psum[:, 4:6, 0:w]).then_inc(s["t_read"], 1)

                for u in range(UNITS):
                    p, qt = divmod(u, TPB)
                    if u + 2 < UNITS:
                        maxima(b, u + 2)
                    if u + 1 < UNITS:
                        invert(b, u + 1)
                    if u:
                        keep_turned(u - 1)
                    if qt == 0 and p + 1 < NP1:
                        lo(b, p + 1, "k", ya, 1.0)
                    if qt == 2 and p + 2 < NP1:
                        lo(b, p + 2, "q", xa, DH1 ** -0.5)
                keep_turned(UNITS - 1)
                for i in range(TPB):
                    dve.wait_ge(s["y_psum"], b * TPB + i + 1)
                    x = x_tok[:, bass.ds(b * TPB + i, 1)].rearrange("p a d -> p (a d)")
                    v.tensor_tensor(x, x, psum[:, Y_BANKS[i], 0:D], ALU.add).then_inc(s["y_read"], 1)
                dve.wait_ge(s["y_read"], b * TPB + TPB)


def quantised_input_l1(nc, psum, x_tok, ident, hqT_hi, hqT_lo):
    with ExitStack() as ctx:
        sb, sem = scopes(nc, ctx)
        hn = sb("hn_all", [P, NT, D])
        h16 = sb("h16", [P, NT, D], I16)
        st = layernorm_buffers(sb, "ln3", NT)
        mx, mx1, gmax, scale, inv = sb("f_mx", [P, B]), sb("f_mx1", [P, 1]), sb("f_gmax", [P, 1]), sb("f_scale", [P, 1]), sb("f_inv", [P, 1])
        names = ("link", "ln_done", "mx_ready", "gmax_ready", "h16_ready", "hq_ready", "hT_psum", "hT_read")
        s = {n: sem(f"f1_{n}") for n in names}
        block = ctx.enter_context(nc.Block())

        @block.gpsimd
        def _(pool):
            pool.wait_ge(s["mx_ready"], 1)
            nc.gpsimd.partition_all_reduce(gmax[:], mx1[:], P, bass.bass_isa.ReduceOp.max).then_inc(s["gmax_ready"], 1)

        @block.vector
        def _(dve):
            v = nc.vector
            chain = Chain(dve, s["link"])
            layernorm_steps(nc, chain, x_tok, 0, hn, st, False, s["ln_done"], NT)
            dve.wait_ge(s["ln_done"], B)
            chain.step(v.tensor_reduce(mx[:], hn[:].rearrange("p (b t) c -> p b (t c)", b=B), AX.X, ALU.max, apply_absolute_value=True))
            v.tensor_reduce(mx1[:], mx[:], AX.X, ALU.max).then_inc(s["mx_ready"], 1)
            dve.wait_ge(s["gmax_ready"], 1)
            chain.step(v.tensor_scalar(scale[:], gmax[:], 1.0 / QMAX16, SCALE_MIN, ALU.mult, ALU.max))
            chain.step(v.reciprocal(inv[:], scale[:]))
            for b in range(B):
                v.tensor_scalar(h16[:, b * TPB:(b + 1) * TPB], hn[:, b * TPB:(b + 1) * TPB], inv[:], None, ALU.mult).then_inc(s["h16_ready"], 1)
            for i in range(B * KC):
                b, k = divmod(i, KC)
                dve.wait_ge(s["hT_read"], i + 1)
                chain.add(v.tensor_tensor(hqT_lo[:, k, b * S:(b + 1) * S], psum[:, i], hqT_hi[:, k, b * S:(b + 1) * S].bitcast(F32), ALU.subtract))
            chain.wait()

        @block.tensor
        def _(pe):
            for b in range(B):
                pe.wait_ge(s["hq_ready"], b + 1)
                for k in range(KC):
                    for i in range(TPB):
                        last = nc.tensor.transpose(psum[:, b * KC + k, i * P:(i + 1) * P], hn[:, b * TPB + i, k * P:(k + 1) * P], ident[:])
                    last.then_inc(s["hT_psum"], 1)

        @block.scalar
        def _(act):
            def turned(b):
                for k in range(KC):
                    act.wait_ge(s["hT_psum"], b * KC + k + 1)
                    nc.scalar.activation(hqT_hi[:, k, b * S:(b + 1) * S], psum[:, b * KC + k], ACT.Copy).then_inc(s["hT_read"], 1)

            for b in range(B):
                act.wait_ge(s["h16_ready"], b + 1)
                nc.scalar.activation(hn[:, b * TPB:(b + 1) * TPB], h16[:, b * TPB:(b + 1) * TPB], ACT.Copy, scale=scale[:]).then_inc(s["hq_ready"], 1)
                if b:
                    turned(b - 1)
            turned(B - 1)


def gate_and_up_l1(nc, psum, gate, up, mx, wgT, wuT, hqT):
    with ExitStack() as ctx:
        _, sem = scopes(nc, ctx)
        done, read, maxed = sem("gu_psum"), sem("gu_read"), sem("gu_max")
        block = ctx.enter_context(nc.Block())

        @block.tensor
        def _(pe):
            passes = [(k, i, j) for k in range(KC) for i, j in ((0, 0), (0, 1), (1, 0))]
            with pe.Fori(0, B) as c:
                for m in range(MF):
                    for n, w in enumerate((wgT, wuT)):
                        b = (2 * m + n) % 8
                        if 2 * m + n >= 8:
                            pe.wait_ge(read, c * (2 * MF) + 2 * m + n - 7)
                        for k, i, j in passes:
                            last = nc.tensor.matmul(psum[:, b], w[i][:, k, m * P:(m + 1) * P], hqT[j][:, k, bass.ds(c * S, S)],
                                                    start=(k, i, j) == passes[0], stop=(k, i, j) == passes[-1])
                        last.then_inc(done, 1)
                pe.wait_ge(read, (c + 1) * (2 * MF))

        @block.scalar
        def _(act):
            with act.Fori(0, B) as c:
                for i in range(2 * MF):
                    m, n = divmod(i, 2)
                    act.wait_ge(done, c * (2 * MF) + i + 1)
                    dst = (gate, up)[n][:, bass.ds(c, 1), m * S:(m + 1) * S].rearrange("p a n -> p (a n)")
                    nc.scalar.activation(dst, psum[:, i % 8], ACT.Copy).then_inc(read, 1)

        @block.vector
        def _(dve):
            for c in range(B):
                dve.wait_ge(read, (c + 1) * 2 * MF)
                for n, t in enumerate((gate, up)):
                    nc.vector.tensor_reduce(mx[:, n, c:c + 1], t[:, c], AX.X, ALU.max, apply_absolute_value=True).then_inc(maxed, 1)
            dve.wait_ge(maxed, 2 * B)


def gated_l1(nc, psum, x_tok, gate, up, mx, wdT):
    CH = MF * S
    with ExitStack() as ctx:
        sb, sem = scopes(nc, ctx)
        a16, b16, u16 = sb("a16", [P, 2, CH], I16), sb("b16", [P, 2, CH], mybir.dt.uint16), sb("u16", [P, B, CH], I16)
        sig = sb("sig", [P, CH])
        mx1, gmax, k = sb("g_mx1", [P, 2]), sb("g_gmax", [P, 2]), sb("g_k", [P, 12])
        names = ("mx", "gmax", "a", "sig", "b", "gated", "u", "scales", "a2", "link", "o", "y_psum", "y_read")
        s = {n: sem(f"f2_{n}") for n in names}
        block = ctx.enter_context(nc.Block())
        S_G, I_G, S_U, I_U, C2, S_2, I_2, SO_IN, S_O, I_O, T0, T1 = (k[:, i:i + 1] for i in range(12))

        @block.tensor
        def _(pe):
            for c in range(B):
                pe.wait_ge(s["o"], c + 1)
                for i in range(TPB):
                    t = c * TPB + i
                    if t >= 8:
                        pe.wait_ge(s["y_read"], t - 7)
                    for m in range(MF):
                        last = nc.tensor.matmul(psum[:, t % 8, 0:D], gate[:, c, m * S + i * P:m * S + (i + 1) * P], wdT[:, m], start=m == 0, stop=m == MF - 1)
                    last.then_inc(s["y_psum"], 1)

        @block.scalar
        def _(act):
            for c in range(B):
                act.wait_ge(s["a"], c + 1)
                nc.scalar.activation(sig[:], a16[:, c % 2], ACT.Sigmoid, scale=S_G).then_inc(s["sig"], 1)
                act.wait_ge(s["sig"], c + 1)
                if c >= 2:
                    act.wait_ge(s["gated"], c - 1)
                nc.scalar.activation(b16[:, c % 2], sig[:], ACT.Copy, scale=65536.0).then_inc(s["b"], 1)
                act.wait_ge(s["b"], c + 1)
            act.wait_ge(s["scales"], 2)
            for c in range(B):
                if c >= 2:
                    act.wait_ge(s["gated"], B + c - 1)
                nc.scalar.activation(a16[:, c % 2], gate[:, c], ACT.Copy, scale=T0).then_inc(s["a2"], 1)
            for c in range(B):
                act.wait_ge(s["a"], B + c + 1)
                nc.scalar.activation(gate[:, c], a16[:, c % 2], ACT.Copy, scale=S_O).then_inc(s["o"], 1)

        @block.gpsimd
        def _(pool):
            for n in range(3):
                pool.wait_ge(s["mx"], n + 1)
                nc.gpsimd.partition_all_reduce(gmax[:], mx1[:], P, bass.bass_isa.ReduceOp.max).then_inc(s["gmax"], 1)
                if n == 0:
                    pool.wait_ge(s["scales"], 1)
                    for c in range(B):
                        nc.gpsimd.tensor_scalar(u16[:, c], up[:, c], I_U, None, ALU.mult).then_inc(s["u"], 1)

        @block.vector
        def _(dve):
            v = nc.vector
            chain = Chain(dve, s["link"])

            def biggest(n):
                v.tensor_reduce(mx1[:], mx[:], AX.X, ALU.max).then_inc(s["mx"], 1)
                dve.wait_ge(s["gmax"], n)

            biggest(1)
            for out, out_i, n in ((S_G, I_G, 0), (S_U, I_U, 1)):
                chain.step(v.tensor_scalar(out, gmax[:, n:n + 1], 1.0 / QMAX16, SCALE_MIN, ALU.mult, ALU.max))
                chain.add(v.reciprocal(out_i, out))
            v.tensor_scalar(C2, S_G, 1.0 / 65536.0, None, ALU.mult).then_inc(s["scales"], 1)
            chain.wait()

            def first_round(c):
                v.tensor_scalar(a16[:, c % 2], gate[:, c], I_G, None, ALU.mult).then_inc(s["a"], 1)

            def product_and_max(c, other, done):
                v.tensor_tensor(gate[:, c], a16[:, c % 2], other, ALU.mult).then_inc(s["gated"], 1)
                dve.wait_ge(s["gated"], done)
                chain.add(v.tensor_reduce(mx[:, 0, c:c + 1], gate[:, c], AX.X, ALU.max, apply_absolute_value=True))

            first_round(0)
            first_round(1)
            for c in range(B):
                dve.wait_ge(s["b"], c + 1)
                product_and_max(c, b16[:, c % 2], c + 1)
                if c + 2 < B:
                    first_round(c + 2)
            chain.wait()
            biggest(2)
            chain.step(v.tensor_tensor(T1, gmax[:, 0:1], C2, ALU.mult))
            chain.step(v.tensor_scalar(S_2, T1, 1.0 / QMAX16, SCALE_MIN, ALU.mult, ALU.max))
            chain.step(v.reciprocal(I_2, S_2))
            v.tensor_tensor(T0, I_2, C2, ALU.mult).then_inc(s["scales"], 1)
            for c in range(B):
                dve.wait_ge(s["a2"], c + 1)
                dve.wait_ge(s["u"], c + 1)
                product_and_max(c, u16[:, c], B + c + 1)
            chain.wait()
            biggest(3)
            chain.step(v.tensor_tensor(SO_IN, S_2, S_U, ALU.mult))
            chain.step(v.tensor_tensor(T1, gmax[:, 0:1], SO_IN, ALU.mult))
            chain.step(v.tensor_scalar(S_O, T1, 1.0 / QMAX16, SCALE_MIN, ALU.mult, ALU.max))
            chain.step(v.reciprocal(I_O, S_O))
            chain.step(v.tensor_tensor(T1, I_O, SO_IN, ALU.mult))
            for c in range(B):
                if c >= 2:
                    dve.wait_ge(s["o"], c - 1)
                v.tensor_scalar(a16[:, c % 2], gate[:, c], T1, None, ALU.mult).then_inc(s["a"], 1)
            for t in range(NT):
                dve.wait_ge(s["y_psum"], t + 1)
                v.tensor_tensor(x_tok[:, t], x_tok[:, t], psum[:, t % 8, 0:D], ALU.add).then_inc(s["y_read"], 1)
            dve.wait_ge(s["y_read"], NT)


def store_x(nc, x_tok, out_dram):
    with ExitStack() as ctx:
        _, sem = scopes(nc, ctx)
        stored = sem("x_stored")
        block = ctx.enter_context(nc.Block())

        @block.sync
        def _(sp):
            sp.dma_start(out_dram.rearrange("b (t p) d -> p (b t) d", p=P), x_tok[:]).then_inc(stored, 16)
            sp.wait_ge(stored, 16)


def build(nc, a, out, stages=4):
    with ExitStack() as ctx:
        sb, sem = scopes(nc, ctx)
        x_tok = sb("x_tok", [P, NT, D])
        ident = sb("ident", [P, P])
        xmask_i, xmask = sb("xmask_i", [P, NT], I32), sb("xmask", [P, NT])
        psum = ctx.enter_context(nc.psum_tensor("psum", [P, 8, 512], F32))

        def scratch(name, shape, dt=F32):
            return nc.dram_tensor(name, shape, dt, kind="Internal").ap()

        q_scr, k_scr = scratch("q_scr", (2, B, D, S)), scratch("k_scr", (2, B, D, S))
        kneg_scr, v_scr = scratch("kneg_scr", (B, NG0, 2, S)), scratch("v_scr", (B, NG0, TPB, P, P))
        rec_scr = scratch("rec_scr", (G0, B * NG0, S))
        load_inputs(nc, a["x"], x_tok, ident, a["xmask"], xmask_i, xmask)
        project_l0(nc, psum[:], x_tok, ident, a["ctxT"], a["kvmask"], a["ln_w"], a["wq0"], a["wk0"], a["wv0"],
                   q_scr, k_scr, kneg_scr, v_scr)
        xs_scr, ys_scr = scratch("xs_scr", (NS * P, D)), scratch("ys_scr", (NS * P, D))
        w1_in, w2_in = sem("w1_in"), sem("w2_in")
        gate_w, slot, expert = sb("gate_w", [P, NT, TOP]), sb("slot", [P, TOP, NT], U32), sb("expert", [1, NS], I32)
        with nc.sbuf_tensor("w1_all", [P, E0, KC, HID], F32) as w1_all:
            with nc.sbuf_tensor("attnT", [P, B * NG0, S], F32) as attnT:
                attend_l0(nc, psum[:], q_scr, k_scr, kneg_scr, v_scr, attnT, a["w1"], w1_all, w1_in, xs_scr)
                finish_l0(nc, psum[:], x_tok, attnT, rec_scr, a["wo0"], xmask)
            if stages >= 2:
                b1_in = sem("b1_in")
                with nc.sbuf_tensor("w2_all", [P, E0, MH, D], F32) as w2_all, nc.sbuf_tensor("b1_all", [P, E0, HID], F32) as b1_all:
                    route_l0(nc, psum[:], x_tok, ident, a["router"], a["w2"], a["b1"], w2_all, b1_all, w2_in, b1_in, xs_scr, gate_w, slot, expert)
                    experts_l0(nc, psum[:], ident, xs_scr, ys_scr, expert, w1_all, w1_in, w2_all, w2_in, b1_all, b1_in, a["b2"])
        if stages >= 2:
            wgT, wuT = ([sb(f"{n}_{part}", [P, KC, FF], F32R) for part in ("hi", "lo")] for n in ("wgT", "wuT"))
            wdT = sb("wdT", [P, MF, D])
            with ExitStack() as attention:
                asb, _ = scopes(nc, attention)
                qkv_hi, qkv_lo = ([asb(f"w{n}1_{part}", [P, KC, E1], F32R) for n in "qkv"] for part in ("hi", "lo"))
                wo1 = asb("wo1", [P, NP1, D])
                combine_l0(nc, psum[:], x_tok, ident, ys_scr, gate_w, slot, a["wg"], a["wu"], a["wd"], wgT, wuT, wdT,
                           (a["wq1"], a["wk1"], a["wv1"]), qkv_hi, qkv_lo, a["wo1"], wo1)
                if stages >= 3:
                    attend_l1(nc, psum[:], x_tok, ident, a["ctxT"], qkv_hi, qkv_lo, wo1)
        if stages >= 4:
            gate, up, mx = sb("gate", [P, B, MF * S]), sb("up", [P, B, MF * S]), sb("g_mx", [P, 2, B])
            with nc.sbuf_tensor("hqT_hi", [P, KC, T], F32R) as hqT_hi, nc.sbuf_tensor("hqT_lo", [P, KC, T], F32R) as hqT_lo:
                quantised_input_l1(nc, psum[:], x_tok, ident, hqT_hi, hqT_lo)
                gate_and_up_l1(nc, psum[:], gate, up, mx, wgT, wuT, (hqT_hi, hqT_lo))
            gated_l1(nc, psum[:], x_tok, gate, up, mx, wdT)
        store_x(nc, x_tok, out)


def layout(inputs):
    n = {k: np.asarray(v) for k, v in inputs.items()}
    c = np.ascontiguousarray
    wo0 = np.zeros((P, NG0, D), np.float32)
    wo0.reshape(G0, SLOT, NG0, D)[:, :DH0] = n["L0_xattn_Wo"].reshape(NG0, G0, DH0, D).transpose(1, 2, 0, 3)
    return {
        "x": c(n["x"]),
        "xmask": c(n["mask_BxS_ik0"].reshape(NT, P).T),
        "kvmask": c(n["mask_BxS2_ik1"].reshape(T)),
        "ctxT": c(n["ctx_1024"].transpose(0, 2, 1)),
        "ln_w": c(n["L0_xattn_ln_w"].reshape(KC, P).T),
        "wq0": c(n["L0_xattn_Wq"]),
        "wk0": c(n["L0_xattn_Wkv"][:, :D]),
        "wv0": c(n["L0_xattn_Wkv"][:, D:]),
        "wo0": wo0,
        "router": c(n["L0_ffn_router_w"].T),
        "w1": c(n["L0_ffn_w1"].transpose(0, 2, 1)),
        "b1": c(n["L0_ffn_b1"]),
        "w2": c(n["L0_ffn_w2"].transpose(0, 2, 1)),
        "b2": c(n["L0_ffn_b2"]),
        "wq1": c(n["L1_xattn_Wq"]),
        "wk1": c(n["L1_xattn_Wk"]),
        "wv1": c(n["L1_xattn_Wv"]),
        "wo1": c(n["L1_xattn_Wo"]),
        "wg": c(n["L1_ffn_w_gate"]),
        "wu": c(n["L1_ffn_w_up"]),
        "wd": c(n["L1_ffn_w_down"]),
    }


def kernel(**inputs):
    import concourse.bacc as bacc
    from concourse.bass_utils import run_bass_kernel_spmd

    arrays = layout(inputs)
    nc = bacc.Bacc("TRN2", target_bir_lowering=False, num_devices=1)
    a = {k: nc.dram_tensor(f"in_{k}", v.shape, mybir.dt.from_np(v.dtype), kind="ExternalInput").ap() for k, v in arrays.items()}
    out = nc.dram_tensor("out_x", (B, S, D), F32, kind="ExternalOutput").ap()
    build(nc, a, out)
    r = run_bass_kernel_spmd(nc, [{f"in_{k}": v for k, v in arrays.items()}], core_ids=[0])
    return r.results[0]["out_x"]
```
